# Optimizing a Trainium2 kernel written in Bass

```python
import numpy as np
import jax
import jax.numpy as jnp

def _softmax(x, axis=-1):
    return jax.nn.softmax(x, axis=axis)

def _gelu(x):
    return jax.nn.gelu(x, approximate=True)

def _silu(x):
    return jax.nn.silu(x)

def _sigmoid(x):
    return jax.nn.sigmoid(x)

def _layernorm(x, axis=-1, eps=1e-05):
    m = jnp.mean(x, axis=axis, keepdims=True)
    v = jnp.var(x, axis=axis, keepdims=True)
    return (x - m) / jnp.sqrt(v + eps)

def _scatter_add(tgt, idx, src, axis=0):
    return tgt.at[idx].add(src)

def _segment_sum(src, seg, n):
    return jax.ops.segment_sum(src, seg, n)
kernel_name = 'mk_rec_standalone_d1_rec_r8_03a2d4'

def setup_inputs(seed: int=0):
    np.random.seed(seed)
    _w = jnp.asarray

    def _rec_inputs():
        import jax
        import jax.numpy as jnp
        _rk = jax.random.key(seed)
        r_user_num = 0.00386106 + 1.00199 * jax.random.normal(jax.random.fold_in(_rk, 1), (512, 8), jnp.float32)
        r_user_cat = jnp.stack([jax.random.randint(jax.random.fold_in(jax.random.fold_in(_rk, 2), 0), (512,), 78, 99953, jnp.int32), jax.random.randint(jax.random.fold_in(jax.random.fold_in(_rk, 2), 1), (512,), 17, 99949, jnp.int32), jax.random.randint(jax.random.fold_in(jax.random.fold_in(_rk, 2), 2), (512,), 86, 99855, jnp.int32), jax.random.randint(jax.random.fold_in(jax.random.fold_in(_rk, 2), 3), (512,), 90, 99862, jnp.int32), jax.random.randint(jax.random.fold_in(jax.random.fold_in(_rk, 2), 4), (512,), 145, 12479, jnp.int32), jax.random.randint(jax.random.fold_in(jax.random.fold_in(_rk, 2), 5), (512,), 72, 99964, jnp.int32)], axis=1)
        r_ctx_cat = jnp.stack([jax.random.randint(jax.random.fold_in(jax.random.fold_in(_rk, 3), 0), (512,), 40, 99858, jnp.int32), jax.random.randint(jax.random.fold_in(jax.random.fold_in(_rk, 3), 1), (512,), 18, 99909, jnp.int32), jax.random.randint(jax.random.fold_in(jax.random.fold_in(_rk, 3), 2), (512,), 30, 99924, jnp.int32), jax.random.randint(jax.random.fold_in(jax.random.fold_in(_rk, 3), 3), (512,), 17, 99982, jnp.int32)], axis=1)
        r_ctx_num = -0.00888005 + 1.00124 * jax.random.normal(jax.random.fold_in(_rk, 4), (512, 4), jnp.float32)
        r_hist_ids = jnp.stack([jax.random.randint(jax.random.fold_in(jax.random.fold_in(_rk, 5), 0), (512,), 47, 99967, jnp.int32), jax.random.randint(jax.random.fold_in(jax.random.fold_in(_rk, 5), 1), (512,), 39, 99974, jnp.int32), jax.random.randint(jax.random.fold_in(jax.random.fold_in(_rk, 5), 2), (512,), 12, 12496, jnp.int32), jax.random.randint(jax.random.fold_in(jax.random.fold_in(_rk, 5), 3), (512,), 12, 12492, jnp.int32), jax.random.randint(jax.random.fold_in(jax.random.fold_in(_rk, 5), 4), (512,), 35, 99980, jnp.int32), jax.random.randint(jax.random.fold_in(jax.random.fold_in(_rk, 5), 5), (512,), 31, 99927, jnp.int32), jax.random.randint(jax.random.fold_in(jax.random.fold_in(_rk, 5), 6), (512,), 141, 99999, jnp.int32), jax.random.randint(jax.random.fold_in(jax.random.fold_in(_rk, 5), 7), (512,), 4, 99941, jnp.int32), jax.random.randint(jax.random.fold_in(jax.random.fold_in(_rk, 5), 8), (512,), 100, 99932, jnp.int32), jax.random.randint(jax.random.fold_in(jax.random.fold_in(_rk, 5), 9), (512,), 11, 99998, jnp.int32), jax.random.randint(jax.random.fold_in(jax.random.fold_in(_rk, 5), 10), (512,), 65, 99987, jnp.int32), jax.random.randint(jax.random.fold_in(jax.random.fold_in(_rk, 5), 11), (512,), 42, 99927, jnp.int32), jax.random.randint(jax.random.fold_in(jax.random.fold_in(_rk, 5), 12), (512,), 57, 99901, jnp.int32), jax.random.randint(jax.random.fold_in(jax.random.fold_in(_rk, 5), 13), (512,), 2, 99911, jnp.int32), jax.random.randint(jax.random.fold_in(jax.random.fold_in(_rk, 5), 14), (512,), 26, 99826, jnp.int32), jax.random.randint(jax.random.fold_in(jax.random.fold_in(_rk, 5), 15), (512,), 34, 12494, jnp.int32), jax.random.randint(jax.random.fold_in(jax.random.fold_in(_rk, 5), 16), (512,), 118, 99979, jnp.int32), jax.random.randint(jax.random.fold_in(jax.random.fold_in(_rk, 5), 17), (512,), 228, 99947, jnp.int32), jax.random.randint(jax.random.fold_in(jax.random.fold_in(_rk, 5), 18), (512,), 39, 99903, jnp.int32), jax.random.randint(jax.random.fold_in(jax.random.fold_in(_rk, 5), 19), (512,), 25, 12497, jnp.int32), jax.random.randint(jax.random.fold_in(jax.random.fold_in(_rk, 5), 20), (512,), 35, 99899, jnp.int32), jax.random.randint(jax.random.fold_in(jax.random.fold_in(_rk, 5), 21), (512,), 6, 99898, jnp.int32), jax.random.randint(jax.random.fold_in(jax.random.fold_in(_rk, 5), 22), (512,), 64, 99994, jnp.int32), jax.random.randint(jax.random.fold_in(jax.random.fold_in(_rk, 5), 23), (512,), 39, 99959, jnp.int32), jax.random.randint(jax.random.fold_in(jax.random.fold_in(_rk, 5), 24), (512,), 24, 99987, jnp.int32), jax.random.randint(jax.random.fold_in(jax.random.fold_in(_rk, 5), 25), (512,), 166, 12497, jnp.int32), jax.random.randint(jax.random.fold_in(jax.random.fold_in(_rk, 5), 26), (512,), 139, 99972, jnp.int32), jax.random.randint(jax.random.fold_in(jax.random.fold_in(_rk, 5), 27), (512,), 6, 12487, jnp.int32), jax.random.randint(jax.random.fold_in(jax.random.fold_in(_rk, 5), 28), (512,), 27, 12498, jnp.int32), jax.random.randint(jax.random.fold_in(jax.random.fold_in(_rk, 5), 29), (512,), 64, 99978, jnp.int32), jax.random.randint(jax.random.fold_in(jax.random.fold_in(_rk, 5), 30), (512,), 11, 99980, jnp.int32), jax.random.randint(jax.random.fold_in(jax.random.fold_in(_rk, 5), 31), (512,), 16, 12493, jnp.int32), jax.random.randint(jax.random.fold_in(jax.random.fold_in(_rk, 5), 32), (512,), 49, 99981, jnp.int32), jax.random.randint(jax.random.fold_in(jax.random.fold_in(_rk, 5), 33), (512,), 221, 99967, jnp.int32), jax.random.randint(jax.random.fold_in(jax.random.fold_in(_rk, 5), 34), (512,), 56, 99954, jnp.int32), jax.random.randint(jax.random.fold_in(jax.random.fold_in(_rk, 5), 35), (512,), 7, 99950, jnp.int32), jax.random.randint(jax.random.fold_in(jax.random.fold_in(_rk, 5), 36), (512,), 49, 99963, jnp.int32), jax.random.randint(jax.random.fold_in(jax.random.fold_in(_rk, 5), 37), (512,), 18, 12494, jnp.int32), jax.random.randint(jax.random.fold_in(jax.random.fold_in(_rk, 5), 38), (512,), 108, 99956, jnp.int32), jax.random.randint(jax.random.fold_in(jax.random.fold_in(_rk, 5), 39), (512,), 5, 99797, jnp.int32), jax.random.randint(jax.random.fold_in(jax.random.fold_in(_rk, 5), 40), (512,), 127, 99907, jnp.int32), jax.random.randint(jax.random.fold_in(jax.random.fold_in(_rk, 5), 41), (512,), 26, 99922, jnp.int32), jax.random.randint(jax.random.fold_in(jax.random.fold_in(_rk, 5), 42), (512,), 172, 99964, jnp.int32), jax.random.randint(jax.random.fold_in(jax.random.fold_in(_rk, 5), 43), (512,), 41, 99974, jnp.int32), jax.random.randint(jax.random.fold_in(jax.random.fold_in(_rk, 5), 44), (512,), 23, 99998, jnp.int32), jax.random.randint(jax.random.fold_in(jax.random.fold_in(_rk, 5), 45), (512,), 55, 99943, jnp.int32), jax.random.randint(jax.random.fold_in(jax.random.fold_in(_rk, 5), 46), (512,), 19, 12500, jnp.int32), jax.random.randint(jax.random.fold_in(jax.random.fold_in(_rk, 5), 47), (512,), 52, 99939, jnp.int32), jax.random.randint(jax.random.fold_in(jax.random.fold_in(_rk, 5), 48), (512,), 236, 99991, jnp.int32), jax.random.randint(jax.random.fold_in(jax.random.fold_in(_rk, 5), 49), (512,), 22, 12499, jnp.int32), jax.random.randint(jax.random.fold_in(jax.random.fold_in(_rk, 5), 50), (512,), 31, 12495, jnp.int32), jax.random.randint(jax.random.fold_in(jax.random.fold_in(_rk, 5), 51), (512,), 13, 99974, jnp.int32), jax.random.randint(jax.random.fold_in(jax.random.fold_in(_rk, 5), 52), (512,), 17, 99972, jnp.int32), jax.random.randint(jax.random.fold_in(jax.random.fold_in(_rk, 5), 53), (512,), 32, 99924, jnp.int32), jax.random.randint(jax.random.fold_in(jax.random.fold_in(_rk, 5), 54), (512,), 39, 99999, jnp.int32), jax.random.randint(jax.random.fold_in(jax.random.fold_in(_rk, 5), 55), (512,), 18, 99997, jnp.int32), jax.random.randint(jax.random.fold_in(jax.random.fold_in(_rk, 5), 56), (512,), 15, 99958, jnp.int32), jax.random.randint(jax.random.fold_in(jax.random.fold_in(_rk, 5), 57), (512,), 40, 99998, jnp.int32), jax.random.randint(jax.random.fold_in(jax.random.fold_in(_rk, 5), 58), (512,), 50, 12494, jnp.int32), jax.random.randint(jax.random.fold_in(jax.random.fold_in(_rk, 5), 59), (512,), 10, 99951, jnp.int32), jax.random.randint(jax.random.fold_in(jax.random.fold_in(_rk, 5), 60), (512,), 9, 12495, jnp.int32), jax.random.randint(jax.random.fold_in(jax.random.fold_in(_rk, 5), 61), (512,), 0, 99979, jnp.int32), jax.random.randint(jax.random.fold_in(jax.random.fold_in(_rk, 5), 62), (512,), 36, 99965, jnp.int32), jax.random.randint(jax.random.fold_in(jax.random.fold_in(_rk, 5), 63), (512,), 88, 99943, jnp.int32), jax.random.randint(jax.random.fold_in(jax.random.fold_in(_rk, 5), 64), (512,), 129, 99994, jnp.int32), jax.random.randint(jax.random.fold_in(jax.random.fold_in(_rk, 5), 65), (512,), 150, 99986, jnp.int32), jax.random.randint(jax.random.fold_in(jax.random.fold_in(_rk, 5), 66), (512,), 10, 99902, jnp.int32), jax.random.randint(jax.random.fold_in(jax.random.fold_in(_rk, 5), 67), (512,), 17, 99985, jnp.int32), jax.random.randint(jax.random.fold_in(jax.random.fold_in(_rk, 5), 68), (512,), 53, 99998, jnp.int32), jax.random.randint(jax.random.fold_in(jax.random.fold_in(_rk, 5), 69), (512,), 73, 99930, jnp.int32), jax.random.randint(jax.random.fold_in(jax.random.fold_in(_rk, 5), 70), (512,), 68, 99970, jnp.int32), jax.random.randint(jax.random.fold_in(jax.random.fold_in(_rk, 5), 71), (512,), 16, 99980, jnp.int32), jax.random.randint(jax.random.fold_in(jax.random.fold_in(_rk, 5), 72), (512,), 6, 99988, jnp.int32), jax.random.randint(jax.random.fold_in(jax.random.fold_in(_rk, 5), 73), (512,), 6, 99957, jnp.int32), jax.random.randint(jax.random.fold_in(jax.random.fold_in(_rk, 5), 74), (512,), 39, 99994, jnp.int32), jax.random.randint(jax.random.fold_in(jax.random.fold_in(_rk, 5), 75), (512,), 37, 99991, jnp.int32), jax.random.randint(jax.random.fold_in(jax.random.fold_in(_rk, 5), 76), (512,), 133, 99975, jnp.int32), jax.random.randint(jax.random.fold_in(jax.random.fold_in(_rk, 5), 77), (512,), 99, 99994, jnp.int32), jax.random.randint(jax.random.fold_in(jax.random.fold_in(_rk, 5), 78), (512,), 114, 99894, jnp.int32), jax.random.randint(jax.random.fold_in(jax.random.fold_in(_rk, 5), 79), (512,), 12, 99949, jnp.int32), jax.random.randint(jax.random.fold_in(jax.random.fold_in(_rk, 5), 80), (512,), 7, 99978, jnp.int32), jax.random.randint(jax.random.fold_in(jax.random.fold_in(_rk, 5), 81), (512,), 1, 99991, jnp.int32), jax.random.randint(jax.random.fold_in(jax.random.fold_in(_rk, 5), 82), (512,), 72, 99995, jnp.int32), jax.random.randint(jax.random.fold_in(jax.random.fold_in(_rk, 5), 83), (512,), 45, 99985, jnp.int32), jax.random.randint(jax.random.fold_in(jax.random.fold_in(_rk, 5), 84), (512,), 16, 99955, jnp.int32), jax.random.randint(jax.random.fold_in(jax.random.fold_in(_rk, 5), 85), (512,), 17, 99997, jnp.int32), jax.random.randint(jax.random.fold_in(jax.random.fold_in(_rk, 5), 86), (512,), 31, 99999, jnp.int32), jax.random.randint(jax.random.fold_in(jax.random.fold_in(_rk, 5), 87), (512,), 47, 99981, jnp.int32), jax.random.randint(jax.random.fold_in(jax.random.fold_in(_rk, 5), 88), (512,), 44, 99962, jnp.int32), jax.random.randint(jax.random.fold_in(jax.random.fold_in(_rk, 5), 89), (512,), 106, 99980, jnp.int32), jax.random.randint(jax.random.fold_in(jax.random.fold_in(_rk, 5), 90), (512,), 110, 99845, jnp.int32), jax.random.randint(jax.random.fold_in(jax.random.fold_in(_rk, 5), 91), (512,), 96, 99980, jnp.int32), jax.random.randint(jax.random.fold_in(jax.random.fold_in(_rk, 5), 92), (512,), 6, 99751, jnp.int32), jax.random.randint(jax.random.fold_in(jax.random.fold_in(_rk, 5), 93), (512,), 27, 99955, jnp.int32), jax.random.randint(jax.random.fold_in(jax.random.fold_in(_rk, 5), 94), (512,), 9, 12496, jnp.int32), jax.random.randint(jax.random.fold_in(jax.random.fold_in(_rk, 5), 95), (512,), 42, 99991, jnp.int32), jax.random.randint(jax.random.fold_in(jax.random.fold_in(_rk, 5), 96), (512,), 68, 99886, jnp.int32), jax.random.randint(jax.random.fold_in(jax.random.fold_in(_rk, 5), 97), (512,), 0, 99915, jnp.int32), jax.random.randint(jax.random.fold_in(jax.random.fold_in(_rk, 5), 98), (512,), 66, 99909, jnp.int32), jax.random.randint(jax.random.fold_in(jax.random.fold_in(_rk, 5), 99), (512,), 77, 99998, jnp.int32), jax.random.randint(jax.random.fold_in(jax.random.fold_in(_rk, 5), 100), (512,), 33, 12500, jnp.int32), jax.random.randint(jax.random.fold_in(jax.random.fold_in(_rk, 5), 101), (512,), 12, 99957, jnp.int32), jax.random.randint(jax.random.fold_in(jax.random.fold_in(_rk, 5), 102), (512,), 28, 99977, jnp.int32), jax.random.randint(jax.random.fold_in(jax.random.fold_in(_rk, 5), 103), (512,), 67, 99951, jnp.int32), jax.random.randint(jax.random.fold_in(jax.random.fold_in(_rk, 5), 104), (512,), 62, 99863, jnp.int32), jax.random.randint(jax.random.fold_in(jax.random.fold_in(_rk, 5), 105), (512,), 18, 99987, jnp.int32), jax.random.randint(jax.random.fold_in(jax.random.fold_in(_rk, 5), 106), (512,), 157, 99988, jnp.int32), jax.random.randint(jax.random.fold_in(jax.random.fold_in(_rk, 5), 107), (512,), 14, 99956, jnp.int32), jax.random.randint(jax.random.fold_in(jax.random.fold_in(_rk, 5), 108), (512,), 33, 99911, jnp.int32), jax.random.randint(jax.random.fold_in(jax.random.fold_in(_rk, 5), 109), (512,), 66, 99924, jnp.int32), jax.random.randint(jax.random.fold_in(jax.random.fold_in(_rk, 5), 110), (512,), 20, 99971, jnp.int32), jax.random.randint(jax.random.fold_in(jax.random.fold_in(_rk, 5), 111), (512,), 27, 12496, jnp.int32), jax.random.randint(jax.random.fold_in(jax.random.fold_in(_rk, 5), 112), (512,), 26, 99770, jnp.int32), jax.random.randint(jax.random.fold_in(jax.random.fold_in(_rk, 5), 113), (512,), 165, 99974, jnp.int32), jax.random.randint(jax.random.fold_in(jax.random.fold_in(_rk, 5), 114), (512,), 49, 99869, jnp.int32), jax.random.randint(jax.random.fold_in(jax.random.fold_in(_rk, 5), 115), (512,), 293, 99948, jnp.int32), jax.random.randint(jax.random.fold_in(jax.random.fold_in(_rk, 5), 116), (512,), 97, 99993, jnp.int32), jax.random.randint(jax.random.fold_in(jax.random.fold_in(_rk, 5), 117), (512,), 54, 99956, jnp.int32), jax.random.randint(jax.random.fold_in(jax.random.fold_in(_rk, 5), 118), (512,), 50, 12493, jnp.int32), jax.random.randint(jax.random.fold_in(jax.random.fold_in(_rk, 5), 119), (512,), 102, 99977, jnp.int32), jax.random.randint(jax.random.fold_in(jax.random.fold_in(_rk, 5), 120), (512,), 4, 99942, jnp.int32), jax.random.randint(jax.random.fold_in(jax.random.fold_in(_rk, 5), 121), (512,), 6, 99997, jnp.int32), jax.random.randint(jax.random.fold_in(jax.random.fold_in(_rk, 5), 122), (512,), 121, 99941, jnp.int32), jax.random.randint(jax.random.fold_in(jax.random.fold_in(_rk, 5), 123), (512,), 40, 99987, jnp.int32), jax.random.randint(jax.random.fold_in(jax.random.fold_in(_rk, 5), 124), (512,), 179, 99893, jnp.int32), jax.random.randint(jax.random.fold_in(jax.random.fold_in(_rk, 5), 125), (512,), 81, 12488, jnp.int32), jax.random.randint(jax.random.fold_in(jax.random.fold_in(_rk, 5), 126), (512,), 34, 99917, jnp.int32), jax.random.randint(jax.random.fold_in(jax.random.fold_in(_rk, 5), 127), (512,), 35, 99970, jnp.int32), jax.random.randint(jax.random.fold_in(jax.random.fold_in(_rk, 5), 128), (512,), 109, 99996, jnp.int32), jax.random.randint(jax.random.fold_in(jax.random.fold_in(_rk, 5), 129), (512,), 34, 99957, jnp.int32), jax.random.randint(jax.random.fold_in(jax.random.fold_in(_rk, 5), 130), (512,), 44, 99981, jnp.int32), jax.random.randint(jax.random.fold_in(jax.random.fold_in(_rk, 5), 131), (512,), 4, 99841, jnp.int32), jax.random.randint(jax.random.fold_in(jax.random.fold_in(_rk, 5), 132), (512,), 30, 99999, jnp.int32), jax.random.randint(jax.random.fold_in(jax.random.fold_in(_rk, 5), 133), (512,), 111, 99858, jnp.int32), jax.random.randint(jax.random.fold_in(jax.random.fold_in(_rk, 5), 134), (512,), 160, 99986, jnp.int32), jax.random.randint(jax.random.fold_in(jax.random.fold_in(_rk, 5), 135), (512,), 24, 99985, jnp.int32), jax.random.randint(jax.random.fold_in(jax.random.fold_in(_rk, 5), 136), (512,), 18, 99905, jnp.int32), jax.random.randint(jax.random.fold_in(jax.random.fold_in(_rk, 5), 137), (512,), 2, 99997, jnp.int32), jax.random.randint(jax.random.fold_in(jax.random.fold_in(_rk, 5), 138), (512,), 35, 99958, jnp.int32), jax.random.randint(jax.random.fold_in(jax.random.fold_in(_rk, 5), 139), (512,), 6, 99990, jnp.int32), jax.random.randint(jax.random.fold_in(jax.random.fold_in(_rk, 5), 140), (512,), 3, 99859, jnp.int32), jax.random.randint(jax.random.fold_in(jax.random.fold_in(_rk, 5), 141), (512,), 144, 99966, jnp.int32), jax.random.randint(jax.random.fold_in(jax.random.fold_in(_rk, 5), 142), (512,), 37, 99990, jnp.int32), jax.random.randint(jax.random.fold_in(jax.random.fold_in(_rk, 5), 143), (512,), 55, 99991, jnp.int32), jax.random.randint(jax.random.fold_in(jax.random.fold_in(_rk, 5), 144), (512,), 72, 99906, jnp.int32), jax.random.randint(jax.random.fold_in(jax.random.fold_in(_rk, 5), 145), (512,), 7, 99897, jnp.int32), jax.random.randint(jax.random.fold_in(jax.random.fold_in(_rk, 5), 146), (512,), 60, 99935, jnp.int32), jax.random.randint(jax.random.fold_in(jax.random.fold_in(_rk, 5), 147), (512,), 12, 12496, jnp.int32), jax.random.randint(jax.random.fold_in(jax.random.fold_in(_rk, 5), 148), (512,), 21, 99998, jnp.int32), jax.random.randint(jax.random.fold_in(jax.random.fold_in(_rk, 5), 149), (512,), 13, 99858, jnp.int32), jax.random.randint(jax.random.fold_in(jax.random.fold_in(_rk, 5), 150), (512,), 9, 99849, jnp.int32), jax.random.randint(jax.random.fold_in(jax.random.fold_in(_rk, 5), 151), (512,), 28, 99941, jnp.int32), jax.random.randint(jax.random.fold_in(jax.random.fold_in(_rk, 5), 152), (512,), 5, 99986, jnp.int32), jax.random.randint(jax.random.fold_in(jax.random.fold_in(_rk, 5), 153), (512,), 20, 99987, jnp.int32), jax.random.randint(jax.random.fold_in(jax.random.fold_in(_rk, 5), 154), (512,), 21, 12488, jnp.int32), jax.random.randint(jax.random.fold_in(jax.random.fold_in(_rk, 5), 155), (512,), 222, 99985, jnp.int32), jax.random.randint(jax.random.fold_in(jax.random.fold_in(_rk, 5), 156), (512,), 33, 99897, jnp.int32), jax.random.randint(jax.random.fold_in(jax.random.fold_in(_rk, 5), 157), (512,), 43, 99921, jnp.int32), jax.random.randint(jax.random.fold_in(jax.random.fold_in(_rk, 5), 158), (512,), 204, 99899, jnp.int32), jax.random.randint(jax.random.fold_in(jax.random.fold_in(_rk, 5), 159), (512,), 33, 99999, jnp.int32), jax.random.randint(jax.random.fold_in(jax.random.fold_in(_rk, 5), 160), (512,), 131, 99846, jnp.int32), jax.random.randint(jax.random.fold_in(jax.random.fold_in(_rk, 5), 161), (512,), 64, 99982, jnp.int32), jax.random.randint(jax.random.fold_in(jax.random.fold_in(_rk, 5), 162), (512,), 53, 99994, jnp.int32), jax.random.randint(jax.random.fold_in(jax.random.fold_in(_rk, 5), 163), (512,), 0, 99978, jnp.int32), jax.random.randint(jax.random.fold_in(jax.random.fold_in(_rk, 5), 164), (512,), 89, 99994, jnp.int32), jax.random.randint(jax.random.fold_in(jax.random.fold_in(_rk, 5), 165), (512,), 59, 99949, jnp.int32), jax.random.randint(jax.random.fold_in(jax.random.fold_in(_rk, 5), 166), (512,), 78, 99889, jnp.int32), jax.random.randint(jax.random.fold_in(jax.random.fold_in(_rk, 5), 167), (512,), 8, 99994, jnp.int32), jax.random.randint(jax.random.fold_in(jax.random.fold_in(_rk, 5), 168), (512,), 23, 99868, jnp.int32), jax.random.randint(jax.random.fold_in(jax.random.fold_in(_rk, 5), 169), (512,), 65, 99966, jnp.int32), jax.random.randint(jax.random.fold_in(jax.random.fold_in(_rk, 5), 170), (512,), 101, 99935, jnp.int32), jax.random.randint(jax.random.fold_in(jax.random.fold_in(_rk, 5), 171), (512,), 95, 99963, jnp.int32), jax.random.randint(jax.random.fold_in(jax.random.fold_in(_rk, 5), 172), (512,), 9, 99834, jnp.int32), jax.random.randint(jax.random.fold_in(jax.random.fold_in(_rk, 5), 173), (512,), 16, 99918, jnp.int32), jax.random.randint(jax.random.fold_in(jax.random.fold_in(_rk, 5), 174), (512,), 32, 99995, jnp.int32), jax.random.randint(jax.random.fold_in(jax.random.fold_in(_rk, 5), 175), (512,), 115, 99964, jnp.int32), jax.random.randint(jax.random.fold_in(jax.random.fold_in(_rk, 5), 176), (512,), 43, 99987, jnp.int32), jax.random.randint(jax.random.fold_in(jax.random.fold_in(_rk, 5), 177), (512,), 103, 99958, jnp.int32), jax.random.randint(jax.random.fold_in(jax.random.fold_in(_rk, 5), 178), (512,), 25, 12497, jnp.int32), jax.random.randint(jax.random.fold_in(jax.random.fold_in(_rk, 5), 179), (512,), 17, 99954, jnp.int32), jax.random.randint(jax.random.fold_in(jax.random.fold_in(_rk, 5), 180), (512,), 43, 99926, jnp.int32), jax.random.randint(jax.random.fold_in(jax.random.fold_in(_rk, 5), 181), (512,), 38, 99965, jnp.int32), jax.random.randint(jax.random.fold_in(jax.random.fold_in(_rk, 5), 182), (512,), 9, 12500, jnp.int32), jax.random.randint(jax.random.fold_in(jax.random.fold_in(_rk, 5), 183), (512,), 9, 99750, jnp.int32), jax.random.randint(jax.random.fold_in(jax.random.fold_in(_rk, 5), 184), (512,), 30, 99987, jnp.int32), jax.random.randint(jax.random.fold_in(jax.random.fold_in(_rk, 5), 185), (512,), 45, 99955, jnp.int32), jax.random.randint(jax.random.fold_in(jax.random.fold_in(_rk, 5), 186), (512,), 56, 99979, jnp.int32), jax.random.randint(jax.random.fold_in(jax.random.fold_in(_rk, 5), 187), (512,), 37, 99981, jnp.int32), jax.random.randint(jax.random.fold_in(jax.random.fold_in(_rk, 5), 188), (512,), 11, 99987, jnp.int32), jax.random.randint(jax.random.fold_in(jax.random.fold_in(_rk, 5), 189), (512,), 32, 99994, jnp.int32), jax.random.randint(jax.random.fold_in(jax.random.fold_in(_rk, 5), 190), (512,), 13, 99974, jnp.int32), jax.random.randint(jax.random.fold_in(jax.random.fold_in(_rk, 5), 191), (512,), 10, 12479, jnp.int32), jax.random.randint(jax.random.fold_in(jax.random.fold_in(_rk, 5), 192), (512,), 11, 99909, jnp.int32), jax.random.randint(jax.random.fold_in(jax.random.fold_in(_rk, 5), 193), (512,), 54, 99940, jnp.int32), jax.random.randint(jax.random.fold_in(jax.random.fold_in(_rk, 5), 194), (512,), 55, 99996, jnp.int32), jax.random.randint(jax.random.fold_in(jax.random.fold_in(_rk, 5), 195), (512,), 16, 99995, jnp.int32), jax.random.randint(jax.random.fold_in(jax.random.fold_in(_rk, 5), 196), (512,), 12, 99879, jnp.int32), jax.random.randint(jax.random.fold_in(jax.random.fold_in(_rk, 5), 197), (512,), 109, 99961, jnp.int32), jax.random.randint(jax.random.fold_in(jax.random.fold_in(_rk, 5), 198), (512,), 0, 99931, jnp.int32), jax.random.randint(jax.random.fold_in(jax.random.fold_in(_rk, 5), 199), (512,), 27, 99999, jnp.int32)], axis=1)
        r_hist_author_ids = jnp.stack([jax.random.randint(jax.random.fold_in(jax.random.fold_in(_rk, 6), 0), (512,), 35, 99987, jnp.int32), jax.random.randint(jax.random.fold_in(jax.random.fold_in(_rk, 6), 1), (512,), 69, 99985, jnp.int32), jax.random.randint(jax.random.fold_in(jax.random.fold_in(_rk, 6), 2), (512,), 25, 12494, jnp.int32), jax.random.randint(jax.random.fold_in(jax.random.fold_in(_rk, 6), 3), (512,), 53, 99987, jnp.int32), jax.random.randint(jax.random.fold_in(jax.random.fold_in(_rk, 6), 4), (512,), 21, 12484, jnp.int32), jax.random.randint(jax.random.fold_in(jax.random.fold_in(_rk, 6), 5), (512,), 74, 99996, jnp.int32), jax.random.randint(jax.random.fold_in(jax.random.fold_in(_rk, 6), 6), (512,), 303, 99995, jnp.int32), jax.random.randint(jax.random.fold_in(jax.random.fold_in(_rk, 6), 7), (512,), 112, 99841, jnp.int32), jax.random.randint(jax.random.fold_in(jax.random.fold_in(_rk, 6), 8), (512,), 120, 99991, jnp.int32), jax.random.randint(jax.random.fold_in(jax.random.fold_in(_rk, 6), 9), (512,), 159, 99953, jnp.int32), jax.random.randint(jax.random.fold_in(jax.random.fold_in(_rk, 6), 10), (512,), 30, 12499, jnp.int32), jax.random.randint(jax.random.fold_in(jax.random.fold_in(_rk, 6), 11), (512,), 59, 99964, jnp.int32), jax.random.randint(jax.random.fold_in(jax.random.fold_in(_rk, 6), 12), (512,), 68, 99991, jnp.int32), jax.random.randint(jax.random.fold_in(jax.random.fold_in(_rk, 6), 13), (512,), 44, 99999, jnp.int32), jax.random.randint(jax.random.fold_in(jax.random.fold_in(_rk, 6), 14), (512,), 14, 12496, jnp.int32), jax.random.randint(jax.random.fold_in(jax.random.fold_in(_rk, 6), 15), (512,), 24, 99939, jnp.int32), jax.random.randint(jax.random.fold_in(jax.random.fold_in(_rk, 6), 16), (512,), 244, 99945, jnp.int32), jax.random.randint(jax.random.fold_in(jax.random.fold_in(_rk, 6), 17), (512,), 26, 99977, jnp.int32), jax.random.randint(jax.random.fold_in(jax.random.fold_in(_rk, 6), 18), (512,), 2, 99740, jnp.int32), jax.random.randint(jax.random.fold_in(jax.random.fold_in(_rk, 6), 19), (512,), 139, 99999, jnp.int32), jax.random.randint(jax.random.fold_in(jax.random.fold_in(_rk, 6), 20), (512,), 23, 99988, jnp.int32), jax.random.randint(jax.random.fold_in(jax.random.fold_in(_rk, 6), 21), (512,), 16, 12499, jnp.int32), jax.random.randint(jax.random.fold_in(jax.random.fold_in(_rk, 6), 22), (512,), 20, 99785, jnp.int32), jax.random.randint(jax.random.fold_in(jax.random.fold_in(_rk, 6), 23), (512,), 14, 99933, jnp.int32), jax.random.randint(jax.random.fold_in(jax.random.fold_in(_rk, 6), 24), (512,), 44, 12494, jnp.int32), jax.random.randint(jax.random.fold_in(jax.random.fold_in(_rk, 6), 25), (512,), 4, 99996, jnp.int32), jax.random.randint(jax.random.fold_in(jax.random.fold_in(_rk, 6), 26), (512,), 21, 12492, jnp.int32), jax.random.randint(jax.random.fold_in(jax.random.fold_in(_rk, 6), 27), (512,), 60, 12496, jnp.int32), jax.random.randint(jax.random.fold_in(jax.random.fold_in(_rk, 6), 28), (512,), 166, 99930, jnp.int32), jax.random.randint(jax.random.fold_in(jax.random.fold_in(_rk, 6), 29), (512,), 42, 99974, jnp.int32), jax.random.randint(jax.random.fold_in(jax.random.fold_in(_rk, 6), 30), (512,), 26, 12498, jnp.int32), jax.random.randint(jax.random.fold_in(jax.random.fold_in(_rk, 6), 31), (512,), 46, 99881, jnp.int32), jax.random.randint(jax.random.fold_in(jax.random.fold_in(_rk, 6), 32), (512,), 8, 99881, jnp.int32), jax.random.randint(jax.random.fold_in(jax.random.fold_in(_rk, 6), 33), (512,), 68, 99991, jnp.int32), jax.random.randint(jax.random.fold_in(jax.random.fold_in(_rk, 6), 34), (512,), 5, 99997, jnp.int32), jax.random.randint(jax.random.fold_in(jax.random.fold_in(_rk, 6), 35), (512,), 14, 99941, jnp.int32), jax.random.randint(jax.random.fold_in(jax.random.fold_in(_rk, 6), 36), (512,), 38, 99951, jnp.int32), jax.random.randint(jax.random.fold_in(jax.random.fold_in(_rk, 6), 37), (512,), 50, 12492, jnp.int32), jax.random.randint(jax.random.fold_in(jax.random.fold_in(_rk, 6), 38), (512,), 84, 99923, jnp.int32), jax.random.randint(jax.random.fold_in(jax.random.fold_in(_rk, 6), 39), (512,), 28, 99994, jnp.int32), jax.random.randint(jax.random.fold_in(jax.random.fold_in(_rk, 6), 40), (512,), 112, 99959, jnp.int32), jax.random.randint(jax.random.fold_in(jax.random.fold_in(_rk, 6), 41), (512,), 176, 99963, jnp.int32), jax.random.randint(jax.random.fold_in(jax.random.fold_in(_rk, 6), 42), (512,), 34, 99939, jnp.int32), jax.random.randint(jax.random.fold_in(jax.random.fold_in(_rk, 6), 43), (512,), 35, 99886, jnp.int32), jax.random.randint(jax.random.fold_in(jax.random.fold_in(_rk, 6), 44), (512,), 188, 99972, jnp.int32), jax.random.randint(jax.random.fold_in(jax.random.fold_in(_rk, 6), 45), (512,), 59, 99986, jnp.int32), jax.random.randint(jax.random.fold_in(jax.random.fold_in(_rk, 6), 46), (512,), 17, 12497, jnp.int32), jax.random.randint(jax.random.fold_in(jax.random.fold_in(_rk, 6), 47), (512,), 39, 99950, jnp.int32), jax.random.randint(jax.random.fold_in(jax.random.fold_in(_rk, 6), 48), (512,), 51, 99975, jnp.int32), jax.random.randint(jax.random.fold_in(jax.random.fold_in(_rk, 6), 49), (512,), 37, 99990, jnp.int32), jax.random.randint(jax.random.fold_in(jax.random.fold_in(_rk, 6), 50), (512,), 24, 99726, jnp.int32), jax.random.randint(jax.random.fold_in(jax.random.fold_in(_rk, 6), 51), (512,), 38, 99969, jnp.int32), jax.random.randint(jax.random.fold_in(jax.random.fold_in(_rk, 6), 52), (512,), 51, 12499, jnp.int32), jax.random.randint(jax.random.fold_in(jax.random.fold_in(_rk, 6), 53), (512,), 37, 99974, jnp.int32), jax.random.randint(jax.random.fold_in(jax.random.fold_in(_rk, 6), 54), (512,), 126, 99932, jnp.int32), jax.random.randint(jax.random.fold_in(jax.random.fold_in(_rk, 6), 55), (512,), 76, 99716, jnp.int32), jax.random.randint(jax.random.fold_in(jax.random.fold_in(_rk, 6), 56), (512,), 237, 99965, jnp.int32), jax.random.randint(jax.random.fold_in(jax.random.fold_in(_rk, 6), 57), (512,), 46, 99986, jnp.int32), jax.random.randint(jax.random.fold_in(jax.random.fold_in(_rk, 6), 58), (512,), 0, 99890, jnp.int32), jax.random.randint(jax.random.fold_in(jax.random.fold_in(_rk, 6), 59), (512,), 64, 99987, jnp.int32), jax.random.randint(jax.random.fold_in(jax.random.fold_in(_rk, 6), 60), (512,), 92, 99996, jnp.int32), jax.random.randint(jax.random.fold_in(jax.random.fold_in(_rk, 6), 61), (512,), 69, 12490, jnp.int32), jax.random.randint(jax.random.fold_in(jax.random.fold_in(_rk, 6), 62), (512,), 75, 99986, jnp.int32), jax.random.randint(jax.random.fold_in(jax.random.fold_in(_rk, 6), 63), (512,), 3, 99907, jnp.int32), jax.random.randint(jax.random.fold_in(jax.random.fold_in(_rk, 6), 64), (512,), 89, 99966, jnp.int32), jax.random.randint(jax.random.fold_in(jax.random.fold_in(_rk, 6), 65), (512,), 33, 99947, jnp.int32), jax.random.randint(jax.random.fold_in(jax.random.fold_in(_rk, 6), 66), (512,), 28, 99995, jnp.int32), jax.random.randint(jax.random.fold_in(jax.random.fold_in(_rk, 6), 67), (512,), 75, 99868, jnp.int32), jax.random.randint(jax.random.fold_in(jax.random.fold_in(_rk, 6), 68), (512,), 23, 99965, jnp.int32), jax.random.randint(jax.random.fold_in(jax.random.fold_in(_rk, 6), 69), (512,), 199, 99994, jnp.int32), jax.random.randint(jax.random.fold_in(jax.random.fold_in(_rk, 6), 70), (512,), 3, 12495, jnp.int32), jax.random.randint(jax.random.fold_in(jax.random.fold_in(_rk, 6), 71), (512,), 18, 99962, jnp.int32), jax.random.randint(jax.random.fold_in(jax.random.fold_in(_rk, 6), 72), (512,), 2, 99861, jnp.int32), jax.random.randint(jax.random.fold_in(jax.random.fold_in(_rk, 6), 73), (512,), 89, 12498, jnp.int32), jax.random.randint(jax.random.fold_in(jax.random.fold_in(_rk, 6), 74), (512,), 44, 99962, jnp.int32), jax.random.randint(jax.random.fold_in(jax.random.fold_in(_rk, 6), 75), (512,), 70, 12497, jnp.int32), jax.random.randint(jax.random.fold_in(jax.random.fold_in(_rk, 6), 76), (512,), 63, 99999, jnp.int32), jax.random.randint(jax.random.fold_in(jax.random.fold_in(_rk, 6), 77), (512,), 8, 99975, jnp.int32), jax.random.randint(jax.random.fold_in(jax.random.fold_in(_rk, 6), 78), (512,), 10, 99988, jnp.int32), jax.random.randint(jax.random.fold_in(jax.random.fold_in(_rk, 6), 79), (512,), 45, 12499, jnp.int32), jax.random.randint(jax.random.fold_in(jax.random.fold_in(_rk, 6), 80), (512,), 18, 99998, jnp.int32), jax.random.randint(jax.random.fold_in(jax.random.fold_in(_rk, 6), 81), (512,), 29, 99991, jnp.int32), jax.random.randint(jax.random.fold_in(jax.random.fold_in(_rk, 6), 82), (512,), 53, 99991, jnp.int32), jax.random.randint(jax.random.fold_in(jax.random.fold_in(_rk, 6), 83), (512,), 70, 12500, jnp.int32), jax.random.randint(jax.random.fold_in(jax.random.fold_in(_rk, 6), 84), (512,), 125, 99939, jnp.int32), jax.random.randint(jax.random.fold_in(jax.random.fold_in(_rk, 6), 85), (512,), 61, 99906, jnp.int32), jax.random.randint(jax.random.fold_in(jax.random.fold_in(_rk, 6), 86), (512,), 15, 99993, jnp.int32), jax.random.randint(jax.random.fold_in(jax.random.fold_in(_rk, 6), 87), (512,), 99, 99937, jnp.int32), jax.random.randint(jax.random.fold_in(jax.random.fold_in(_rk, 6), 88), (512,), 48, 99969, jnp.int32), jax.random.randint(jax.random.fold_in(jax.random.fold_in(_rk, 6), 89), (512,), 85, 99734, jnp.int32), jax.random.randint(jax.random.fold_in(jax.random.fold_in(_rk, 6), 90), (512,), 5, 99997, jnp.int32), jax.random.randint(jax.random.fold_in(jax.random.fold_in(_rk, 6), 91), (512,), 80, 99953, jnp.int32), jax.random.randint(jax.random.fold_in(jax.random.fold_in(_rk, 6), 92), (512,), 11, 99991, jnp.int32), jax.random.randint(jax.random.fold_in(jax.random.fold_in(_rk, 6), 93), (512,), 77, 99926, jnp.int32), jax.random.randint(jax.random.fold_in(jax.random.fold_in(_rk, 6), 94), (512,), 5, 12495, jnp.int32), jax.random.randint(jax.random.fold_in(jax.random.fold_in(_rk, 6), 95), (512,), 44, 99887, jnp.int32), jax.random.randint(jax.random.fold_in(jax.random.fold_in(_rk, 6), 96), (512,), 121, 99937, jnp.int32), jax.random.randint(jax.random.fold_in(jax.random.fold_in(_rk, 6), 97), (512,), 6, 12496, jnp.int32), jax.random.randint(jax.random.fold_in(jax.random.fold_in(_rk, 6), 98), (512,), 85, 99863, jnp.int32), jax.random.randint(jax.random.fold_in(jax.random.fold_in(_rk, 6), 99), (512,), 20, 99995, jnp.int32), jax.random.randint(jax.random.fold_in(jax.random.fold_in(_rk, 6), 100), (512,), 30, 99935, jnp.int32), jax.random.randint(jax.random.fold_in(jax.random.fold_in(_rk, 6), 101), (512,), 49, 99978, jnp.int32), jax.random.randint(jax.random.fold_in(jax.random.fold_in(_rk, 6), 102), (512,), 12, 99913, jnp.int32), jax.random.randint(jax.random.fold_in(jax.random.fold_in(_rk, 6), 103), (512,), 17, 12491, jnp.int32), jax.random.randint(jax.random.fold_in(jax.random.fold_in(_rk, 6), 104), (512,), 92, 99979, jnp.int32), jax.random.randint(jax.random.fold_in(jax.random.fold_in(_rk, 6), 105), (512,), 18, 99917, jnp.int32), jax.random.randint(jax.random.fold_in(jax.random.fold_in(_rk, 6), 106), (512,), 86, 99983, jnp.int32), jax.random.randint(jax.random.fold_in(jax.random.fold_in(_rk, 6), 107), (512,), 21, 99991, jnp.int32), jax.random.randint(jax.random.fold_in(jax.random.fold_in(_rk, 6), 108), (512,), 73, 99948, jnp.int32), jax.random.randint(jax.random.fold_in(jax.random.fold_in(_rk, 6), 109), (512,), 54, 99969, jnp.int32), jax.random.randint(jax.random.fold_in(jax.random.fold_in(_rk, 6), 110), (512,), 25, 99983, jnp.int32), jax.random.randint(jax.random.fold_in(jax.random.fold_in(_rk, 6), 111), (512,), 24, 99994, jnp.int32), jax.random.randint(jax.random.fold_in(jax.random.fold_in(_rk, 6), 112), (512,), 64, 99986, jnp.int32), jax.random.randint(jax.random.fold_in(jax.random.fold_in(_rk, 6), 113), (512,), 75, 99859, jnp.int32), jax.random.randint(jax.random.fold_in(jax.random.fold_in(_rk, 6), 114), (512,), 39, 99867, jnp.int32), jax.random.randint(jax.random.fold_in(jax.random.fold_in(_rk, 6), 115), (512,), 12, 99951, jnp.int32), jax.random.randint(jax.random.fold_in(jax.random.fold_in(_rk, 6), 116), (512,), 88, 99930, jnp.int32), jax.random.randint(jax.random.fold_in(jax.random.fold_in(_rk, 6), 117), (512,), 81, 99978, jnp.int32), jax.random.randint(jax.random.fold_in(jax.random.fold_in(_rk, 6), 118), (512,), 2, 99999, jnp.int32), jax.random.randint(jax.random.fold_in(jax.random.fold_in(_rk, 6), 119), (512,), 7, 99981, jnp.int32), jax.random.randint(jax.random.fold_in(jax.random.fold_in(_rk, 6), 120), (512,), 10, 99977, jnp.int32), jax.random.randint(jax.random.fold_in(jax.random.fold_in(_rk, 6), 121), (512,), 22, 99950, jnp.int32), jax.random.randint(jax.random.fold_in(jax.random.fold_in(_rk, 6), 122), (512,), 5, 99971, jnp.int32), jax.random.randint(jax.random.fold_in(jax.random.fold_in(_rk, 6), 123), (512,), 4, 99963, jnp.int32), jax.random.randint(jax.random.fold_in(jax.random.fold_in(_rk, 6), 124), (512,), 51, 99788, jnp.int32), jax.random.randint(jax.random.fold_in(jax.random.fold_in(_rk, 6), 125), (512,), 17, 12494, jnp.int32), jax.random.randint(jax.random.fold_in(jax.random.fold_in(_rk, 6), 126), (512,), 1, 99990, jnp.int32), jax.random.randint(jax.random.fold_in(jax.random.fold_in(_rk, 6), 127), (512,), 17, 99991, jnp.int32), jax.random.randint(jax.random.fold_in(jax.random.fold_in(_rk, 6), 128), (512,), 12, 99964, jnp.int32), jax.random.randint(jax.random.fold_in(jax.random.fold_in(_rk, 6), 129), (512,), 24, 99990, jnp.int32), jax.random.randint(jax.random.fold_in(jax.random.fold_in(_rk, 6), 130), (512,), 29, 99961, jnp.int32), jax.random.randint(jax.random.fold_in(jax.random.fold_in(_rk, 6), 131), (512,), 78, 99970, jnp.int32), jax.random.randint(jax.random.fold_in(jax.random.fold_in(_rk, 6), 132), (512,), 100, 99863, jnp.int32), jax.random.randint(jax.random.fold_in(jax.random.fold_in(_rk, 6), 133), (512,), 21, 99941, jnp.int32), jax.random.randint(jax.random.fold_in(jax.random.fold_in(_rk, 6), 134), (512,), 25, 99994, jnp.int32), jax.random.randint(jax.random.fold_in(jax.random.fold_in(_rk, 6), 135), (512,), 38, 99931, jnp.int32), jax.random.randint(jax.random.fold_in(jax.random.fold_in(_rk, 6), 136), (512,), 43, 99989, jnp.int32), jax.random.randint(jax.random.fold_in(jax.random.fold_in(_rk, 6), 137), (512,), 37, 99996, jnp.int32), jax.random.randint(jax.random.fold_in(jax.random.fold_in(_rk, 6), 138), (512,), 34, 99980, jnp.int32), jax.random.randint(jax.random.fold_in(jax.random.fold_in(_rk, 6), 139), (512,), 4, 99930, jnp.int32), jax.random.randint(jax.random.fold_in(jax.random.fold_in(_rk, 6), 140), (512,), 74, 99975, jnp.int32), jax.random.randint(jax.random.fold_in(jax.random.fold_in(_rk, 6), 141), (512,), 102, 99988, jnp.int32), jax.random.randint(jax.random.fold_in(jax.random.fold_in(_rk, 6), 142), (512,), 22, 99970, jnp.int32), jax.random.randint(jax.random.fold_in(jax.random.fold_in(_rk, 6), 143), (512,), 103, 99965, jnp.int32), jax.random.randint(jax.random.fold_in(jax.random.fold_in(_rk, 6), 144), (512,), 15, 99997, jnp.int32), jax.random.randint(jax.random.fold_in(jax.random.fold_in(_rk, 6), 145), (512,), 17, 99954, jnp.int32), jax.random.randint(jax.random.fold_in(jax.random.fold_in(_rk, 6), 146), (512,), 37, 12499, jnp.int32), jax.random.randint(jax.random.fold_in(jax.random.fold_in(_rk, 6), 147), (512,), 0, 99994, jnp.int32), jax.random.randint(jax.random.fold_in(jax.random.fold_in(_rk, 6), 148), (512,), 45, 99967, jnp.int32), jax.random.randint(jax.random.fold_in(jax.random.fold_in(_rk, 6), 149), (512,), 26, 99949, jnp.int32), jax.random.randint(jax.random.fold_in(jax.random.fold_in(_rk, 6), 150), (512,), 104, 99961, jnp.int32), jax.random.randint(jax.random.fold_in(jax.random.fold_in(_rk, 6), 151), (512,), 33, 99972, jnp.int32), jax.random.randint(jax.random.fold_in(jax.random.fold_in(_rk, 6), 152), (512,), 75, 99995, jnp.int32), jax.random.randint(jax.random.fold_in(jax.random.fold_in(_rk, 6), 153), (512,), 34, 99954, jnp.int32), jax.random.randint(jax.random.fold_in(jax.random.fold_in(_rk, 6), 154), (512,), 0, 99852, jnp.int32), jax.random.randint(jax.random.fold_in(jax.random.fold_in(_rk, 6), 155), (512,), 11, 99950, jnp.int32), jax.random.randint(jax.random.fold_in(jax.random.fold_in(_rk, 6), 156), (512,), 43, 99933, jnp.int32), jax.random.randint(jax.random.fold_in(jax.random.fold_in(_rk, 6), 157), (512,), 94, 99892, jnp.int32), jax.random.randint(jax.random.fold_in(jax.random.fold_in(_rk, 6), 158), (512,), 21, 99946, jnp.int32), jax.random.randint(jax.random.fold_in(jax.random.fold_in(_rk, 6), 159), (512,), 6, 99875, jnp.int32), jax.random.randint(jax.random.fold_in(jax.random.fold_in(_rk, 6), 160), (512,), 27, 99991, jnp.int32), jax.random.randint(jax.random.fold_in(jax.random.fold_in(_rk, 6), 161), (512,), 38, 99974, jnp.int32), jax.random.randint(jax.random.fold_in(jax.random.fold_in(_rk, 6), 162), (512,), 55, 99934, jnp.int32), jax.random.randint(jax.random.fold_in(jax.random.fold_in(_rk, 6), 163), (512,), 15, 12496, jnp.int32), jax.random.randint(jax.random.fold_in(jax.random.fold_in(_rk, 6), 164), (512,), 8, 99763, jnp.int32), jax.random.randint(jax.random.fold_in(jax.random.fold_in(_rk, 6), 165), (512,), 8, 99910, jnp.int32), jax.random.randint(jax.random.fold_in(jax.random.fold_in(_rk, 6), 166), (512,), 102, 99978, jnp.int32), jax.random.randint(jax.random.fold_in(jax.random.fold_in(_rk, 6), 167), (512,), 20, 99986, jnp.int32), jax.random.randint(jax.random.fold_in(jax.random.fold_in(_rk, 6), 168), (512,), 18, 99975, jnp.int32), jax.random.randint(jax.random.fold_in(jax.random.fold_in(_rk, 6), 169), (512,), 18, 99934, jnp.int32), jax.random.randint(jax.random.fold_in(jax.random.fold_in(_rk, 6), 170), (512,), 6, 99991, jnp.int32), jax.random.randint(jax.random.fold_in(jax.random.fold_in(_rk, 6), 171), (512,), 19, 99959, jnp.int32), jax.random.randint(jax.random.fold_in(jax.random.fold_in(_rk, 6), 172), (512,), 67, 99990, jnp.int32), jax.random.randint(jax.random.fold_in(jax.random.fold_in(_rk, 6), 173), (512,), 6, 99907, jnp.int32), jax.random.randint(jax.random.fold_in(jax.random.fold_in(_rk, 6), 174), (512,), 7, 99969, jnp.int32), jax.random.randint(jax.random.fold_in(jax.random.fold_in(_rk, 6), 175), (512,), 42, 99922, jnp.int32), jax.random.randint(jax.random.fold_in(jax.random.fold_in(_rk, 6), 176), (512,), 159, 99995, jnp.int32), jax.random.randint(jax.random.fold_in(jax.random.fold_in(_rk, 6), 177), (512,), 0, 99954, jnp.int32), jax.random.randint(jax.random.fold_in(jax.random.fold_in(_rk, 6), 178), (512,), 62, 99924, jnp.int32), jax.random.randint(jax.random.fold_in(jax.random.fold_in(_rk, 6), 179), (512,), 1, 99990, jnp.int32), jax.random.randint(jax.random.fold_in(jax.random.fold_in(_rk, 6), 180), (512,), 42, 99948, jnp.int32), jax.random.randint(jax.random.fold_in(jax.random.fold_in(_rk, 6), 181), (512,), 108, 12495, jnp.int32), jax.random.randint(jax.random.fold_in(jax.random.fold_in(_rk, 6), 182), (512,), 37, 99969, jnp.int32), jax.random.randint(jax.random.fold_in(jax.random.fold_in(_rk, 6), 183), (512,), 18, 99959, jnp.int32), jax.random.randint(jax.random.fold_in(jax.random.fold_in(_rk, 6), 184), (512,), 12, 99746, jnp.int32), jax.random.randint(jax.random.fold_in(jax.random.fold_in(_rk, 6), 185), (512,), 139, 99983, jnp.int32), jax.random.randint(jax.random.fold_in(jax.random.fold_in(_rk, 6), 186), (512,), 54, 99994, jnp.int32), jax.random.randint(jax.random.fold_in(jax.random.fold_in(_rk, 6), 187), (512,), 47, 99964, jnp.int32), jax.random.randint(jax.random.fold_in(jax.random.fold_in(_rk, 6), 188), (512,), 28, 12495, jnp.int32), jax.random.randint(jax.random.fold_in(jax.random.fold_in(_rk, 6), 189), (512,), 148, 99991, jnp.int32), jax.random.randint(jax.random.fold_in(jax.random.fold_in(_rk, 6), 190), (512,), 16, 12496, jnp.int32), jax.random.randint(jax.random.fold_in(jax.random.fold_in(_rk, 6), 191), (512,), 64, 99916, jnp.int32), jax.random.randint(jax.random.fold_in(jax.random.fold_in(_rk, 6), 192), (512,), 16, 99989, jnp.int32), jax.random.randint(jax.random.fold_in(jax.random.fold_in(_rk, 6), 193), (512,), 140, 12495, jnp.int32), jax.random.randint(jax.random.fold_in(jax.random.fold_in(_rk, 6), 194), (512,), 19, 99986, jnp.int32), jax.random.randint(jax.random.fold_in(jax.random.fold_in(_rk, 6), 195), (512,), 25, 99988, jnp.int32), jax.random.randint(jax.random.fold_in(jax.random.fold_in(_rk, 6), 196), (512,), 26, 99971, jnp.int32), jax.random.randint(jax.random.fold_in(jax.random.fold_in(_rk, 6), 197), (512,), 15, 99973, jnp.int32), jax.random.randint(jax.random.fold_in(jax.random.fold_in(_rk, 6), 198), (512,), 99, 12493, jnp.int32), jax.random.randint(jax.random.fold_in(jax.random.fold_in(_rk, 6), 199), (512,), 1, 12492, jnp.int32)], axis=1)
        r_hist_tag_ids = jnp.stack([jax.random.randint(jax.random.fold_in(jax.random.fold_in(_rk, 7), 0), (512,), 124, 12498, jnp.int32), jax.random.randint(jax.random.fold_in(jax.random.fold_in(_rk, 7), 1), (512,), 82, 99909, jnp.int32), jax.random.randint(jax.random.fold_in(jax.random.fold_in(_rk, 7), 2), (512,), 4, 99989, jnp.int32), jax.random.randint(jax.random.fold_in(jax.random.fold_in(_rk, 7), 3), (512,), 124, 99978, jnp.int32), jax.random.randint(jax.random.fold_in(jax.random.fold_in(_rk, 7), 4), (512,), 25, 99999, jnp.int32), jax.random.randint(jax.random.fold_in(jax.random.fold_in(_rk, 7), 5), (512,), 77, 99899, jnp.int32), jax.random.randint(jax.random.fold_in(jax.random.fold_in(_rk, 7), 6), (512,), 35, 99970, jnp.int32), jax.random.randint(jax.random.fold_in(jax.random.fold_in(_rk, 7), 7), (512,), 26, 12500, jnp.int32), jax.random.randint(jax.random.fold_in(jax.random.fold_in(_rk, 7), 8), (512,), 36, 99890, jnp.int32), jax.random.randint(jax.random.fold_in(jax.random.fold_in(_rk, 7), 9), (512,), 40, 99999, jnp.int32), jax.random.randint(jax.random.fold_in(jax.random.fold_in(_rk, 7), 10), (512,), 0, 99955, jnp.int32), jax.random.randint(jax.random.fold_in(jax.random.fold_in(_rk, 7), 11), (512,), 43, 99988, jnp.int32), jax.random.randint(jax.random.fold_in(jax.random.fold_in(_rk, 7), 12), (512,), 17, 99961, jnp.int32), jax.random.randint(jax.random.fold_in(jax.random.fold_in(_rk, 7), 13), (512,), 25, 99973, jnp.int32), jax.random.randint(jax.random.fold_in(jax.random.fold_in(_rk, 7), 14), (512,), 25, 99997, jnp.int32), jax.random.randint(jax.random.fold_in(jax.random.fold_in(_rk, 7), 15), (512,), 25, 99996, jnp.int32), jax.random.randint(jax.random.fold_in(jax.random.fold_in(_rk, 7), 16), (512,), 2, 12485, jnp.int32), jax.random.randint(jax.random.fold_in(jax.random.fold_in(_rk, 7), 17), (512,), 15, 99987, jnp.int32), jax.random.randint(jax.random.fold_in(jax.random.fold_in(_rk, 7), 18), (512,), 1, 12498, jnp.int32), jax.random.randint(jax.random.fold_in(jax.random.fold_in(_rk, 7), 19), (512,), 11, 99957, jnp.int32), jax.random.randint(jax.random.fold_in(jax.random.fold_in(_rk, 7), 20), (512,), 10, 99934, jnp.int32), jax.random.randint(jax.random.fold_in(jax.random.fold_in(_rk, 7), 21), (512,), 76, 99986, jnp.int32), jax.random.randint(jax.random.fold_in(jax.random.fold_in(_rk, 7), 22), (512,), 12, 99899, jnp.int32), jax.random.randint(jax.random.fold_in(jax.random.fold_in(_rk, 7), 23), (512,), 203, 99974, jnp.int32), jax.random.randint(jax.random.fold_in(jax.random.fold_in(_rk, 7), 24), (512,), 52, 99950, jnp.int32), jax.random.randint(jax.random.fold_in(jax.random.fold_in(_rk, 7), 25), (512,), 26, 99998, jnp.int32), jax.random.randint(jax.random.fold_in(jax.random.fold_in(_rk, 7), 26), (512,), 71, 99987, jnp.int32), jax.random.randint(jax.random.fold_in(jax.random.fold_in(_rk, 7), 27), (512,), 63, 99886, jnp.int32), jax.random.randint(jax.random.fold_in(jax.random.fold_in(_rk, 7), 28), (512,), 62, 99931, jnp.int32), jax.random.randint(jax.random.fold_in(jax.random.fold_in(_rk, 7), 29), (512,), 40, 99907, jnp.int32), jax.random.randint(jax.random.fold_in(jax.random.fold_in(_rk, 7), 30), (512,), 60, 99963, jnp.int32), jax.random.randint(jax.random.fold_in(jax.random.fold_in(_rk, 7), 31), (512,), 85, 99906, jnp.int32), jax.random.randint(jax.random.fold_in(jax.random.fold_in(_rk, 7), 32), (512,), 95, 99958, jnp.int32), jax.random.randint(jax.random.fold_in(jax.random.fold_in(_rk, 7), 33), (512,), 187, 99898, jnp.int32), jax.random.randint(jax.random.fold_in(jax.random.fold_in(_rk, 7), 34), (512,), 53, 99955, jnp.int32), jax.random.randint(jax.random.fold_in(jax.random.fold_in(_rk, 7), 35), (512,), 44, 99946, jnp.int32), jax.random.randint(jax.random.fold_in(jax.random.fold_in(_rk, 7), 36), (512,), 57, 99959, jnp.int32), jax.random.randint(jax.random.fold_in(jax.random.fold_in(_rk, 7), 37), (512,), 268, 12500, jnp.int32), jax.random.randint(jax.random.fold_in(jax.random.fold_in(_rk, 7), 38), (512,), 68, 99999, jnp.int32), jax.random.randint(jax.random.fold_in(jax.random.fold_in(_rk, 7), 39), (512,), 16, 99972, jnp.int32), jax.random.randint(jax.random.fold_in(jax.random.fold_in(_rk, 7), 40), (512,), 44, 99996, jnp.int32), jax.random.randint(jax.random.fold_in(jax.random.fold_in(_rk, 7), 41), (512,), 122, 99967, jnp.int32), jax.random.randint(jax.random.fold_in(jax.random.fold_in(_rk, 7), 42), (512,), 234, 99895, jnp.int32), jax.random.randint(jax.random.fold_in(jax.random.fold_in(_rk, 7), 43), (512,), 15, 99965, jnp.int32), jax.random.randint(jax.random.fold_in(jax.random.fold_in(_rk, 7), 44), (512,), 87, 99989, jnp.int32), jax.random.randint(jax.random.fold_in(jax.random.fold_in(_rk, 7), 45), (512,), 103, 99986, jnp.int32), jax.random.randint(jax.random.fold_in(jax.random.fold_in(_rk, 7), 46), (512,), 24, 12493, jnp.int32), jax.random.randint(jax.random.fold_in(jax.random.fold_in(_rk, 7), 47), (512,), 94, 99778, jnp.int32), jax.random.randint(jax.random.fold_in(jax.random.fold_in(_rk, 7), 48), (512,), 15, 99938, jnp.int32), jax.random.randint(jax.random.fold_in(jax.random.fold_in(_rk, 7), 49), (512,), 73, 12500, jnp.int32), jax.random.randint(jax.random.fold_in(jax.random.fold_in(_rk, 7), 50), (512,), 108, 99990, jnp.int32), jax.random.randint(jax.random.fold_in(jax.random.fold_in(_rk, 7), 51), (512,), 41, 99933, jnp.int32), jax.random.randint(jax.random.fold_in(jax.random.fold_in(_rk, 7), 52), (512,), 140, 99980, jnp.int32), jax.random.randint(jax.random.fold_in(jax.random.fold_in(_rk, 7), 53), (512,), 26, 99965, jnp.int32), jax.random.randint(jax.random.fold_in(jax.random.fold_in(_rk, 7), 54), (512,), 20, 99990, jnp.int32), jax.random.randint(jax.random.fold_in(jax.random.fold_in(_rk, 7), 55), (512,), 14, 99914, jnp.int32), jax.random.randint(jax.random.fold_in(jax.random.fold_in(_rk, 7), 56), (512,), 13, 12499, jnp.int32), jax.random.randint(jax.random.fold_in(jax.random.fold_in(_rk, 7), 57), (512,), 12, 99966, jnp.int32), jax.random.randint(jax.random.fold_in(jax.random.fold_in(_rk, 7), 58), (512,), 16, 99949, jnp.int32), jax.random.randint(jax.random.fold_in(jax.random.fold_in(_rk, 7), 59), (512,), 62, 99811, jnp.int32), jax.random.randint(jax.random.fold_in(jax.random.fold_in(_rk, 7), 60), (512,), 33, 99771, jnp.int32), jax.random.randint(jax.random.fold_in(jax.random.fold_in(_rk, 7), 61), (512,), 54, 99945, jnp.int32), jax.random.randint(jax.random.fold_in(jax.random.fold_in(_rk, 7), 62), (512,), 57, 99995, jnp.int32), jax.random.randint(jax.random.fold_in(jax.random.fold_in(_rk, 7), 63), (512,), 58, 99966, jnp.int32), jax.random.randint(jax.random.fold_in(jax.random.fold_in(_rk, 7), 64), (512,), 3, 99971, jnp.int32), jax.random.randint(jax.random.fold_in(jax.random.fold_in(_rk, 7), 65), (512,), 1, 99958, jnp.int32), jax.random.randint(jax.random.fold_in(jax.random.fold_in(_rk, 7), 66), (512,), 41, 12500, jnp.int32), jax.random.randint(jax.random.fold_in(jax.random.fold_in(_rk, 7), 67), (512,), 52, 99987, jnp.int32), jax.random.randint(jax.random.fold_in(jax.random.fold_in(_rk, 7), 68), (512,), 46, 99956, jnp.int32), jax.random.randint(jax.random.fold_in(jax.random.fold_in(_rk, 7), 69), (512,), 44, 99945, jnp.int32), jax.random.randint(jax.random.fold_in(jax.random.fold_in(_rk, 7), 70), (512,), 41, 12494, jnp.int32), jax.random.randint(jax.random.fold_in(jax.random.fold_in(_rk, 7), 71), (512,), 8, 99948, jnp.int32), jax.random.randint(jax.random.fold_in(jax.random.fold_in(_rk, 7), 72), (512,), 53, 12492, jnp.int32), jax.random.randint(jax.random.fold_in(jax.random.fold_in(_rk, 7), 73), (512,), 243, 99998, jnp.int32), jax.random.randint(jax.random.fold_in(jax.random.fold_in(_rk, 7), 74), (512,), 44, 99993, jnp.int32), jax.random.randint(jax.random.fold_in(jax.random.fold_in(_rk, 7), 75), (512,), 25, 99881, jnp.int32), jax.random.randint(jax.random.fold_in(jax.random.fold_in(_rk, 7), 76), (512,), 8, 99901, jnp.int32), jax.random.randint(jax.random.fold_in(jax.random.fold_in(_rk, 7), 77), (512,), 54, 99908, jnp.int32), jax.random.randint(jax.random.fold_in(jax.random.fold_in(_rk, 7), 78), (512,), 36, 99934, jnp.int32), jax.random.randint(jax.random.fold_in(jax.random.fold_in(_rk, 7), 79), (512,), 14, 99956, jnp.int32), jax.random.randint(jax.random.fold_in(jax.random.fold_in(_rk, 7), 80), (512,), 15, 99915, jnp.int32), jax.random.randint(jax.random.fold_in(jax.random.fold_in(_rk, 7), 81), (512,), 108, 99917, jnp.int32), jax.random.randint(jax.random.fold_in(jax.random.fold_in(_rk, 7), 82), (512,), 28, 12500, jnp.int32), jax.random.randint(jax.random.fold_in(jax.random.fold_in(_rk, 7), 83), (512,), 27, 99965, jnp.int32), jax.random.randint(jax.random.fold_in(jax.random.fold_in(_rk, 7), 84), (512,), 15, 99972, jnp.int32), jax.random.randint(jax.random.fold_in(jax.random.fold_in(_rk, 7), 85), (512,), 21, 99974, jnp.int32), jax.random.randint(jax.random.fold_in(jax.random.fold_in(_rk, 7), 86), (512,), 45, 99975, jnp.int32), jax.random.randint(jax.random.fold_in(jax.random.fold_in(_rk, 7), 87), (512,), 16, 99911, jnp.int32), jax.random.randint(jax.random.fold_in(jax.random.fold_in(_rk, 7), 88), (512,), 101, 99937, jnp.int32), jax.random.randint(jax.random.fold_in(jax.random.fold_in(_rk, 7), 89), (512,), 28, 99972, jnp.int32), jax.random.randint(jax.random.fold_in(jax.random.fold_in(_rk, 7), 90), (512,), 11, 99899, jnp.int32), jax.random.randint(jax.random.fold_in(jax.random.fold_in(_rk, 7), 91), (512,), 38, 99924, jnp.int32), jax.random.randint(jax.random.fold_in(jax.random.fold_in(_rk, 7), 92), (512,), 64, 12500, jnp.int32), jax.random.randint(jax.random.fold_in(jax.random.fold_in(_rk, 7), 93), (512,), 30, 99924, jnp.int32), jax.random.randint(jax.random.fold_in(jax.random.fold_in(_rk, 7), 94), (512,), 24, 99991, jnp.int32), jax.random.randint(jax.random.fold_in(jax.random.fold_in(_rk, 7), 95), (512,), 12, 99975, jnp.int32), jax.random.randint(jax.random.fold_in(jax.random.fold_in(_rk, 7), 96), (512,), 17, 99996, jnp.int32), jax.random.randint(jax.random.fold_in(jax.random.fold_in(_rk, 7), 97), (512,), 71, 99915, jnp.int32), jax.random.randint(jax.random.fold_in(jax.random.fold_in(_rk, 7), 98), (512,), 35, 12500, jnp.int32), jax.random.randint(jax.random.fold_in(jax.random.fold_in(_rk, 7), 99), (512,), 19, 99860, jnp.int32), jax.random.randint(jax.random.fold_in(jax.random.fold_in(_rk, 7), 100), (512,), 48, 99918, jnp.int32), jax.random.randint(jax.random.fold_in(jax.random.fold_in(_rk, 7), 101), (512,), 31, 99989, jnp.int32), jax.random.randint(jax.random.fold_in(jax.random.fold_in(_rk, 7), 102), (512,), 44, 99997, jnp.int32), jax.random.randint(jax.random.fold_in(jax.random.fold_in(_rk, 7), 103), (512,), 58, 99947, jnp.int32), jax.random.randint(jax.random.fold_in(jax.random.fold_in(_rk, 7), 104), (512,), 6, 99962, jnp.int32), jax.random.randint(jax.random.fold_in(jax.random.fold_in(_rk, 7), 105), (512,), 38, 99981, jnp.int32), jax.random.randint(jax.random.fold_in(jax.random.fold_in(_rk, 7), 106), (512,), 10, 12499, jnp.int32), jax.random.randint(jax.random.fold_in(jax.random.fold_in(_rk, 7), 107), (512,), 9, 99869, jnp.int32), jax.random.randint(jax.random.fold_in(jax.random.fold_in(_rk, 7), 108), (512,), 110, 99997, jnp.int32), jax.random.randint(jax.random.fold_in(jax.random.fold_in(_rk, 7), 109), (512,), 41, 99955, jnp.int32), jax.random.randint(jax.random.fold_in(jax.random.fold_in(_rk, 7), 110), (512,), 82, 99939, jnp.int32), jax.random.randint(jax.random.fold_in(jax.random.fold_in(_rk, 7), 111), (512,), 125, 99985, jnp.int32), jax.random.randint(jax.random.fold_in(jax.random.fold_in(_rk, 7), 112), (512,), 6, 99997, jnp.int32), jax.random.randint(jax.random.fold_in(jax.random.fold_in(_rk, 7), 113), (512,), 50, 99942, jnp.int32), jax.random.randint(jax.random.fold_in(jax.random.fold_in(_rk, 7), 114), (512,), 70, 99955, jnp.int32), jax.random.randint(jax.random.fold_in(jax.random.fold_in(_rk, 7), 115), (512,), 9, 99949, jnp.int32), jax.random.randint(jax.random.fold_in(jax.random.fold_in(_rk, 7), 116), (512,), 20, 99963, jnp.int32), jax.random.randint(jax.random.fold_in(jax.random.fold_in(_rk, 7), 117), (512,), 45, 99988, jnp.int32), jax.random.randint(jax.random.fold_in(jax.random.fold_in(_rk, 7), 118), (512,), 2, 99938, jnp.int32), jax.random.randint(jax.random.fold_in(jax.random.fold_in(_rk, 7), 119), (512,), 14, 12499, jnp.int32), jax.random.randint(jax.random.fold_in(jax.random.fold_in(_rk, 7), 120), (512,), 7, 99962, jnp.int32), jax.random.randint(jax.random.fold_in(jax.random.fold_in(_rk, 7), 121), (512,), 62, 99973, jnp.int32), jax.random.randint(jax.random.fold_in(jax.random.fold_in(_rk, 7), 122), (512,), 138, 99987, jnp.int32), jax.random.randint(jax.random.fold_in(jax.random.fold_in(_rk, 7), 123), (512,), 1, 99995, jnp.int32), jax.random.randint(jax.random.fold_in(jax.random.fold_in(_rk, 7), 124), (512,), 1, 99950, jnp.int32), jax.random.randint(jax.random.fold_in(jax.random.fold_in(_rk, 7), 125), (512,), 49, 99958, jnp.int32), jax.random.randint(jax.random.fold_in(jax.random.fold_in(_rk, 7), 126), (512,), 154, 99796, jnp.int32), jax.random.randint(jax.random.fold_in(jax.random.fold_in(_rk, 7), 127), (512,), 141, 99924, jnp.int32), jax.random.randint(jax.random.fold_in(jax.random.fold_in(_rk, 7), 128), (512,), 42, 99969, jnp.int32), jax.random.randint(jax.random.fold_in(jax.random.fold_in(_rk, 7), 129), (512,), 69, 12495, jnp.int32), jax.random.randint(jax.random.fold_in(jax.random.fold_in(_rk, 7), 130), (512,), 20, 99990, jnp.int32), jax.random.randint(jax.random.fold_in(jax.random.fold_in(_rk, 7), 131), (512,), 76, 99970, jnp.int32), jax.random.randint(jax.random.fold_in(jax.random.fold_in(_rk, 7), 132), (512,), 4, 99985, jnp.int32), jax.random.randint(jax.random.fold_in(jax.random.fold_in(_rk, 7), 133), (512,), 12, 99925, jnp.int32), jax.random.randint(jax.random.fold_in(jax.random.fold_in(_rk, 7), 134), (512,), 14, 99999, jnp.int32), jax.random.randint(jax.random.fold_in(jax.random.fold_in(_rk, 7), 135), (512,), 10, 99961, jnp.int32), jax.random.randint(jax.random.fold_in(jax.random.fold_in(_rk, 7), 136), (512,), 207, 12493, jnp.int32), jax.random.randint(jax.random.fold_in(jax.random.fold_in(_rk, 7), 137), (512,), 88, 99973, jnp.int32), jax.random.randint(jax.random.fold_in(jax.random.fold_in(_rk, 7), 138), (512,), 16, 99983, jnp.int32), jax.random.randint(jax.random.fold_in(jax.random.fold_in(_rk, 7), 139), (512,), 59, 99955, jnp.int32), jax.random.randint(jax.random.fold_in(jax.random.fold_in(_rk, 7), 140), (512,), 88, 99989, jnp.int32), jax.random.randint(jax.random.fold_in(jax.random.fold_in(_rk, 7), 141), (512,), 15, 99977, jnp.int32), jax.random.randint(jax.random.fold_in(jax.random.fold_in(_rk, 7), 142), (512,), 15, 99798, jnp.int32), jax.random.randint(jax.random.fold_in(jax.random.fold_in(_rk, 7), 143), (512,), 10, 99914, jnp.int32), jax.random.randint(jax.random.fold_in(jax.random.fold_in(_rk, 7), 144), (512,), 24, 12498, jnp.int32), jax.random.randint(jax.random.fold_in(jax.random.fold_in(_rk, 7), 145), (512,), 23, 99961, jnp.int32), jax.random.randint(jax.random.fold_in(jax.random.fold_in(_rk, 7), 146), (512,), 45, 12499, jnp.int32), jax.random.randint(jax.random.fold_in(jax.random.fold_in(_rk, 7), 147), (512,), 124, 99935, jnp.int32), jax.random.randint(jax.random.fold_in(jax.random.fold_in(_rk, 7), 148), (512,), 62, 99740, jnp.int32), jax.random.randint(jax.random.fold_in(jax.random.fold_in(_rk, 7), 149), (512,), 44, 99967, jnp.int32), jax.random.randint(jax.random.fold_in(jax.random.fold_in(_rk, 7), 150), (512,), 33, 99922, jnp.int32), jax.random.randint(jax.random.fold_in(jax.random.fold_in(_rk, 7), 151), (512,), 37, 99985, jnp.int32), jax.random.randint(jax.random.fold_in(jax.random.fold_in(_rk, 7), 152), (512,), 20, 99983, jnp.int32), jax.random.randint(jax.random.fold_in(jax.random.fold_in(_rk, 7), 153), (512,), 42, 99969, jnp.int32), jax.random.randint(jax.random.fold_in(jax.random.fold_in(_rk, 7), 154), (512,), 15, 99949, jnp.int32), jax.random.randint(jax.random.fold_in(jax.random.fold_in(_rk, 7), 155), (512,), 120, 99866, jnp.int32), jax.random.randint(jax.random.fold_in(jax.random.fold_in(_rk, 7), 156), (512,), 24, 12495, jnp.int32), jax.random.randint(jax.random.fold_in(jax.random.fold_in(_rk, 7), 157), (512,), 6, 99994, jnp.int32), jax.random.randint(jax.random.fold_in(jax.random.fold_in(_rk, 7), 158), (512,), 23, 12497, jnp.int32), jax.random.randint(jax.random.fold_in(jax.random.fold_in(_rk, 7), 159), (512,), 10, 99929, jnp.int32), jax.random.randint(jax.random.fold_in(jax.random.fold_in(_rk, 7), 160), (512,), 52, 12487, jnp.int32), jax.random.randint(jax.random.fold_in(jax.random.fold_in(_rk, 7), 161), (512,), 9, 99969, jnp.int32), jax.random.randint(jax.random.fold_in(jax.random.fold_in(_rk, 7), 162), (512,), 16, 99849, jnp.int32), jax.random.randint(jax.random.fold_in(jax.random.fold_in(_rk, 7), 163), (512,), 36, 99926, jnp.int32), jax.random.randint(jax.random.fold_in(jax.random.fold_in(_rk, 7), 164), (512,), 24, 99995, jnp.int32), jax.random.randint(jax.random.fold_in(jax.random.fold_in(_rk, 7), 165), (512,), 66, 99988, jnp.int32), jax.random.randint(jax.random.fold_in(jax.random.fold_in(_rk, 7), 166), (512,), 70, 99839, jnp.int32), jax.random.randint(jax.random.fold_in(jax.random.fold_in(_rk, 7), 167), (512,), 36, 99949, jnp.int32), jax.random.randint(jax.random.fold_in(jax.random.fold_in(_rk, 7), 168), (512,), 6, 99977, jnp.int32), jax.random.randint(jax.random.fold_in(jax.random.fold_in(_rk, 7), 169), (512,), 40, 12496, jnp.int32), jax.random.randint(jax.random.fold_in(jax.random.fold_in(_rk, 7), 170), (512,), 31, 99979, jnp.int32), jax.random.randint(jax.random.fold_in(jax.random.fold_in(_rk, 7), 171), (512,), 20, 99990, jnp.int32), jax.random.randint(jax.random.fold_in(jax.random.fold_in(_rk, 7), 172), (512,), 78, 99929, jnp.int32), jax.random.randint(jax.random.fold_in(jax.random.fold_in(_rk, 7), 173), (512,), 58, 12498, jnp.int32), jax.random.randint(jax.random.fold_in(jax.random.fold_in(_rk, 7), 174), (512,), 28, 99951, jnp.int32), jax.random.randint(jax.random.fold_in(jax.random.fold_in(_rk, 7), 175), (512,), 16, 99932, jnp.int32), jax.random.randint(jax.random.fold_in(jax.random.fold_in(_rk, 7), 176), (512,), 106, 99950, jnp.int32), jax.random.randint(jax.random.fold_in(jax.random.fold_in(_rk, 7), 177), (512,), 48, 99926, jnp.int32), jax.random.randint(jax.random.fold_in(jax.random.fold_in(_rk, 7), 178), (512,), 7, 99970, jnp.int32), jax.random.randint(jax.random.fold_in(jax.random.fold_in(_rk, 7), 179), (512,), 18, 99815, jnp.int32), jax.random.randint(jax.random.fold_in(jax.random.fold_in(_rk, 7), 180), (512,), 36, 99958, jnp.int32), jax.random.randint(jax.random.fold_in(jax.random.fold_in(_rk, 7), 181), (512,), 20, 99983, jnp.int32), jax.random.randint(jax.random.fold_in(jax.random.fold_in(_rk, 7), 182), (512,), 62, 99943, jnp.int32), jax.random.randint(jax.random.fold_in(jax.random.fold_in(_rk, 7), 183), (512,), 119, 99957, jnp.int32), jax.random.randint(jax.random.fold_in(jax.random.fold_in(_rk, 7), 184), (512,), 119, 99946, jnp.int32), jax.random.randint(jax.random.fold_in(jax.random.fold_in(_rk, 7), 185), (512,), 11, 99881, jnp.int32), jax.random.randint(jax.random.fold_in(jax.random.fold_in(_rk, 7), 186), (512,), 16, 12496, jnp.int32), jax.random.randint(jax.random.fold_in(jax.random.fold_in(_rk, 7), 187), (512,), 22, 99957, jnp.int32), jax.random.randint(jax.random.fold_in(jax.random.fold_in(_rk, 7), 188), (512,), 40, 99965, jnp.int32), jax.random.randint(jax.random.fold_in(jax.random.fold_in(_rk, 7), 189), (512,), 25, 99889, jnp.int32), jax.random.randint(jax.random.fold_in(jax.random.fold_in(_rk, 7), 190), (512,), 79, 99855, jnp.int32), jax.random.randint(jax.random.fold_in(jax.random.fold_in(_rk, 7), 191), (512,), 80, 99820, jnp.int32), jax.random.randint(jax.random.fold_in(jax.random.fold_in(_rk, 7), 192), (512,), 33, 99996, jnp.int32), jax.random.randint(jax.random.fold_in(jax.random.fold_in(_rk, 7), 193), (512,), 4, 99956, jnp.int32), jax.random.randint(jax.random.fold_in(jax.random.fold_in(_rk, 7), 194), (512,), 33, 99943, jnp.int32), jax.random.randint(jax.random.fold_in(jax.random.fold_in(_rk, 7), 195), (512,), 52, 12495, jnp.int32), jax.random.randint(jax.random.fold_in(jax.random.fold_in(_rk, 7), 196), (512,), 59, 99981, jnp.int32), jax.random.randint(jax.random.fold_in(jax.random.fold_in(_rk, 7), 197), (512,), 10, 99961, jnp.int32), jax.random.randint(jax.random.fold_in(jax.random.fold_in(_rk, 7), 198), (512,), 46, 99890, jnp.int32), jax.random.randint(jax.random.fold_in(jax.random.fold_in(_rk, 7), 199), (512,), 23, 99973, jnp.int32)], axis=1)
        r_hist_mask = jax.random.randint(jax.random.fold_in(_rk, 8), (512, 200), 0, 2, jnp.int32)
        r_item_cat = jnp.stack([jax.random.randint(jax.random.fold_in(jax.random.fold_in(_rk, 9), 0), (512,), 22, 99997, jnp.int32), jax.random.randint(jax.random.fold_in(jax.random.fold_in(_rk, 9), 1), (512,), 3, 99978, jnp.int32), jax.random.randint(jax.random.fold_in(jax.random.fold_in(_rk, 9), 2), (512,), 78, 99971, jnp.int32), jax.random.randint(jax.random.fold_in(jax.random.fold_in(_rk, 9), 3), (512,), 16, 99998, jnp.int32), jax.random.randint(jax.random.fold_in(jax.random.fold_in(_rk, 9), 4), (512,), 41, 12491, jnp.int32), jax.random.randint(jax.random.fold_in(jax.random.fold_in(_rk, 9), 5), (512,), 26, 12496, jnp.int32), jax.random.randint(jax.random.fold_in(jax.random.fold_in(_rk, 9), 6), (512,), 53, 12493, jnp.int32), jax.random.randint(jax.random.fold_in(jax.random.fold_in(_rk, 9), 7), (512,), 8, 99974, jnp.int32)], axis=1)
        r_item_num = -0.00268083 + 0.997254 * jax.random.normal(jax.random.fold_in(_rk, 10), (512, 6), jnp.float32)
        return (r_user_num, r_user_cat, r_ctx_cat, r_ctx_num, r_hist_ids, r_hist_author_ids, r_hist_tag_ids, r_hist_mask, r_item_cat, r_item_num)
    r_user_num, r_user_cat, r_ctx_cat, r_ctx_num, r_hist_ids, r_hist_author_ids, r_hist_tag_ids, r_hist_mask, r_item_cat, r_item_num = _rec_inputs()

    def _L0_rec_setup():
        import jax, jax.numpy as jnp
        import numpy as np
        B, L, E, V = (256, 200, 64, 12500)
        NU, NI, NC = (6, 8, 4)
        DU, DI, DC = (8, 6, 4)
        HID, MID = (256, 128)
        FEAT = (NU + NI + NC) * E + 8 * E
        D1H, D2H, D3H = (512, 256, 256)

        def _mlp3(x, W1, b1, W2, b2, W3, b3):
            h = jax.nn.relu(x @ W1 + b1)
            h = jax.nn.relu(h @ W2 + b2)
            return h @ W3 + b3

        def _gather_group(tables, cat):
            return jax.vmap(lambda t, i: t[i], in_axes=(0, 1), out_axes=1)(tables, cat)

        def _mean_pool(emb, maskf):
            m = maskf[..., None]
            return (emb * m).sum(1) / jnp.maximum(m.sum(1), 1e-06)
        key = jax.random.key(seed)
        ks = iter(jax.random.split(key, 48))
        nk = lambda: next(ks)
        s = 0.02
        inp = {}
        inp['user_cat'] = jax.random.randint(nk(), (B, NU), 0, V)
        inp['user_num'] = jax.random.normal(nk(), (B, DU), jnp.float32)
        inp['ctx_cat'] = jax.random.randint(nk(), (B, NC), 0, V)
        inp['ctx_num'] = jax.random.normal(nk(), (B, DC), jnp.float32)
        inp['hist_ids'] = jax.random.randint(nk(), (B, L), 0, V)
        inp['hist_author_ids'] = jax.random.randint(nk(), (B, L), 0, V)
        inp['hist_tag_ids'] = jax.random.randint(nk(), (B, L), 0, V)
        inp['hist_mask'] = jax.random.randint(nk(), (B, L), 0, 2)
        inp['item_cat'] = jax.random.randint(nk(), (B, NI), 0, V)
        inp['item_num'] = jax.random.normal(nk(), (B, DI), jnp.float32)
        inp['user_emb'] = jax.random.normal(nk(), (NU, V, E), jnp.float32) * s
        inp['item_emb'] = jax.random.normal(nk(), (NI, V, E), jnp.float32) * s
        inp['ctx_emb'] = jax.random.normal(nk(), (NC, V, E), jnp.float32) * s
        inp['Wu'] = jax.random.normal(nk(), (DU, E)) * s
        inp['bu'] = jnp.zeros((E,))
        inp['Wi'] = jax.random.normal(nk(), (DI, E)) * s
        inp['bi'] = jnp.zeros((E,))
        inp['Wc'] = jax.random.normal(nk(), (DC, E)) * s
        inp['bc'] = jnp.zeros((E,))
        inp['A1'] = jax.random.normal(nk(), (4 * E, HID)) * s
        inp['a1'] = jnp.zeros((HID,))
        inp['A2'] = jax.random.normal(nk(), (HID, MID)) * s
        inp['a2'] = jnp.zeros((MID,))
        inp['A3'] = jax.random.normal(nk(), (MID, 1)) * s
        inp['a3'] = jnp.zeros((1,))
        inp['cross_w'] = jax.random.normal(nk(), (3, FEAT)) * s
        inp['cross_b'] = jnp.zeros((3, FEAT))
        inp['D1'] = jax.random.normal(nk(), (FEAT, D1H)) * s
        inp['d1'] = jnp.zeros((D1H,))
        inp['D2'] = jax.random.normal(nk(), (D1H, D2H)) * s
        inp['d2'] = jnp.zeros((D2H,))
        inp['D3'] = jax.random.normal(nk(), (D2H, D3H)) * s
        inp['d3'] = jnp.zeros((D3H,))
        inp['Wh'] = jax.random.normal(nk(), (FEAT + D3H, 1)) * s
        inp['bh'] = jnp.zeros((1,))
        return inp
    _L0_rec_all = _L0_rec_setup()
    _L0_rec_in = {k: v for k, v in _L0_rec_all.items() if k in ('user_emb', 'item_emb', 'ctx_emb', 'Wu', 'bu', 'Wi', 'bi', 'Wc', 'bc', 'A1', 'a1', 'A2', 'a2', 'A3', 'a3', 'cross_w', 'cross_b', 'D1', 'd1', 'D2', 'd2', 'D3', 'd3', 'Wh', 'bh')}
    del _L0_rec_all
    return {'r_user_num': r_user_num, 'r_user_cat': r_user_cat, 'r_ctx_cat': r_ctx_cat, 'r_ctx_num': r_ctx_num, 'r_hist_ids': r_hist_ids, 'r_hist_author_ids': r_hist_author_ids, 'r_hist_tag_ids': r_hist_tag_ids, 'r_hist_mask': r_hist_mask, 'r_item_cat': r_item_cat, 'r_item_num': r_item_num, 'L0_rec_user_emb': _L0_rec_in['user_emb'], 'L0_rec_item_emb': _L0_rec_in['item_emb'], 'L0_rec_ctx_emb': _L0_rec_in['ctx_emb'], 'L0_rec_Wu': _L0_rec_in['Wu'], 'L0_rec_bu': _L0_rec_in['bu'], 'L0_rec_Wi': _L0_rec_in['Wi'], 'L0_rec_bi': _L0_rec_in['bi'], 'L0_rec_Wc': _L0_rec_in['Wc'], 'L0_rec_bc': _L0_rec_in['bc'], 'L0_rec_A1': _L0_rec_in['A1'], 'L0_rec_a1': _L0_rec_in['a1'], 'L0_rec_A2': _L0_rec_in['A2'], 'L0_rec_a2': _L0_rec_in['a2'], 'L0_rec_A3': _L0_rec_in['A3'], 'L0_rec_a3': _L0_rec_in['a3'], 'L0_rec_cross_w': _L0_rec_in['cross_w'], 'L0_rec_cross_b': _L0_rec_in['cross_b'], 'L0_rec_D1': _L0_rec_in['D1'], 'L0_rec_d1': _L0_rec_in['d1'], 'L0_rec_D2': _L0_rec_in['D2'], 'L0_rec_d2': _L0_rec_in['d2'], 'L0_rec_D3': _L0_rec_in['D3'], 'L0_rec_d3': _L0_rec_in['d3'], 'L0_rec_Wh': _L0_rec_in['Wh'], 'L0_rec_bh': _L0_rec_in['bh']}

def reference(r_user_num, r_user_cat, r_ctx_cat, r_ctx_num, r_hist_ids, r_hist_author_ids, r_hist_tag_ids, r_hist_mask, r_item_cat, r_item_num, L0_rec_user_emb, L0_rec_item_emb, L0_rec_ctx_emb, L0_rec_Wu, L0_rec_bu, L0_rec_Wi, L0_rec_bi, L0_rec_Wc, L0_rec_bc, L0_rec_A1, L0_rec_a1, L0_rec_A2, L0_rec_a2, L0_rec_A3, L0_rec_a3, L0_rec_cross_w, L0_rec_cross_b, L0_rec_D1, L0_rec_d1, L0_rec_D2, L0_rec_d2, L0_rec_D3, L0_rec_d3, L0_rec_Wh, L0_rec_bh):
    import jax
    import jax.numpy as jnp

    def _L0_rec_ref(user_cat, user_num, ctx_cat, ctx_num, hist_ids, hist_author_ids, hist_tag_ids, hist_mask, item_cat, item_num, user_emb, item_emb, ctx_emb, Wu, bu, Wi, bi, Wc, bc, A1, a1, A2, a2, A3, a3, cross_w, cross_b, D1, d1, D2, d2, D3, d3, Wh, bh):
        import jax, jax.numpy as jnp
        import numpy as np
        B, L, E, V = (256, 200, 64, 12500)
        NU, NI, NC = (6, 8, 4)
        DU, DI, DC = (8, 6, 4)
        HID, MID = (256, 128)
        FEAT = (NU + NI + NC) * E + 8 * E
        D1H, D2H, D3H = (512, 256, 256)

        def _mlp3(x, W1, b1, W2, b2, W3, b3):
            h = jax.nn.relu(x @ W1 + b1)
            h = jax.nn.relu(h @ W2 + b2)
            return h @ W3 + b3

        def _gather_group(tables, cat):
            return jax.vmap(lambda t, i: t[i], in_axes=(0, 1), out_axes=1)(tables, cat)

        def _mean_pool(emb, maskf):
            m = maskf[..., None]
            return (emb * m).sum(1) / jnp.maximum(m.sum(1), 1e-06)
        user_g = _gather_group(user_emb, user_cat)
        item_g = _gather_group(item_emb, item_cat)
        ctx_g = _gather_group(ctx_emb, ctx_cat)
        u_num = jax.nn.relu(user_num @ Wu + bu)
        i_num = jax.nn.relu(item_num @ Wi + bi)
        c_num = jax.nn.relu(ctx_num @ Wc + bc)
        target_video = item_g[:, 0]
        hist_emb = item_emb[0][hist_ids]
        maskf = hist_mask.astype(jnp.float32)
        q = jnp.broadcast_to(target_video[:, None, :], hist_emb.shape)
        attn_in = jnp.concatenate([q, hist_emb, q - hist_emb, q * hist_emb], axis=-1)
        score = _mlp3(attn_in, A1, a1, A2, a2, A3, a3)[..., 0]
        score = jnp.where(hist_mask <= 0, -1000000000.0, score)
        w = jax.nn.softmax(score, axis=-1) * maskf
        w = w / jnp.maximum(w.sum(-1, keepdims=True), 1e-06)
        hist_att = (w[..., None] * hist_emb).sum(1)
        author_pool = _mean_pool(item_emb[1][hist_author_ids], maskf)
        tag_pool = _mean_pool(item_emb[7][hist_tag_ids], maskf)
        base = jnp.concatenate([user_g.reshape(user_g.shape[0], -1), item_g.reshape(item_g.shape[0], -1), ctx_g.reshape(ctx_g.shape[0], -1), u_num, i_num, c_num, hist_att, author_pool, tag_pool, target_video * hist_att, target_video - hist_att], axis=-1)
        xl = base
        for k in range(cross_w.shape[0]):
            xw = (xl * cross_w[k]).sum(-1, keepdims=True)
            xl = base * xw + cross_b[k] + xl
        deep = _mlp3(base, D1, d1, D2, d2, D3, d3)
        final = jnp.concatenate([xl, deep], axis=-1)
        return (final @ Wh + bh)[..., 0]
    y = _L0_rec_ref(r_user_cat, r_user_num, r_ctx_cat, r_ctx_num, r_hist_ids, r_hist_author_ids, r_hist_tag_ids, r_hist_mask, r_item_cat, r_item_num, L0_rec_user_emb, L0_rec_item_emb, L0_rec_ctx_emb, L0_rec_Wu, L0_rec_bu, L0_rec_Wi, L0_rec_bi, L0_rec_Wc, L0_rec_bc, L0_rec_A1, L0_rec_a1, L0_rec_A2, L0_rec_a2, L0_rec_A3, L0_rec_a3, L0_rec_cross_w, L0_rec_cross_b, L0_rec_D1, L0_rec_d1, L0_rec_D2, L0_rec_d2, L0_rec_D3, L0_rec_d3, L0_rec_Wh, L0_rec_bh)
    return y

_drawn_inputs = setup_inputs


def setup_inputs(seed=0):
    import zlib

    import numpy as np

    out = dict(_drawn_inputs(seed))
    spreads = {'L0_rec_bu': (0.0, 0.1),
     'L0_rec_bi': (0.0, 0.41),
     'L0_rec_bc': (0.0, 0.1),
     'L0_rec_a1': (0.0, 2.0),
     'L0_rec_a2': (0.0, 2.0),
     'L0_rec_cross_b': (0.0, 0.1),
     'L0_rec_d1': (0.0, 0.8),
     'L0_rec_d2': (0.0, 0.395),
     'L0_rec_d3': (0.0, 0.1)}
    factors = {'r_item_num': 3.284,
     'L0_rec_A1': 64.0,
     'L0_rec_A2': 64.0,
     'L0_rec_A3': 64.0,
     'L0_rec_cross_w': 3.871,
     'L0_rec_D1': 8.0,
     'L0_rec_D2': 8.0}
    for name, (base, spread) in spreads.items():
        noise = np.random.default_rng([zlib.crc32(name.encode()), seed]).standard_normal(out[name].shape)
        drawn = base * np.exp(spread * noise) if base else spread * noise
        out[name] = jnp.asarray(drawn.astype(out[name].dtype))
    for name, factor in factors.items():
        out[name] = (out[name] * factor).astype(out[name].dtype)
    return out
```

```python
from contextlib import ExitStack

import concourse.bass as bass
from concourse import mybir

ALU = mybir.AluOpType
ACT = mybir.ActivationFunctionType
AX_X = mybir.AxisListType.X
F32 = mybir.dt.float32
BF16 = mybir.dt.bfloat16
I32 = mybir.dt.int32
U32 = mybir.dt.uint32

P = 128


def recommender(nc, user_cat, user_num, ctx_cat, ctx_num, hist_ids, author_ids, tag_ids, hist_mask,
                item_cat, item_num, user_emb, item_emb, ctx_emb, Wu, bu, Wi, bi, Wc, bc,
                A1, a1, A2, a2, A3, a3, cross_w, cross_b, D1, d1, D2, d2, D3, d3, Wh, bh, out):
    B, L = hist_ids.shape
    V, E = item_emb.shape[1:]
    NU, NI, NC = user_cat.shape[1], item_cat.shape[1], ctx_cat.shape[1]
    NCAT = NU + NI + NC
    HID, MID = A2.shape
    FEAT, H1 = D1.shape
    H2, H3 = D2.shape[1], D3.shape[1]
    Q = B // P
    HALF = B // 2
    PB = 16
    NBLK = HALF // PB
    CH = PB * L // P
    TG = -(-CH // 4)
    HC = HALF * L // P
    LH = L // 2
    NHI = -(-V // P)
    VS = 4
    KT = FEAT // P
    HK, M1, M2 = HID // P, H1 // P, H2 // P
    GR = 100
    assert 2 * E == P and PB * L == CH * P and NBLK % 2 == 0 and VS * PB * NBLK == 2 * B
    assert HK == 2 and MID == P and FEAT == KT * P and H3 == H2

    R_CW, R_CB, R_WH = 0, 3 * KT, 6 * KT
    R_WH2 = R_WH + KT
    R_A1 = R_WH2 + M2
    R_A2 = R_A1 + HK
    R_A3 = R_A2 + 1
    R_D1 = R_A3 + 1
    R_D2 = R_D1 + M1
    R_D3 = R_D2 + M2
    NR = R_D3 + M2
    F_ITEM, F_CTX, F_NUM = NU * E, (NU + NI) * E, NCAT * E
    F_ATT = F_NUM + 3 * E
    F_POOL = F_ATT + E
    F_MUL, F_DIF = F_POOL + 2 * E, F_POOL + 3 * E

    with ExitStack() as ctx:
        def sb(name, shape, dt=F32):
            return ctx.enter_context(nc.sbuf_tensor(name, shape, dt))

        def sem(name):
            return ctx.enter_context(nc.semaphore(name))

        emb = sb("emb", [P, CH, 2 * E])
        embT = sb("embT", [P, 2, CH * P])
        h1 = sb("h1", [P, 2, HK, 2 * L])
        h2 = sb("h2", [P, 2, 2 * L])
        parts_r = sb("parts", [P, 2, NHI * 3 * E], BF16)
        cnt_r = sb("cnt", [P, KT * B])
        oh_lo = sb("oh_lo", [P, 2, 2 * VS, P], BF16)
        oh_hi = sb("oh_hi", [P, 2, 2 * VS, NHI], BF16)
        wq = sb("wq", [P, 2, HID])
        sel = sb("sel", [32, PB, P])
        A1p = sb("A1p", [P, HID])
        A1hd = sb("A1hd", [P, HID])
        A2s = sb("A2s", [P, HK, MID])
        A3s = sb("A3s", [P, 32])
        iota = sb("iota", [P, P], BF16)
        ident = sb("ident", [P, P])
        idT = sb("idT", [P, 2, 2 * B * 2], BF16)
        hidx = sb("hidx", [P, 2, HC], U32)
        istage = sb("istage", [P, 2, 2, CH], U32)
        qT = sb("qT", [P, HALF])
        qbias = sb("qbias", [P, HK, 2, HALF])
        attS = sb("attS", [P, 2, PB])
        attT = sb("attT", [P, HALF])
        junk = sb("junk", [P, 2, L])
        msk = sb("msk", [32, NBLK, L], BF16)
        srow = sb("srow", [P, 2, 2 * L])
        Sc = sb("Sc", [32, L])
        smk = sb("smk", [32, L])
        mkb = sb("mkb", [32, L], BF16)
        ex = sb("ex", [32, L])
        exm = sb("exm", [32, L])
        wts = sb("wts", [32, L])
        pen = wts
        st = sb("st", [32, 8])
        cat_i = sb("cat_i", [P, Q, NCAT], I32)
        cat_w = sb("cat_w", [P, Q, NCAT])
        cat_f = sb("cat_f", [P, Q, NCAT])
        cat_x = sb("cat_x", [P, NCAT, Q], U32)
        tv = sb("tv", [P, Q, E])
        pooled = sb("pooled", [P, 2 * Q, E])
        rlen = sb("rlen", [P, Q])
        vrow = sb("vrow", [NR, P])
        vecT = sb("vecT", [P, NR])
        a3c = sb("a3c", [P, 1])
        bhc = sb("bhc", [P, 1])
        nums = sb("nums", [P, Q, 19])
        Wn = sb("Wn", [19, 3 * E])
        kpart = sb("kpart", [P, 4, KT])
        kk = sb("kk", [P, 4])
        xw = sb("xw", [P, KT, 4])
        fin = sb("fin", [P, 12, Q])

        parts = [parts_r[:, t, :].rearrange("p (h e) -> p h e", e=3 * E) for t in range(2)]
        cnt = cnt_r[:, :].bitcast(BF16)[:, 0:NHI * P].rearrange("p (h v) -> p h v", v=P)
        baseT = cnt_r[:, :].rearrange("p (k b) -> p k b", b=B)
        tab = [embT[:, :, :].rearrange("p a b -> p (a b)")[:, 0:NHI * E].rearrange("p (h e) -> p h e", e=E),
               cnt_r[:, 0:NHI * E].rearrange("p (h e) -> p h e", e=E)]
        low = parts_r[:, 0, :].bitcast(F32)
        high = parts_r[:, 1, :].bitcast(F32)
        base = low[:, 0:Q * FEAT].rearrange("p (q f) -> p q f", f=FEAT)
        hid_i = low[0:GR, 0:1024].bitcast(I32)
        hid_w = low[0:GR, 1024:2048]
        hid_f = low[0:GR, 2048:3072]
        A1d = low[:, 3072:4096].rearrange("p (f n) -> p f n", n=HID)
        A1s = low[:, 4096:4096 + HID]
        QL = Q * L
        ids_i = [high[:, 0:QL].bitcast(I32), high[:, QL:2 * QL].bitcast(I32)]
        msk_i = high[:, 2 * QL:3 * QL].bitcast(I32)
        ids_w = high[:, 3 * QL:4 * QL]
        ids_f = high[:, 4 * QL:5 * QL]
        ids_c = high[:, 5 * QL:6 * QL].bitcast(I32)
        tag_lo, tag_hi = high[:, 0:QL], high[:, QL:2 * QL]
        mb_i = high[0:32, 6 * QL:6 * QL + NBLK * L].bitcast(I32)
        assert 6 * QL + NBLK * L <= NHI * 3 * E // 2 and Q * FEAT <= NHI * 3 * E // 2
        D1s = high[:, 0:KT * H1].rearrange("p (k n) -> p k n", n=H1)
        D2s = high[:, KT * H1:KT * H1 + M1 * H2].rearrange("p (k n) -> p k n", n=H2)
        D3s = high[:, KT * H1 + M1 * H2:KT * H1 + M1 * H2 + M2 * H3].rearrange("p (k n) -> p k n", n=H3)
        embf = emb[:, :, :].rearrange("p a b -> p (a b)")
        g1 = embf[:, 0:M1 * B].rearrange("p (k b) -> p k b", b=B)
        g2 = h1[:, :, :, :].rearrange("p a b c -> p (a b c)")[:, 0:M2 * B].rearrange("p (k b) -> p k b", b=B)
        g3 = embf[:, M1 * B:M1 * B + M2 * B].rearrange("p (k b) -> p k b", b=B)
        iota_i = junk[:, 0, 0:P].bitcast(I32)
        numT = oh_lo[:, :, :, :].rearrange("p a b c -> p (a b c)").bitcast(F32)[0:19, 0:B]
        onesq = wq[:, 0, 0:P]
        finT = pen[0:Q, 0:P]
        tvq = tv[:, :, :].rearrange("p (a b) e -> p b a e", a=2)

        def by_quarter(x):
            return x.rearrange("p (b a) e -> p b a e", a=2)

        xrow = srow[0:4, :, :].rearrange("p a b -> p (a b)")[:, 0:B]
        drow = h2[0:1, :, :].rearrange("p a b -> p (a b)")[:, 0:B]

        ps = ctx.enter_context(nc.psum_tensor("ps", [P, 8, 512], F32))
        BZ1, BZ2, BSC, BWB, BTR, BCN, BPL = 0, 2, 3, 4, 5, 6, 7

        ld_hid, ld_cat, ld_ids, ld_mask, ld_w, ld_vec, ld_tab0, ld_tab1, ld_late = map(sem, [
            "ld_hid", "ld_cat", "ld_ids", "ld_mask", "ld_w", "ld_vec", "ld_tab0", "ld_tab1", "ld_late"])
        consts = sem("consts")
        prep = sem("prep")
        hid_ok = sem("hid_ok")
        cat_ok = sem("cat_ok")
        ids_ok = sem("ids_ok")
        a1_ok = sem("a1_ok")
        hidx_ok = sem("hidx_ok")
        setT = sem("setT")
        setE = sem("setE")
        tv_got = sem("tv_got")
        tab_hi = sem("tab_hi")
        tab_sub = sem("tab_sub")
        tab_zero = sem("tab_zero")
        staged = sem("staged")
        got = [sem(f"got{c}") for c in range(CH)]
        turns = sem("turns")
        emb_t = sem("emb_t")
        embT_ok = sem("embT_ok")
        wq_ok = sem("wq_ok")
        z1_ok = sem("z1_ok")
        h1_ok = sem("h1_ok")
        z2_ok = sem("z2_ok")
        h2_ok = sem("h2_ok")
        sc_ok = sem("sc_ok")
        srow_ok = sem("srow_ok")
        sc_moved = [sem(f"sc_moved{n}") for n in range(4)]
        soft = sem("soft")
        exp_ok = sem("exp_ok")
        w_ok = sem("w_ok")
        wb_ok = sem("wb_ok")
        att_ok = sem("att_ok")
        att_mv = sem("att_mv")
        oh_ok = sem("oh_ok")
        cn_ok = sem("cn_ok")
        cn_mv = sem("cn_mv")
        pl_ok = sem("pl_ok")
        pl_mv = sem("pl_mv")
        pl_ch = sem("pl_ch")
        cats_got = [sem(f"cats_got{k}") for k in range(NCAT // 2)]
        msk_ok = sem("msk_ok")
        numT_ok = sem("numT_ok")
        kpart_ok = sem("kpart_ok")
        kk_ok = sem("kk_ok")
        tv_ok = sem("tv_ok")
        dch = sem("dch")
        ach = sem("ach")
        base_ok = sem("base_ok")
        rows_ok = sem("rows_ok")
        fin_ok = sem("fin_ok")
        finT_ok = sem("finT_ok")
        bT = sem("bT")
        bT_mv = sem("bT_mv")
        pe_e = sem("pe_e")
        out_ok = sem("out_ok")

        block = ctx.enter_context(nc.Block())

        N_VEC = 20
        N_SET = 6 + 2 * Q
        SOFT = 10

        @block.sync
        def _(sp):
            sp.dma_start(hid_i.rearrange("c (g p) -> c g p", p=P),
                         hist_ids.rearrange("b l -> (b l)").rearrange("(g c p) -> c g p", c=GR, p=P)
                         ).then_inc(ld_hid, 16)
            for t, off in ((user_cat, 0), (item_cat, NU), (ctx_cat, NU + NI)):
                sp.dma_start(cat_i[:, :, off:off + t.shape[1]],
                             t.rearrange("(q p) f -> p q f", p=P)).then_inc(ld_cat, 16)
            for h in range(2):
                sp.dma_start(A1d[E * h:E * h + E, :, :], A1.rearrange("(f e) n -> e f n", e=E)).then_inc(ld_w, 16)
            sp.dma_start(A2s[:, :, :], A2.rearrange("(k p) m -> p k m", p=P)).then_inc(ld_w, 16)
            for t, src in enumerate((author_ids, tag_ids)):
                sp.dma_start(ids_i[t].rearrange("p (q l) -> p q l", l=L),
                             src.rearrange("(q p) l -> p q l", p=P)).then_inc(ld_ids, 16)
            sp.dma_start(msk_i.rearrange("p (q l) -> p q l", l=L),
                         hist_mask.rearrange("(q p) l -> p q l", p=P)).then_inc(ld_ids, 16)
            for h in range(2):
                sp.dma_start(mb_i[PB * h:PB * h + PB, :].rearrange("j (i l) -> j i l", l=L),
                             hist_mask[HALF * h:HALF * h + HALF, :].rearrange("(i j) l -> j i l", j=PB)
                             ).then_inc(ld_mask, 16)
            sp.wait_ge(tab_zero, 2)
            for t, (row, ld) in enumerate(((1, ld_tab0), (NI - 1, ld_tab1))):
                full = (NHI - 1) * P
                sp.dma_start(tab[t][:, 0:NHI - 1, :],
                             item_emb[row, 0:full, :].rearrange("(h p) e -> p h e", p=P)).then_inc(ld, 16)
                sp.dma_start(tab[t][0:V - full, NHI - 1, :], item_emb[row, full:V, :]).then_inc(ld, 16)

            def move_scores(b, first):
                for n in range(4):
                    sp.wait_ge(srow_ok, 4 * b + n + 1)
                    if n == 0 and not first:
                        sp.wait_ge(soft, SOFT * (b - 1) + 2)
                    for h in range(2):
                        sp.dma_start(Sc[PB * h + 4 * n:PB * h + 4 * n + 4, :],
                                     srow[0:97:32, n % 2, L * h:L * h + L]).then_inc(sc_moved[n], 16)

            move_scores(0, True)
            with sp.Fori(1, NBLK) as b:
                move_scores(b, False)

            sp.wait_ge(pl_ok, 2 * Q)
            sp.dma_start(D1s, D1.rearrange("(k p) n -> p k n", p=P)).then_inc(ld_late, 16)
            sp.dma_start(D2s, D2.rearrange("(k p) n -> p k n", p=P)).then_inc(ld_late, 16)
            sp.dma_start(D3s, D3.rearrange("(k p) n -> p k n", p=P)).then_inc(ld_late, 16)
            sp.wait_ge(finT_ok, 1)
            sp.dma_start(out.rearrange("(q p) -> q p", p=P), finT).then_inc(out_ok, 16)
            sp.wait_ge(out_ok, 16)

        @block.gpsimd
        def _(pool):
            pool.memset(ident[:, :], 0.0).then_inc(consts, 1)
            pool.memset(sel[:, :, :], 0.0).then_inc(consts, 1)
            pool.iota(iota_i, pattern=[[1, P]], base=0, channel_multiplier=0).then_inc(consts, 1)
            pool.wait_ge(consts, 3)
            pool.affine_select(out=ident[:, :], in_=ident[:, :], compare_op=ALU.not_equal, fill=1.0, base=0,
                               pattern=[[-1, P]], channel_multiplier=1).then_inc(consts, 1)
            pool.affine_select(out=sel[:, :, :].rearrange("k j (h c) -> k j h c", h=2),
                               in_=sel[:, :, :].rearrange("k j (h c) -> k j h c", h=2),
                               compare_op=ALU.not_equal, fill=1.0, base=0,
                               pattern=[[-1, PB], [-PB, 2], [0, E]], channel_multiplier=1).then_inc(consts, 1)

            def gather(dst, table, idx, done):
                pool.indirect_dma_start(out=dst, out_offset=None, in_=table,
                                        in_offset=bass.IndirectOffsetOnAxis(ap=idx, axis=0)).then_inc(done, 16)

            pool.wait_ge(cat_ok, 1)
            for q in range(Q):
                gather(tv[:, q % 2 * 2 + q // 2, :], item_emb[0], cat_x[:, NU, q:q + 1], tv_got)




            def gather_block(b, u, first):
                pool.wait_ge(staged, b + 1)
                pool.sem_inc(turns, 1)
                for c in range(CH):
                    if not first and c % 4 == 0:
                        pool.wait_ge(emb_t, TG * (b - 1) + c // 4 + 1)
                        pool.sem_inc(turns, 1)
                    for h in range(2):
                        gather(emb[:, c, E * h:E * h + E], item_emb[0], istage[:, u, h, c:c + 1], got[c])

            gather_block(0, 0, True)
            with pool.Fori(1, NBLK - 1, 2) as b:
                gather_block(b, 1, False)
                gather_block(b + 1, 0, False)
            gather_block(NBLK - 1, 1, False)

            pool.wait_ge(pl_ok, Q)
            for f in range(NCAT):
                if f == NU:
                    continue
                t = user_emb if f < NU else item_emb if f < NU + NI else ctx_emb
                for q in range(Q):
                    gather(base[:, q, E * f:E * f + E], t.rearrange("f v e -> (f v) e"), cat_x[:, f, q:q + 1], cats_got[f // 2])

        @block.tensor
        def _(pe):
            mm = nc.tensor.matmul

            n_set = [0]

            def set_bank():
                n = n_set[0]
                if n >= 2:
                    pe.wait_ge(setE, n - 1)
                n_set[0] += 1
                return BWB + n % 2

            pe.wait_ge(consts, 5)
            pe.wait_ge(hid_ok, 1)
            for h in range(2):
                k = set_bank()
                for g in range(4):
                    i = nc.tensor.transpose(ps[:, k, P * g:P * g + GR],
                                            hid_f[:, (4 * h + g) * P:(4 * h + g + 1) * P], ident[0:GR, 0:GR])
                i.then_inc(setT, 1)
            k = set_bank()
            pe.wait_ge(ld_vec, 16 * N_VEC)
            nc.tensor.transpose(ps[:, k, 0:NR], vrow[:, :], ident[0:NR, 0:NR]).then_inc(setT, 1)
            k = set_bank()
            pe.wait_ge(tv_got, 16 * Q)
            for q in range(2):
                i = nc.tensor.transpose(ps[:, k, P * q:P * q + P], tv[:, 2 * q:2 * q + 2, :].rearrange("p a e -> p (a e)"), ident[:, :])
            i.then_inc(setT, 1)
            pe.wait_ge(setE, 4)
            pe.wait_ge(a1_ok, 1)
            for h in range(2):
                k = set_bank()
                for m in range(HK):
                    i = mm(ps[:, k, HALF * m:HALF * m + HALF], A1s[E * h:E * h + E, P * m:P * m + P],
                           qT[E * h:E * h + E, :], start=True, stop=True)
                i.then_inc(setT, 1)
            for t in range(2):
                for q in range(Q):
                    k = set_bank()
                    pe.wait_ge(ids_ok, t + 1)
                    for comp, src in enumerate((ids_w, ids_f) if t == 0 else (tag_lo, tag_hi)):
                        for h in range(2):
                            i = nc.tensor.transpose(ps[0:LH, k, (2 * comp + h) * P:(2 * comp + h + 1) * P],
                                                    src[:, L * q + LH * h:L * q + LH * h + LH], ident[:, :])
                    i.then_inc(setT, 1)

            def transpose_group(b, g, first=False):
                if first and g == 0:
                    pe.wait_ge(setE, n_set[0])
                if not (first and g == 0):
                    pe.wait_ge(embT_ok, TG * b + g)
                for n, c in enumerate(range(4 * g, min(4 * g + 4, CH))):
                    pe.wait_ge(got[c], 32 * (b + 1))
                    i = nc.tensor.transpose(ps[:, BTR, P * n:P * n + P], emb[:, c, :], ident[:, :])
                i.then_inc(emb_t, 1)

            def layer1(b, j, u, first):
                s = PB * b + j
                cover = lambda jj: -(-L * (jj + 1) // 512)
                if j == 0 or cover(j) != cover(j - 1):
                    pe.wait_ge(embT_ok, TG * b + min(cover(j), TG))
                pe.wait_ge(wq_ok, s + 1)
                for m in range(HK):
                    for h in range(2):
                        if m == 0 and not (first and j == 0):
                            pe.wait_ge(h1_ok, 2 * s - 1 + h)
                        i = mm(ps[:, BZ1 + h, L * m:L * m + L], wq[E * h:E * h + E, j % 2, P * m:P * m + P],
                               embT[E * h:E * h + E, u, L * j:L * j + L], start=True, stop=True)
                        if m == HK - 1:
                            i.then_inc(z1_ok, 1)

            def counts(b, j, first):
                s = PB * b + j
                pe.wait_ge(oh_ok, s + 1)
                if not (first and j == 0):
                    pe.wait_ge(cn_mv, s)
                for v in range(VS):
                    for h in range(2):
                        i = mm(ps[:, BCN, NHI * v:NHI * v + NHI], oh_lo[0:LH, j % 2, 2 * v + h, :],
                               oh_hi[0:LH, j % 2, 2 * v + h, :], start=(h == 0), stop=(h == 1))
                i.then_inc(cn_ok, 1)

            def pool_product(k):
                pe.wait_ge(cn_mv, 2 * PB * (k + 1))
                pe.wait_ge(pl_mv, k + 1)
                t = k // Q if isinstance(k, int) else None
                for hi in range(NHI):
                    rhs = parts_r[:, :, :].rearrange("p t n -> p (t n)")[
                        :, bass.ds((k // Q) * (NHI * 3 * E) + 3 * E * hi, 3 * E)] if t is None else parts[t][:, hi, :]
                    i = mm(ps[:, BPL, 0:3 * E], cnt[:, hi, :], rhs, start=(hi == 0), stop=(hi == NHI - 1))
                i.then_inc(pl_ok, 1)

            def layer2(b, j, first):
                s = PB * b + j
                if first and j == 0:
                    return
                pe.wait_ge(h1_ok, 2 * s)
                if not (first and j == 1):
                    pe.wait_ge(h2_ok, s - 1)
                for m in range(HK):
                    i = mm(ps[:, BZ2, 0:2 * L], A2s[:, m, :], h1[:, (j - 1) % 2, m, :], start=(m == 0), stop=(m == HK - 1))
                i.then_inc(z2_ok, 1)

            def layer3(b, j, first):
                s = PB * b + j
                if first and j < 2:
                    return
                pe.wait_ge(h2_ok, s - 1)
                n = (j - 2) % 4
                if n == 0 and not (first and j == 2):
                    pe.wait_ge(srow_ok, 4 * b + (j - 2) // 4)
                mm(ps[32 * n:32 * n + 32, BSC, 0:2 * L], A3s[:, :], h2[:, j % 2, :], start=True, stop=True,
                   tile_position=(0, 32 * n)).then_inc(sc_ok, 1)

            def spread(b, m):
                if m == 0:
                    pe.wait_ge(w_ok, b + 1)
                else:
                    pe.wait_ge(att_ok, PB * b + 2 * m)
                for r in range(2):
                    i = mm(ps[:, BWB, L * r:L * r + L], sel[:, 2 * m + r, :], wts[:, :], start=True, stop=True)
                i.then_inc(wb_ok, 1)

            def steps(b, u, first=False, last=False, k=None):
                for j in range(PB):
                    layer1(b, j, u, first)
                    if j == 0 and k is not None:
                        pool_product(k)
                    counts(b, j, first)
                    layer2(b, j, first)
                    layer3(b, j, first)
                    if not first and 4 <= j < 12:
                        spread(b - 1, j - 4)
                    if not last and j >= PB - TG:
                        transpose_group(b + 1, j - (PB - TG))

            for g in range(TG):
                transpose_group(0, g, True)
            steps(0, 0, first=True)
            with pe.Fori(0, NBLK // 2 - 1) as k:
                steps(2 * k + 1, 1)
                steps(2 * k + 2, 0, k=k)
            steps(NBLK - 1, 1, last=True)
            pool_product(2 * Q - 1)
            layer2(NBLK, 0, False)
            layer3(NBLK, 0, False)
            layer3(NBLK, 1, False)

            pe.wait_ge(prep, 2)
            pe.wait_ge(ld_vec, 16 * N_VEC)
            for q in range(Q):
                i = nc.tensor.transpose(ps[0:19, BTR, P * q:P * q + P], nums[:, q, :], ident[:, :])
            i.then_inc(pe_e, 1)
            pe.wait_ge(numT_ok, 1)
            pe.wait_ge(pl_mv, 2 * Q + 1)
            for q in range(Q):
                i = mm(ps[:, BCN + q // 2, 3 * E * (q % 2):3 * E * (q % 2) + 3 * E], numT[:, P * q:P * q + P],
                       Wn[:, :], start=True, stop=True)
            i.then_inc(pe_e, 1)
            pe.wait_ge(kpart_ok, 1)
            mm(ps[:, BTR, 0:3], onesq, kk[:, 0:3], start=True, stop=True).then_inc(pe_e, 1)
            for m in range(PB // 2):
                spread(NBLK - 1, m)
            pe.wait_ge(att_mv, NBLK)
            pe.wait_ge(kk_ok, 1)
            for q in range(2):
                i = nc.tensor.transpose(ps[:, BTR, P * q:P * q + P], attT[:, P * q:P * q + P], ident[:, :])
            i.then_inc(pe_e, 1)

            pe.wait_ge(tv_ok, 1)
            pe.wait_ge(ach, 2)
            bank = (BCN, BPL)

            def deep1(kf):
                pe.wait_ge(bT_mv, kf + 1)
                for m in range(M1):
                    mm(ps[:, m, :], D1s[:, kf, P * m:P * m + P], baseT[:, kf, :], start=(kf == 0), stop=(kf == KT - 1))
                i = mm(ps[0:4, BWB, :], xw[:, kf, :], baseT[:, kf, :], start=(kf == 0), stop=(kf == KT - 1))
                if kf == KT - 1:
                    i.then_inc(pe_e, 1)

            pe.wait_ge(ld_late, 48)
            for kf in range(KT):
                if kf == F_ATT // P:
                    pe.wait_ge(base_ok, 1)
                if kf < NCAT // 2:
                    pe.wait_ge(cats_got[kf], 16 * Q * (2 - (kf == NU // 2)))
                if kf >= 2:
                    pe.wait_ge(bT_mv, kf - 1)
                for q in range(Q):
                    i = nc.tensor.transpose(ps[:, bank[kf % 2], P * q:P * q + P],
                                            base[:, q, P * kf:P * kf + P], ident[:, :])
                i.then_inc(bT, 1)
                if kf >= 1:
                    deep1(kf - 1)
            deep1(KT - 1)
            for m in range(M2):
                for kf in range(M1):
                    if m == 0:
                        pe.wait_ge(ach, 2 + kf + 1)
                    i = mm(ps[:, BCN + m, :], D2s[:, kf, P * m:P * m + P], g1[:, kf, :], start=(kf == 0), stop=(kf == M1 - 1))
                i.then_inc(pe_e, 1)
            for m in range(M2):
                for kf in range(M2):
                    if m == 0:
                        pe.wait_ge(ach, 2 + M1 + kf + 1)
                    i = mm(ps[:, m, :], D3s[:, kf, P * m:P * m + P], g2[:, kf, :], start=(kf == 0), stop=(kf == M2 - 1))
                i.then_inc(pe_e, 1)
            for kf in range(M2):
                pe.wait_ge(ach, 2 + M1 + M2 + kf + 1)
                i = mm(ps[0:1, 2, :], vecT[:, R_WH2 + kf:R_WH2 + kf + 1], g3[:, kf, :], start=(kf == 0), stop=(kf == M2 - 1))
            i.then_inc(pe_e, 1)
            pe.wait_ge(rows_ok, 1)
            for q in range(Q):
                nc.tensor.transpose(ps[:, BWB, 4 * q:4 * q + 4], xrow[:, P * q:P * q + P], ident[0:4, 0:4])
            for q in range(Q):
                i = nc.tensor.transpose(ps[:, BWB, 16 + q:17 + q], drow[:, P * q:P * q + P], ident[0:1, 0:1])
            i.then_inc(pe_e, 1)
            pe.wait_ge(fin_ok, 1)
            nc.tensor.transpose(ps[0:Q, BWB, 0:P], fin[:, 11, :], ident[:, :]).then_inc(pe_e, 1)

        @block.scalar
        def _(act):
            def rows(dst, n, src):
                act.dma_start(vrow[dst:dst + n, :], src).then_inc(ld_vec, 16)
            rows(R_CW, 3 * KT, cross_w.rearrange("v (k p) -> (v k) p", p=P))
            rows(R_CB, 3 * KT, cross_b.rearrange("v (k p) -> (v k) p", p=P))
            rows(R_WH, KT + M2, Wh.rearrange("(k p) o -> k (p o)", p=P))
            rows(R_A1, HK, a1.rearrange("(k p) -> k p", p=P))
            rows(R_A2, 1, a2.rearrange("(k p) -> k p", p=P))
            rows(R_A3, 1, A3.rearrange("(k p) o -> k (p o)", p=P))
            rows(R_D1, M1, d1.rearrange("(k p) -> k p", p=P))
            rows(R_D2, M2, d2.rearrange("(k p) -> k p", p=P))
            rows(R_D3, M2, d3.rearrange("(k p) -> k p", p=P))
            act.dma_start(a3c[:, :], a3.rearrange("(a n) -> a n", a=1).to_broadcast([P, 1])).then_inc(ld_vec, 16)
            act.dma_start(bhc[:, :], bh.rearrange("(a n) -> a n", a=1).to_broadcast([P, 1])).then_inc(ld_vec, 16)
            act.wait_ge(prep, 2)
            col = 0
            for n, (x, w, bias) in enumerate(((user_num, Wu, bu), (item_num, Wi, bi), (ctx_num, Wc, bc))):
                d = x.shape[1]
                act.dma_start(nums[:, :, col:col + d], x.rearrange("(q p) f -> p q f", p=P)).then_inc(ld_vec, 16)
                act.dma_start(Wn[col:col + d, E * n:E * n + E], w).then_inc(ld_vec, 16)
                act.dma_start(Wn[18:19, E * n:E * n + E], bias.rearrange("(a n) -> a n", a=1)).then_inc(ld_vec, 16)
                col += d

            for t, ld in enumerate((ld_tab0, ld_tab1)):
                act.wait_ge(ld, 32)
                if t == 0:
                    act.wait_ge(setE, 6)
                else:
                    act.wait_ge(setE, 6 + 2 * Q)
                    act.wait_ge(msk_ok, 1)
                for n in range(3):
                    if n:
                        act.wait_ge(tab_sub, 2 * t + n)
                    nc.scalar.activation(parts[t][:, :, E * n:E * n + E], tab[t], ACT.Copy).then_inc(tab_hi, 1)

            def transposed(b, g, u, reused):
                act.wait_ge(emb_t, TG * b + g + 1)
                if reused:
                    n = min(PB, -(-min(512 * (g + 1), CH * P) // L))
                    act.wait_ge(att_ok, PB * (b - 2) + n)
                w = min(512, CH * P - 512 * g)
                nc.scalar.activation(embT[:, u, 512 * g:512 * g + w], ps[:, BTR, 0:w], ACT.Copy).then_inc(embT_ok, 1)

            def relu1(b, j, first):
                s = PB * b + j
                for h in range(2):
                    act.wait_ge(z1_ok, 2 * s + h + 1)
                    if h == 0 and not (first and j < 2):
                        act.wait_ge(z2_ok, s - 1)
                    for m in range(HK):
                        bias = qbias[:, m, h, s:s + 1] if isinstance(s, int) else qbias[:, m, h, bass.ds(s, 1)]
                        i = nc.scalar.activation(h1[:, j % 2, m, L * h:L * h + L], ps[:, BZ1 + h, L * m:L * m + L],
                                                 ACT.Relu, bias=bias)
                    i.then_inc(h1_ok, 1)

            def counts_out(b, j, u, first, k):
                s = PB * b + j
                act.wait_ge(cn_ok, s + 1)
                if j == 0 and k is not None:
                    act.wait_ge(pl_ok, k + 1)
                v0 = PB * VS * u + VS * j
                nc.scalar.activation(cnt[:, :, v0:v0 + VS].rearrange("p h v -> p v h"),
                                     ps[:, BCN, 0:VS * NHI].rearrange("p (v h) -> p v h", v=VS),
                                     ACT.Copy).then_inc(cn_mv, 1)

            def relu2(b, j, first):
                s = PB * b + j
                if first and j == 0:
                    return
                act.wait_ge(z2_ok, s)
                if not (first and j < 3):
                    act.wait_ge(sc_ok, s - 2)
                nc.scalar.activation(h2[:, (j - 1) % 2, :], ps[:, BZ2, 0:2 * L], ACT.Relu,
                                     bias=vecT[:, R_A2:R_A2 + 1]).then_inc(h2_ok, 1)

            def scores_out(b, j, first):
                if first and j == 1:
                    return
                n = (j - 2) // 4 % 4
                act.wait_ge(sc_ok, PB * b + j - 1)
                before = b - 1 if n == 3 else b
                if n >= 2:
                    act.wait_ge(sc_moved[n - 2], 32 * (before + 1))
                elif not first:
                    act.wait_ge(sc_moved[n + 2], 32 * before)
                nc.scalar.activation(srow[:, n % 2, :], ps[:, BSC, 0:2 * L], ACT.Identity,
                                     bias=a3c[:, 0:1]).then_inc(srow_ok, 1)

            def exps(b):
                act.wait_ge(soft, SOFT * b + 6)
                nc.scalar.activation(ex[:, :], smk[:, :], ACT.Exp, bias=st[:, 1:2], accum_out=st[:, 2:3]).then_inc(exp_ok, 1)

            def steps(b, u, first=False, last=False, k=None):
                for j in range(PB):
                    relu1(b, j, first)
                    counts_out(b, j, u, first, k)
                    relu2(b, j, first)
                    if j % 4 == 1:
                        scores_out(b, j, first)
                    if j == 3 and not first:
                        exps(b - 1)
                    if not last and j >= PB - TG:
                        transposed(b + 1, j - (PB - TG), 1 - u, not first)

            act.wait_ge(setE, N_SET)
            for g in range(TG):
                transposed(0, g, 0, False)
            act.wait_ge(tab_hi, 6)
            steps(0, 0, first=True)
            with act.Fori(0, NBLK // 2 - 1) as k:
                steps(2 * k + 1, 1)
                steps(2 * k + 2, 0, k=k)
            steps(NBLK - 1, 1, last=True)
            relu2(NBLK, 0, False)
            scores_out(NBLK, 1, False)
            exps(NBLK - 1)

            act.wait_ge(pe_e, 2)
            for n in range(2):
                nc.scalar.activation(base[:, 2 * n:2 * n + 2, F_NUM:F_NUM + 3 * E],
                                     ps[:, BCN + n, 0:6 * E].rearrange("p (q f) -> p q f", q=2),
                                     ACT.Relu).then_inc(ach, 1)
            act.wait_ge(pe_e, 5)
            for m in range(M1):
                nc.scalar.activation(g1[:, m, :], ps[:, m, :], ACT.Relu, bias=vecT[:, R_D1 + m:R_D1 + m + 1]).then_inc(ach, 1)
            for m in range(M2):
                act.wait_ge(pe_e, 5 + m + 1)
                nc.scalar.activation(g2[:, m, :], ps[:, BCN + m, :], ACT.Relu, bias=vecT[:, R_D2 + m:R_D2 + m + 1]).then_inc(ach, 1)
            for m in range(M2):
                act.wait_ge(pe_e, 5 + M2 + m + 1)
                nc.scalar.activation(g3[:, m, :], ps[:, m, :], ACT.Identity, bias=vecT[:, R_D3 + m:R_D3 + m + 1]).then_inc(ach, 1)

        @block.vector
        def _(dve):
            v = nc.vector
            done = [0]

            def chain(i):
                done[0] += 1
                i.then_inc(prep, 1)
                dve.wait_ge(prep, done[0])

            v.memset(st[:, :], 0.0).then_inc(pl_mv, 1)
            chain(v.memset(Wn[:, :], 0.0))
            chain(v.memset(nums[:, :, 18:19], 1.0))
            v.memset(tab[0][:, NHI - 1, :], 0.0).then_inc(tab_zero, 1)
            v.memset(tab[1][:, NHI - 1, :], 0.0).then_inc(tab_zero, 1)

            def clamp(f, i, w, signal=None):
                chain(v.tensor_scalar(w, i, 0.0, float(V), ALU.is_lt, ALU.mult))
                chain(v.tensor_tensor(w, i, w, ALU.add))
                last = v.tensor_scalar(f, w, 0.0, float(V - 1), ALU.max, ALU.min)
                chain(last) if signal is None else last.then_inc(signal, 1)

            dve.wait_ge(ld_cat, 48)
            clamp(cat_f[:, :, :], cat_i[:, :, :], cat_w[:, :, :])
            for f in range(NCAT):
                first = 0 if f < NU else NU if f < NU + NI else NU + NI
                i = v.tensor_scalar(cat_x[:, f, :], cat_f[:, :, f], float((f - first) * V), None, ALU.add)
            i.then_inc(cat_ok, 1)
            dve.wait_ge(ld_hid, 16)
            clamp(hid_f, hid_i, hid_w, hid_ok)
            dve.wait_ge(ld_w, 48)
            v.tensor_tensor(A1hd[:, :], A1d[:, 1, :], A1d[:, 2, :], ALU.subtract)
            v.tensor_copy(A1p[:, :], A1d[:, 3, :])
            v.tensor_tensor(A1s, A1d[:, 0, :], A1d[:, 2, :], ALU.add).then_inc(a1_ok, 1)

            n_set = [0]

            def set_out():
                k = BWB + n_set[0] % 2
                n_set[0] += 1
                dve.wait_ge(setT, n_set[0])
                return k

            for h in range(2):
                k = set_out()
                v.tensor_copy(hidx[:, h, :].rearrange("p (g c) -> p g c", c=GR),
                              ps[:, k, :].rearrange("p (g c) -> p g c", c=P)[:, :, 0:GR]).then_inc(setE, 1)
            dve.wait_ge(setE, 2)
            for b in range(2):
                v.tensor_scalar(istage[:, b, :, :], hidx[:, :, CH * b:CH * b + CH], 1.0, None, ALU.mult).then_inc(staged, 1)
            k = set_out()
            v.tensor_copy(vecT[:, :], ps[:, k, 0:NR]).then_inc(setE, 1)
            dve.wait_ge(setE, 3)
            v.tensor_copy(A3s[:, :], vecT[:, R_A3:R_A3 + 1].to_broadcast([P, 32]))
            k = set_out()
            v.tensor_copy(qT[:, :], ps[:, k, 0:HALF]).then_inc(setE, 1)
            for h in range(2):
                k = set_out()
                for m in range(HK):
                    i = v.tensor_scalar(qbias[:, m, h, :], ps[:, k, HALF * m:HALF * m + HALF],
                                        vecT[:, R_A1 + m:R_A1 + m + 1], None, ALU.add)
                i.then_inc(setE, 1)
            dve.wait_ge(consts, 3)
            chain(v.tensor_copy(iota[:, :], iota_i))

            dve.wait_ge(ld_ids, 48)
            chain(v.tensor_scalar(msk_i, msk_i, 0.0, None, ALU.is_gt))
            with nc.allow_low_precision(reason="sums of 0 and 1"):
                chain(v.tensor_reduce(rlen[:, :], msk_i.rearrange("p (q l) -> p q l", l=L), AX_X, ALU.add))
            chain(v.tensor_scalar(rlen[:, :], rlen[:, :], 1e-6, None, ALU.max))
            chain(v.reciprocal(rlen[:, :], rlen[:, :]))
            for t, (w, lo, hi) in enumerate(((ids_w, ids_w, ids_f), (tag_lo, tag_lo, tag_hi))):
                if t == 1:
                    dve.wait_ge(ids_ok, 1)
                clamp(ids_c, ids_i[t], w)
                chain(v.tensor_scalar(ids_i[t], ids_c, 7, None, ALU.arith_shift_right))
                chain(v.tensor_scalar(ids_c, ids_c, 127, None, ALU.bitwise_and))
                chain(v.tensor_copy(lo, ids_c))
                chain(v.tensor_scalar(ids_i[t], ids_i[t], 1.0, None, ALU.add))
                chain(v.tensor_tensor(ids_i[t], ids_i[t], msk_i, ALU.mult))
                v.tensor_scalar(hi, ids_i[t], -1.0, None, ALU.add).then_inc(ids_ok, 1)
                for q in range(Q):
                    k = set_out()
                    v0 = 2 * (B * t + P * q)
                    v.tensor_copy(idT[0:LH, :, v0:v0 + 2 * P].rearrange("l c (v h) -> l c h v", h=2),
                                  ps[0:LH, k, :].rearrange("l (c h v) -> l c h v", c=2, h=2)).then_inc(setE, 1)
            assert n_set[0] == N_SET
            dve.wait_ge(ld_mask, 32)
            v.tensor_copy(msk[:, :, :], mb_i.rearrange("j (i l) -> j i l", l=L)).then_inc(msk_ok, 1)
            dve.wait_ge(setE, N_SET)
            dve.wait_ge(a1_ok, 1)

            def weights(s, j, free):
                if free is not None:
                    dve.wait_ge(z1_ok, free)
                q = qT[:, s:s + 1] if isinstance(s, int) else qT[:, bass.ds(s, 1)]
                v.scalar_tensor_tensor(out=wq[:, j % 2, :], in0=A1p[:, :], scalar=q, in1=A1hd[:, :],
                                       op0=ALU.mult, op1=ALU.add).then_inc(wq_ok, 1)

            def onehots(s, j, free):
                if free is not None:
                    dve.wait_ge(cn_ok, free)
                for comp, (oh, n) in enumerate(((oh_lo, P), (oh_hi, NHI))):
                    code = idT[0:LH, comp, 2 * VS * s:2 * VS * s + 2 * VS] if isinstance(s, int) else \
                        idT[0:LH, comp, bass.ds(s * (2 * VS), 2 * VS)]
                    i = v.tensor_tensor(oh[0:LH, j % 2, :, :], iota[0:LH, None, 0:n].to_broadcast([LH, 2 * VS, n]),
                                        code.unsqueeze(2).to_broadcast([LH, 2 * VS, n]), ALU.is_equal)
                i.then_inc(oh_ok, 1)

            def softmax(b):
                for n in range(4):
                    dve.wait_ge(sc_moved[n], 32 * (b + 1))
                mk = msk[:, b, :] if isinstance(b, int) else msk[:, bass.ds(b, 1), :].rearrange("j i l -> j (i l)")
                v.tensor_scalar(mkb[:, :], mk, 1.0, None, ALU.mult).then_inc(soft, 1)
                v.tensor_tensor(smk[:, :], Sc[:, :], mk, ALU.mult).then_inc(soft, 1)
                v.tensor_scalar(pen[:, :], mk, 1e9, -1e9, ALU.mult, ALU.add).then_inc(soft, 1)
                dve.wait_ge(soft, SOFT * b + 3)
                v.tensor_tensor(smk[:, :], smk[:, :], pen[:, :], ALU.add).then_inc(soft, 1)
                dve.wait_ge(soft, SOFT * b + 4)
                v.tensor_reduce(st[:, 0:1], smk[:, :], AX_X, ALU.max).then_inc(soft, 1)
                dve.wait_ge(soft, SOFT * b + 5)
                v.tensor_scalar(st[:, 1:2], st[:, 0:1], -1.0, None, ALU.mult).then_inc(soft, 1)
                dve.wait_ge(exp_ok, b + 1)
                v.tensor_tensor_reduce(out=exm[:, :], in0=ex[:, :], in1=mkb[:, :], scale=1.0, scalar=0.0, op0=ALU.mult,
                                       op1=ALU.add, accum_out=st[:, 3:4]).then_inc(soft, 1)
                v.reciprocal(st[:, 4:5], st[:, 2:3]).then_inc(soft, 1)
                dve.wait_ge(soft, SOFT * b + 8)
                v.tensor_scalar(st[:, 5:6], st[:, 3:4], st[:, 4:5], 1e-6, ALU.mult, ALU.max).then_inc(soft, 1)
                dve.wait_ge(soft, SOFT * b + 9)
                v.reciprocal(st[:, 6:7], st[:, 5:6]).then_inc(soft, 1)
                dve.wait_ge(soft, SOFT * b + 10)
                v.tensor_scalar(wts[:, :], exm[:, :], st[:, 4:5], st[:, 6:7], ALU.mult, ALU.mult).then_inc(w_ok, 1)

            def attend(b, m, u):
                dve.wait_ge(wb_ok, PB // 2 * b + m + 1)
                for r in range(2):
                    j = 2 * m + r
                    if m:
                        dve.wait_ge(att_ok, PB * b + j - 1)
                    v.tensor_tensor_reduce(out=junk[:, j % 2, :], in0=ps[:, BWB, L * r:L * r + L],
                                           in1=embT[:, u, L * j:L * j + L], scale=1.0, scalar=0.0, op0=ALU.mult,
                                           op1=ALU.add, accum_out=attS[:, 0, j:j + 1]).then_inc(att_ok, 1)

            def place(b):
                dve.wait_ge(att_ok, PB * b + PB)
                dst = attT[:, PB * b:PB * b + PB] if isinstance(b, int) else attT[:, bass.ds(b * PB, PB)]
                v.tensor_scalar(dst, attS[:, 0, :], 1.0, None, ALU.mult).then_inc(att_mv, 1)

            def stage(b, u):
                dve.wait_ge(emb_t, TG * (b + 1))
                src = hidx[:, :, CH * (b + 2):CH * (b + 3)] if isinstance(b, int) else \
                    hidx[:, :, bass.ds(CH * (b + 2), CH)]
                v.tensor_scalar(istage[:, u, :, :], src, 1.0, None, ALU.mult).then_inc(staged, 1)

            def pool_out(k):
                dve.wait_ge(pl_ok, k + 1)
                dst = pooled[:, k, :] if isinstance(k, int) else pooled[:, bass.ds(k, 1), :].rearrange("p a e -> p (a e)")
                v.tensor_scalar(dst, ps[:, BPL, 2 * E:3 * E], 1.0, None, ALU.mult).then_inc(pl_ch, 1)
                dve.wait_ge(pl_ch, 2 * k + 1)
                v.tensor_tensor(dst, ps[:, BPL, E:2 * E], dst, ALU.add).then_inc(pl_ch, 1)
                dve.wait_ge(pl_ch, 2 * k + 2)
                v.tensor_tensor(dst, ps[:, BPL, 0:E], dst, ALU.add).then_inc(pl_mv, 1)

            def steps(b, u, first=False, last=False, k=None, nostage=False):
                for j in range(PB):
                    s = PB * b + j
                    start = first and j == 0
                    if not (last and j == PB - 1):
                        weights(s + 1, j + 1, None if start else 2 * s)
                        onehots(s + 1, j + 1, None if start else s)
                    if j == 1 and k is not None:
                        pool_out(k)
                    if not first and j == 3:
                        softmax(b - 1)
                    if not first and 4 <= j < 12:
                        attend(b - 1, j - 4, 1 - u)
                    if not first and j == 12:
                        place(b - 1)
                    if j == 8 and not nostage:
                        stage(b, u)

            weights(0, 0, None)
            onehots(0, 0, None)
            for t in range(2):
                for n in range(2):
                    dve.wait_ge(tab_hi, 3 * t + n + 1)
                    v.tensor_tensor(tab[t], tab[t], parts[t][:, :, E * n:E * n + E], ALU.subtract).then_inc(tab_sub, 1)
            steps(0, 0, first=True)
            with dve.Fori(0, NBLK // 2 - 2) as k:
                steps(2 * k + 1, 1)
                steps(2 * k + 2, 0, k=k)
            steps(NBLK - 3, 1)
            steps(NBLK - 2, 0, k=NBLK // 2 - 2, nostage=True)
            steps(NBLK - 1, 1, last=True, nostage=True)
            pool_out(2 * Q - 1)

            n = [0]

            def link(i):
                n[0] += 1
                i.then_inc(dch, 1)
                dve.wait_ge(dch, n[0])

            cw = lambda i: vecT[:, R_CW + KT * i:R_CW + KT * i + KT]
            cb = lambda i: vecT[:, R_CB + KT * i:R_CB + KT * i + KT]
            wh = vecT[:, R_WH:R_WH + KT]
            link(v.tensor_tensor(kpart[:, 0, :], cb(0), cw(1), ALU.mult))
            link(v.tensor_tensor(kpart[:, 3, :], cb(0), cb(1), ALU.add))
            link(v.tensor_tensor(kpart[:, 1, :], kpart[:, 3, :], cw(2), ALU.mult))
            link(v.tensor_tensor(kpart[:, 3, :], kpart[:, 3, :], cb(2), ALU.add))
            link(v.tensor_tensor(kpart[:, 2, :], kpart[:, 3, :], wh, ALU.mult))
            for i in range(3):
                link(v.tensor_copy(xw[:, :, i], cw(i)))
            link(v.tensor_copy(xw[:, :, 3], wh))
            dve.wait_ge(z1_ok, 2 * HALF)
            link(v.memset(onesq, 1.0))
            v.tensor_reduce(kk[:, 0:3], kpart[:, 0:3, :], AX_X, ALU.add).then_inc(kpart_ok, 1)
            softmax(NBLK - 1)
            dve.wait_ge(pe_e, 1)
            v.tensor_copy(numT, ps[0:19, BTR, :]).then_inc(numT_ok, 1)
            for q in range(Q):
                for t in range(2):
                    link(v.tensor_scalar(base[:, q, F_POOL + E * t:F_POOL + E * t + E], pooled[:, Q * t + q, :],
                                         rlen[:, q:q + 1], None, ALU.mult))
            v.tensor_copy(by_quarter(base[:, :, F_ITEM:F_ITEM + E]), tvq).then_inc(tv_ok, 1)
            dve.wait_ge(pe_e, 3)
            v.tensor_copy(kk[:, 0:3], ps[:, BTR, 0:3]).then_inc(kk_ok, 1)
            for m in range(PB // 2):
                attend(NBLK - 1, m, 1)
            place(NBLK - 1)
            dve.wait_ge(pe_e, 4)
            att = base[:, :, F_ATT:F_ATT + E]
            for h in range(2):
                link(v.tensor_copy(att[:, 2 * h:2 * h + 2, :],
                                   ps[:, BTR, 0:2 * P].rearrange("p (q h e) -> p q h e", q=2, h=2)[:, :, h, :]))
            link(v.tensor_tensor(by_quarter(base[:, :, F_MUL:F_MUL + E]), tvq, by_quarter(att), ALU.mult))
            v.tensor_tensor(by_quarter(base[:, :, F_DIF:F_DIF + E]), tvq, by_quarter(att), ALU.subtract).then_inc(base_ok, 1)
            for kf in range(KT):
                dve.wait_ge(bT, kf + 1)
                v.tensor_copy(baseT[:, kf, :], ps[:, (BCN, BPL)[kf % 2], :]).then_inc(bT_mv, 1)
            dve.wait_ge(pe_e, 5)
            link(v.tensor_copy(xrow, ps[0:4, BWB, :]))
            dve.wait_ge(pe_e, 6 + 2 * M2)
            v.tensor_copy(drow, ps[0:1, 2, :]).then_inc(rows_ok, 1)
            dve.wait_ge(pe_e, 7 + 2 * M2)
            f = lambda i: fin[:, i, :]
            link(v.tensor_copy(fin[:, 0:4, :].rearrange("p i q -> p q i"),
                               ps[:, BWB, 0:4 * Q].rearrange("p (q i) -> p q i", i=4)))
            link(v.tensor_copy(f(4), ps[:, BWB, 4 * Q:5 * Q]))
            link(v.tensor_scalar(f(5), f(0), 1.0, None, ALU.add))
            for i, (c, t, nxt) in enumerate(((5, 6, 7), (7, 8, 9))):
                link(v.tensor_tensor(f(t), f(c), f(i + 1), ALU.mult))
                link(v.tensor_scalar(f(t), f(t), kk[:, i:i + 1], None, ALU.add))
                link(v.tensor_tensor(f(nxt), f(t), f(c), ALU.add))
            link(v.tensor_tensor(f(10), f(9), f(3), ALU.mult))
            link(v.tensor_tensor(f(10), f(10), f(4), ALU.add))
            v.tensor_scalar(f(11), f(10), kk[:, 2:3], bhc[:, 0:1], ALU.add, ALU.add).then_inc(fin_ok, 1)
            dve.wait_ge(pe_e, 8 + 2 * M2)
            v.tensor_copy(finT, ps[0:Q, BWB, 0:P]).then_inc(finT_ok, 1)


_INS = ["r_user_cat", "r_user_num", "r_ctx_cat", "r_ctx_num", "r_hist_ids", "r_hist_author_ids", "r_hist_tag_ids",
        "r_hist_mask", "r_item_cat", "r_item_num", "L0_rec_user_emb", "L0_rec_item_emb", "L0_rec_ctx_emb",
        "L0_rec_Wu", "L0_rec_bu", "L0_rec_Wi", "L0_rec_bi", "L0_rec_Wc", "L0_rec_bc", "L0_rec_A1", "L0_rec_a1",
        "L0_rec_A2", "L0_rec_a2", "L0_rec_A3", "L0_rec_a3", "L0_rec_cross_w", "L0_rec_cross_b", "L0_rec_D1",
        "L0_rec_d1", "L0_rec_D2", "L0_rec_d2", "L0_rec_D3", "L0_rec_d3", "L0_rec_Wh", "L0_rec_bh"]


def kernel(**inputs):
    import numpy as np
    import concourse.bacc as bacc
    from concourse.bass_utils import run_bass_kernel_spmd

    nc = bacc.Bacc("TRN2", target_bir_lowering=False, num_devices=1)
    arrays, args = {}, []
    for name in _INS:
        a = np.ascontiguousarray(inputs[name])
        arrays["in_" + name] = a
        args.append(nc.dram_tensor("in_" + name, a.shape, mybir.dt.from_np(a.dtype), kind="ExternalInput").ap())
    out = nc.dram_tensor("out_0", (inputs["r_hist_ids"].shape[0],), F32, kind="ExternalOutput").ap()
    recommender(nc, *args, out)
    r = run_bass_kernel_spmd(nc, [arrays], core_ids=[0])
    return r.results[0]["out_0"]
```

```python
from contextlib import ExitStack

import concourse.bass as bass
from concourse import mybir

ALU = mybir.AluOpType
ACT = mybir.ActivationFunctionType
AX_X = mybir.AxisListType.X
F32 = mybir.dt.float32
BF16 = mybir.dt.bfloat16
I32 = mybir.dt.int32
U32 = mybir.dt.uint32

P = 128


def recommender(nc, user_cat, user_num, ctx_cat, ctx_num, hist_ids, author_ids, tag_ids, hist_mask,
                item_cat, item_num, user_emb, item_emb, ctx_emb, Wu, bu, Wi, bi, Wc, bc,
                A1, a1, A2, a2, A3, a3, cross_w, cross_b, D1, d1, D2, d2, D3, d3, Wh, bh, out):
    B, L = hist_ids.shape
    V, E = item_emb.shape[1:]
    NU, NI, NC = user_cat.shape[1], item_cat.shape[1], ctx_cat.shape[1]
    NCAT = NU + NI + NC
    HID, MID = A2.shape
    FEAT, H1 = D1.shape
    H2, H3 = D2.shape[1], D3.shape[1]
    Q = B // P
    HALF = B // 2
    PB = 16
    NBLK = HALF // PB
    CH = PB * L // P
    TG = -(-CH // 4)
    HC = HALF * L // P
    LH = L // 2
    NG = -(-V // (2 * P))
    NHI = 2 * NG
    NGH = (-(-NG // 2), NG // 2)
    VS = 4
    KT = FEAT // P
    HK, M1, M2 = HID // P, H1 // P, H2 // P
    GR = 100
    assert 2 * E == P and PB * L == CH * P and NBLK % 2 == 0 and VS * PB * NBLK == 2 * B
    assert HK == 2 and MID == P and FEAT == KT * P and H3 == H2

    R_CW, R_CB, R_WH = 0, 3 * KT, 6 * KT
    R_WH2 = R_WH + KT
    R_A1 = R_WH2 + M2
    R_A2 = R_A1 + HK
    R_A3 = R_A2 + 1
    R_D1 = R_A3 + 1
    R_D2 = R_D1 + M1
    R_D3 = R_D2 + M2
    NR = R_D3 + M2
    F_ITEM, F_CTX, F_NUM = NU * E, (NU + NI) * E, NCAT * E
    F_ATT = F_NUM + 3 * E
    F_POOL = F_ATT + E
    F_MUL, F_DIF = F_POOL + 2 * E, F_POOL + 3 * E

    with ExitStack() as ctx:
        def sb(name, shape, dt=F32):
            return ctx.enter_context(nc.sbuf_tensor(name, shape, dt))

        def sem(name):
            return ctx.enter_context(nc.semaphore(name))

        emb = sb("emb", [P, CH, 2 * E])
        embT = sb("embT", [P, 2, CH * P])
        h1 = sb("h1", [P, 2, HK, 2 * L])
        h2 = sb("h2", [P, 4, 2 * L])
        parts_r = sb("parts", [P, 2, NHI * 3 * E], BF16)
        cnt_r = sb("cnt", [P, KT * B])
        oh_lo = sb("oh_lo", [P, 2, P, 2 * VS], BF16)
        oh_hi = sb("oh_hi", [P, 2, NHI, 2 * VS], BF16)
        wq = sb("wq", [P, 2, HID])
        sel = sb("sel", [96, PB, P], BF16)
        A1p = sb("A1p", [P, HID])
        A1hd = sb("A1hd", [P, HID])
        A2s = sb("A2s", [P, HK, MID])
        A3s = sb("A3s", [P, 32])
        iota = sb("iota", [P, P, 2 * VS], BF16)
        ident = sb("ident", [P, P])
        idT = sb("idT", [P, 2, 2 * B * 2], BF16)
        hidx = sb("hidx", [P, 2, HC], U32)
        istage = sb("istage", [P, 2, 2, CH], U32)
        qT = sb("qT", [P, HALF])
        qbias = sb("qbias", [P, HK, 2, HALF])
        attS = sb("attS", [P, 2, PB])
        attT = sb("attT", [P, HALF])
        junk = sb("junk", [P, 2, L], BF16)
        mrow = sb("mrow", [32, L], I32)
        srow = sb("srow", [P, 2, 2 * L])
        Sc = sb("Sc", [32, L])
        smk = sb("smk", [32, L])
        mkb = sb("mkb", [32, L], BF16)
        ex = sb("ex", [32, L])
        exm = smk
        wts = sb("wts", [32, L])
        pen = wts
        wpart = sb("wpart", [96, L], BF16)
        wmid = mkb
        st = sb("st", [32, 8])
        cat_i = sb("cat_i", [P, Q, NCAT], I32)
        cat_w = sb("cat_w", [P, Q, NCAT])
        cat_f = sb("cat_f", [P, Q, NCAT])
        cat_x = sb("cat_x", [P, NCAT, Q], U32)
        tv = sb("tv", [P, Q, E])
        pooled = sb("pooled", [P, 2 * Q, E])
        rlen = sb("rlen", [P, Q])
        vrow = sb("vrow", [NR, P])
        vecT = sb("vecT", [P, NR])
        a3c = sb("a3c", [P, 1])
        bhc = sb("bhc", [P, 1])
        nums = sb("nums", [P, Q, 19])
        Wn = sb("Wn", [19, 3 * E])
        kpart = sb("kpart", [P, 4, KT])
        kk = sb("kk", [P, 4])
        xw = sb("xw", [P, KT, 32])
        xsum = sb("xsum", [P, 4])
        fin = sb("fin", [P, 12, Q])

        parts = [parts_r[:, t, :].rearrange("p (h e) -> p h e", e=3 * E) for t in range(2)]
        cnt = cnt_r[:, :].bitcast(BF16)[:, 0:NHI * P].rearrange("p (h v) -> p h v", v=P)
        baseT = cnt_r[:, :].rearrange("p (k b) -> p k b", b=B)
        tab0 = cnt_r[:, 0:NHI * E].rearrange("p (h e) -> p h e", e=E)
        tab1 = [embT[:, 1, 0:2 * n * E].rearrange("p (h e) -> p h e", e=E) for n in NGH]
        NHH = 2 * NGH[0]
        pieces = [(0, (0, NHH), tab0[:, 0:NHH, :]), (0, (NHH, NHI), tab0[:, NHH:NHI, :]),
                  (1, (0, NHH), tab1[0]), (1, (NHH, NHI), tab1[1])]
        low = parts_r[:, 0, :].bitcast(F32)
        high = parts_r[:, 1, :].bitcast(F32)
        base = low[:, 0:Q * FEAT].rearrange("p (q f) -> p q f", f=FEAT)
        hid_i = low[0:GR, 0:1024].bitcast(I32)
        hid_w = low[0:GR, 1024:2048]
        hid_f = low[0:GR, 2048:3072]
        A1d = low[:, 3072:4096].rearrange("p (f n) -> p f n", n=HID)
        A1s = low[:, 4096:4096 + HID]
        QL = Q * L
        ids_i = [high[:, 0:QL].bitcast(I32), high[:, QL:2 * QL].bitcast(I32)]
        msk_i = high[:, 2 * QL:3 * QL].bitcast(I32)
        ids_w = high[:, 3 * QL:4 * QL]
        ids_f = high[:, 4 * QL:5 * QL]
        ids_c = high[:, 5 * QL:6 * QL].bitcast(I32)
        tag_lo, tag_hi = high[:, 0:QL], high[:, QL:2 * QL]
        assert 6 * QL <= NHI * 3 * E // 2 and NHH * E <= CH * P and V % 2 == 0 and Q * FEAT <= NHI * 3 * E // 2
        KE = (NHI * 3 * E // 2 - Q * FEAT) // H1
        D1e = low[:, Q * FEAT:Q * FEAT + KE * H1].rearrange("p (k n) -> p k n", n=H1)
        D1l = high[:, 0:(KT - KE) * H1].rearrange("p (k n) -> p k n", n=H1)
        late = (KT - KE) * H1
        D2s = high[:, late:late + M1 * H2].rearrange("p (k n) -> p k n", n=H2)
        D3s = high[:, late + M1 * H2:late + M1 * H2 + M2 * H3].rearrange("p (k n) -> p k n", n=H3)
        embf = emb[:, :, :].rearrange("p a b -> p (a b)")
        g1 = embf[:, 0:M1 * B].rearrange("p (k b) -> p k b", b=B)
        g2 = h1[:, :, :, :].rearrange("p a b c -> p (a b c)")[:, 0:M2 * B].rearrange("p (k b) -> p k b", b=B)
        g3 = embf[:, M1 * B:M1 * B + M2 * B].rearrange("p (k b) -> p k b", b=B)
        iota_i = junk[:, :, :].rearrange("p a b -> p (a b)").bitcast(I32)[:, 0:P]
        numT = oh_lo[:, :, :, :].rearrange("p a b c -> p (a b c)").bitcast(F32)[0:19, 0:B]
        onesq = wq[:, 0, 0:P]
        xrow = srow[:, :, :].rearrange("p a b -> p (a b)")[:, 0:B]
        finT = pen[0:Q, 0:P]
        tvq = tv[:, :, :].rearrange("p (a b) e -> p b a e", a=2)

        def by_quarter(x):
            return x.rearrange("p (b a) e -> p b a e", a=2)

        ps = ctx.enter_context(nc.psum_tensor("ps", [P, 8, 512], F32))
        BZ1, BZ2, BSC, BWB, BTR, BCN, BPL = 0, 2, 3, 4, 5, 6, 7

        ld_hid, ld_cat, ld_ids, ld_w, ld_vec, ld_late = map(sem, [
            "ld_hid", "ld_cat", "ld_ids", "ld_w", "ld_vec", "ld_late"])
        ld_tab = [sem(f"ld_tab{n}") for n in range(4)]
        ld_d1e = sem("ld_d1e")
        ld_mrow = sem("ld_mrow")
        consts = sem("consts")
        sel_ok = sem("sel_ok")
        prep = sem("prep")
        hid_ok = sem("hid_ok")
        cat_ok = sem("cat_ok")
        ids_ok = sem("ids_ok")
        a1_ok = sem("a1_ok")
        hidx_ok = sem("hidx_ok")
        setT = sem("setT")
        setE = sem("setE")
        idE = sem("idE")
        tv_got = sem("tv_got")
        tab_hi = sem("tab_hi")
        tab_sub = sem("tab_sub")
        tab_zero = sem("tab_zero")
        staged = sem("staged")
        got = [sem(f"got{c}") for c in range(CH)]
        turns = sem("turns")
        emb_t = sem("emb_t")
        embT_ok = sem("embT_ok")
        wq_ok = sem("wq_ok")
        z1_ok = sem("z1_ok")
        h1_ok = sem("h1_ok")
        z2_ok = sem("z2_ok")
        h2_ok = sem("h2_ok")
        sc_ok = sem("sc_ok")
        srow_ok = sem("srow_ok")
        sc_moved = [sem(f"sc_moved{n}") for n in range(4)]
        soft = sem("soft")
        exp_ok = sem("exp_ok")
        w_ok = sem("w_ok")
        wb_ok = sem("wb_ok")
        att_ok = sem("att_ok")
        att_mv = sem("att_mv")
        oh_ok = sem("oh_ok")
        cn_ok = sem("cn_ok")
        cn_mv = sem("cn_mv")
        pl_ok = sem("pl_ok")
        pl_mv = sem("pl_mv")
        pl_ch = sem("pl_ch")
        cats_got = [sem(f"cats_got{k}") for k in range(NCAT // 2)]
        numT_ok = sem("numT_ok")
        kpart_ok = sem("kpart_ok")
        kk_ok = sem("kk_ok")
        tv_ok = sem("tv_ok")
        dch = sem("dch")
        ach = sem("ach")
        base_ok = sem("base_ok")
        x_ok = sem("x_ok")
        x_mv = sem("x_mv")
        fin_ok = sem("fin_ok")
        finT_ok = sem("finT_ok")
        bT = sem("bT")
        bT_mv = sem("bT_mv")
        pe_e = sem("pe_e")
        out_ok = sem("out_ok")

        block = ctx.enter_context(nc.Block())

        N_VEC = 20
        N_SET = 6
        EARLY = {0: (3,), 2: (4,), 4: (5,), 5: (6,)}
        SOFT = 15

        @block.sync
        def _(sp):
            sp.dma_start(hid_i.rearrange("c (g p) -> c g p", p=P),
                         hist_ids.rearrange("b l -> (b l)").rearrange("(g c p) -> c g p", c=GR, p=P)
                         ).then_inc(ld_hid, 16)
            for t, off in ((user_cat, 0), (item_cat, NU), (ctx_cat, NU + NI)):
                sp.dma_start(cat_i[:, :, off:off + t.shape[1]],
                             t.rearrange("(q p) f -> p q f", p=P)).then_inc(ld_cat, 16)
            for h in range(2):
                sp.dma_start(A1d[E * h:E * h + E, :, :], A1.rearrange("(f e) n -> e f n", e=E)).then_inc(ld_w, 16)
            sp.dma_start(A2s[:, :, :], A2.rearrange("(k p) m -> p k m", p=P)).then_inc(ld_w, 16)
            for t, src in enumerate((author_ids, tag_ids)):
                sp.dma_start(ids_i[t].rearrange("p (q l) -> p q l", l=L),
                             src.rearrange("(q p) l -> p q l", p=P)).then_inc(ld_ids, 16)
            sp.dma_start(msk_i.rearrange("p (q l) -> p q l", l=L),
                         hist_mask.rearrange("(q p) l -> p q l", p=P)).then_inc(ld_ids, 16)
            def load_mask(b):
                for h in range(2):
                    r0 = HALF * h + PB * b
                    sp.dma_start(mrow[PB * h:PB * h + PB, :],
                                 hist_mask[r0:r0 + PB, :] if isinstance(b, int) else hist_mask[bass.ds(r0, PB), :]
                                 ).then_inc(ld_mrow, 16)

            load_mask(0)
            sp.wait_ge(ld_vec, 16 * N_VEC)
            sp.wait_ge(ld_ids, 48)
            for n, (t, (h0, h1_), dst) in enumerate(pieces):
                if n == 1:
                    sp.wait_ge(tab_zero, 1)
                if n == 3:
                    sp.wait_ge(tab_zero, 2)
                rows = item_emb[(1, NI - 1)[t], P * h0:min(P * h1_, V), :]
                full = rows.shape[0] // (2 * P)
                sp.dma_start(dst[:, 0:2 * full, :].rearrange("p (g b) e -> p g (b e)", b=2),
                             rows[0:2 * P * full, :].rearrange("(g p b) e -> p g (b e)", p=P, b=2)
                             ).then_inc(ld_tab[n], 16)
                rest = rows.shape[0] - 2 * P * full
                if rest:
                    sp.dma_start(dst[0:rest // 2, 2 * full:2 * full + 2, :].rearrange("p b e -> p (b e)"),
                                 rows[2 * P * full:, :].rearrange("(p b) e -> p (b e)", b=2)
                                 ).then_inc(ld_tab[n], 16)

            def move_scores(b, first):
                if not first:
                    sp.wait_ge(soft, SOFT * (b - 1) + 3)
                    load_mask(b)
                for n in range(4):
                    sp.wait_ge(srow_ok, 4 * b + n + 1)
                    for h in range(2):
                        sp.dma_start(Sc[PB * h + 4 * n:PB * h + 4 * n + 4, :],
                                     srow[0:97:32, n % 2, L * h:L * h + L]).then_inc(sc_moved[n], 16)

            move_scores(0, True)
            with sp.Fori(1, NBLK) as b:
                move_scores(b, False)

            sp.wait_ge(pl_ok, 2 * Q)
            sp.dma_start(D1l, D1[P * KE:, :].rearrange("(k p) n -> p k n", p=P)).then_inc(ld_late, 16)
            sp.dma_start(D2s, D2.rearrange("(k p) n -> p k n", p=P)).then_inc(ld_late, 16)
            sp.dma_start(D3s, D3.rearrange("(k p) n -> p k n", p=P)).then_inc(ld_late, 16)
            sp.wait_ge(finT_ok, 1)
            sp.dma_start(out.rearrange("(q p) -> q p", p=P), finT).then_inc(out_ok, 16)
            sp.wait_ge(out_ok, 16)

        @block.gpsimd
        def _(pool):
            pool.memset(ident[:, :], 0.0).then_inc(consts, 1)
            pool.memset(sel[0:32, :, :], 0.0).then_inc(consts, 1)
            pool.iota(iota_i, pattern=[[1, P]], base=0, channel_multiplier=0).then_inc(consts, 1)
            pool.wait_ge(consts, 3)
            pool.affine_select(out=ident[:, :], in_=ident[:, :], compare_op=ALU.not_equal, fill=1.0, base=0,
                               pattern=[[-1, P]], channel_multiplier=1).then_inc(consts, 1)
            pool.affine_select(out=sel[0:32, :, :].rearrange("k j (h c) -> k j h c", h=2),
                               in_=sel[0:32, :, :].rearrange("k j (h c) -> k j h c", h=2),
                               compare_op=ALU.not_equal, fill=1.0, base=0,
                               pattern=[[-1, PB], [-PB, 2], [0, E]], channel_multiplier=1).then_inc(consts, 1)

            def gather(dst, table, idx, done):
                pool.indirect_dma_start(out=dst, out_offset=None, in_=table,
                                        in_offset=bass.IndirectOffsetOnAxis(ap=idx, axis=0)).then_inc(done, 16)

            pool.wait_ge(cat_ok, 1)
            for q in range(Q):
                gather(tv[:, q % 2 * 2 + q // 2, :], item_emb[0], cat_x[:, NU, q:q + 1], tv_got)




            def gather_block(b, u, first):
                pool.wait_ge(staged, b + 1)
                pool.sem_inc(turns, 1)
                for c in range(CH):
                    if not first and c % 4 == 0:
                        pool.wait_ge(emb_t, TG * (b - 1) + c // 4 + 1)
                        pool.sem_inc(turns, 1)
                    for h in range(2):
                        gather(emb[:, c, E * h:E * h + E], item_emb[0], istage[:, u, h, c:c + 1], got[c])

            gather_block(0, 0, True)
            with pool.Fori(1, NBLK - 1, 2) as b:
                gather_block(b, 1, False)
                gather_block(b + 1, 0, False)
            gather_block(NBLK - 1, 1, False)

            pool.wait_ge(pl_ok, Q)
            for f in range(NCAT):
                if f == NU:
                    continue
                t = user_emb if f < NU else item_emb if f < NU + NI else ctx_emb
                for q in range(Q):
                    gather(base[:, q, E * f:E * f + E], t.rearrange("f v e -> (f v) e"), cat_x[:, f, q:q + 1], cats_got[f // 2])
            pool.dma_start(D1e, D1[0:P * KE, :].rearrange("(k p) n -> p k n", p=P)).then_inc(ld_d1e, 16)

        @block.tensor
        def _(pe):
            mm = nc.tensor.matmul

            n_set = [0]

            def set_bank():
                n = n_set[0]
                if n >= N_SET + 2:
                    pe.wait_ge(idE, n - N_SET - 1)
                elif n >= 2:
                    pe.wait_ge(setE, n - 1)
                n_set[0] += 1
                return (BWB, BPL)[n % 2]

            pe.wait_ge(consts, 5)
            pe.wait_ge(hid_ok, 1)
            for h in range(2):
                k = set_bank()
                for g in range(4):
                    i = nc.tensor.transpose(ps[:, k, P * g:P * g + GR],
                                            hid_f[:, (4 * h + g) * P:(4 * h + g + 1) * P], ident[0:GR, 0:GR])
                i.then_inc(setT, 1)
            k = set_bank()
            pe.wait_ge(ld_vec, 16 * N_VEC)
            nc.tensor.transpose(ps[:, k, 0:NR], vrow[:, :], ident[0:NR, 0:NR]).then_inc(setT, 1)
            k = set_bank()
            pe.wait_ge(tv_got, 16 * Q)
            for q in range(2):
                i = nc.tensor.transpose(ps[:, k, P * q:P * q + P], tv[:, 2 * q:2 * q + 2, :].rearrange("p a e -> p (a e)"), ident[:, :])
            i.then_inc(setT, 1)
            pe.wait_ge(setE, 4)
            pe.wait_ge(a1_ok, 1)
            for h in range(2):
                k = set_bank()
                for m in range(HK):
                    i = mm(ps[:, k, HALF * m:HALF * m + HALF], A1s[E * h:E * h + E, P * m:P * m + P],
                           qT[E * h:E * h + E, :], start=True, stop=True)
                i.then_inc(setT, 1)

            def transpose_ids(t):
                for q in range(Q):
                    k = set_bank()
                    if q == 0:
                        pe.wait_ge(ids_ok, t + 1)
                    for comp, src in enumerate((ids_w, ids_f) if t == 0 else (tag_lo, tag_hi)):
                        for h in range(2):
                            i = nc.tensor.transpose(ps[0:LH, k, (2 * comp + h) * P:(2 * comp + h + 1) * P],
                                                    src[:, L * q + LH * h:L * q + LH * h + LH], ident[:, :])
                    i.then_inc(setT, 1)

            def transpose_group(b, g, first=False):
                if not (first and g == 0):
                    pe.wait_ge(embT_ok, TG * b + g)
                for n, c in enumerate(range(4 * g, min(4 * g + 4, CH))):
                    pe.wait_ge(got[c], 32 * (b + 1))
                    i = nc.tensor.transpose(ps[:, BTR, P * n:P * n + P], emb[:, c, :], ident[:, :])
                i.then_inc(emb_t, 1)

            def layer1(b, j, u, first):
                s = PB * b + j
                cover = lambda jj: -(-L * (jj + 1) // 512)
                if j == 0 or cover(j) != cover(j - 1):
                    pe.wait_ge(embT_ok, TG * b + min(cover(j), TG))
                pe.wait_ge(wq_ok, s + 1)
                for m in range(HK):
                    for h in range(2):
                        if m == 0 and not (first and j == 0):
                            pe.wait_ge(h1_ok, 2 * s - 1 + h)
                        i = mm(ps[:, BZ1 + h, L * m:L * m + L], wq[E * h:E * h + E, j % 2, P * m:P * m + P],
                               embT[E * h:E * h + E, u, L * j:L * j + L], start=True, stop=True)
                        if m == HK - 1:
                            i.then_inc(z1_ok, 1)

            def counts(b, j, first):
                s = PB * b + j
                pe.wait_ge(oh_ok, s + 1)
                if not (first and j == 0):
                    pe.wait_ge(cn_mv, s)
                for v in range(VS):
                    for h in range(2):
                        i = mm(ps[:, BCN, NHI * v:NHI * v + NHI], oh_lo[0:LH, j % 2, :, 2 * v + h],
                               oh_hi[0:LH, j % 2, :, 2 * v + h], start=(h == 0), stop=(h == 1))
                i.then_inc(cn_ok, 1)

            def pool_product(k, t):
                pe.wait_ge(cn_mv, 2 * PB * (k + 1))
                pe.wait_ge(pl_mv, k + 1)
                for hi in range(NHI):
                    i = mm(ps[:, BPL, 0:3 * E], cnt[:, hi, :], parts[t][:, hi, :], start=(hi == 0), stop=(hi == NHI - 1))
                i.then_inc(pl_ok, 1)

            def layer2(b, j, first):
                s = PB * b + j
                if first and j == 0:
                    return
                pe.wait_ge(h1_ok, 2 * s)
                if not (first and j == 1):
                    pe.wait_ge(h2_ok, s - 1)
                for m in range(HK):
                    i = mm(ps[:, BZ2, 0:2 * L], A2s[:, m, :], h1[:, (j - 1) % 2, m, :], start=(m == 0), stop=(m == HK - 1))
                i.then_inc(z2_ok, 1)

            def layer3(b, j, first):
                if first and j == 1:
                    return
                pe.wait_ge(h2_ok, PB * b + j - 1)
                if not (first and j == 5):
                    pe.wait_ge(srow_ok, 4 * b + (j - 5) // 4)
                for n in range(4):
                    i = mm(ps[32 * n:32 * n + 32, BSC, 0:2 * L], A3s[:, :], h2[:, n, :], start=True, stop=True,
                           tile_position=(0, 32 * n))
                i.then_inc(sc_ok, 1)

            def spread(b, m):
                if m == 0:
                    pe.wait_ge(sel_ok, 2)
                    pe.wait_ge(w_ok, b + 1)
                else:
                    pe.wait_ge(att_ok, PB * b + 2 * m)
                for r in range(2):
                    i = mm(ps[:, BWB, L * r:L * r + L], sel[:, 2 * m + r, :], wpart[:, :], start=True, stop=True)
                i.then_inc(wb_ok, 1)

            def steps(b, u, first=False, last=False, k=None, t=None):
                for j in range(PB):
                    if first:
                        for g in EARLY.get(j, ()):
                            transpose_group(0, g)
                    layer1(b, j, u, first)
                    if j == 0 and k is not None:
                        pool_product(k, t)
                    counts(b, j, first)
                    if j % 4 == 1:
                        layer3(b, j, first)
                    layer2(b, j, first)
                    if not first and 5 <= j < 13:
                        spread(b - 1, j - 5)
                    if not last and j >= PB - TG:
                        transpose_group(b + 1, j - (PB - TG))

            transpose_ids(0)
            transpose_group(0, 0, True)
            transpose_group(0, 1)
            transpose_ids(1)
            transpose_group(0, 2)
            pe.wait_ge(idE, 2 * Q)
            steps(0, 0, first=True)
            pe.wait_ge(tab_sub, 8)
            for t, k0, k1 in ((0, 0, Q), (1, Q, 2 * Q - 1)):
                with pe.Fori(k0, k1) as k:
                    steps(2 * k + 1, 1)
                    steps(2 * k + 2, 0, k=k, t=t)
            steps(NBLK - 1, 1, last=True)
            pool_product(2 * Q - 1, 1)
            layer2(NBLK, 0, False)
            layer3(NBLK, 1, False)

            pe.wait_ge(prep, 2)
            pe.wait_ge(ld_vec, 16 * N_VEC)
            for q in range(Q):
                i = nc.tensor.transpose(ps[0:19, BTR, P * q:P * q + P], nums[:, q, :], ident[:, :])
            i.then_inc(pe_e, 1)
            pe.wait_ge(numT_ok, 1)
            pe.wait_ge(pl_mv, 2 * Q + 1)
            for q in range(Q):
                i = mm(ps[:, BCN + q // 2, 3 * E * (q % 2):3 * E * (q % 2) + 3 * E], numT[:, P * q:P * q + P],
                       Wn[:, :], start=True, stop=True)
            i.then_inc(pe_e, 1)
            pe.wait_ge(kpart_ok, 1)
            mm(ps[:, BTR, 0:3], onesq, kk[:, 0:3], start=True, stop=True).then_inc(pe_e, 1)

            bank = (BCN, BPL)

            def base_tile(kf):
                if kf < 2:
                    pe.wait_ge(ach, 2)
                else:
                    pe.wait_ge(bT_mv, kf - 1)
                if kf == F_ITEM // P:
                    pe.wait_ge(tv_ok, 1)
                if kf == F_ATT // P:
                    pe.wait_ge(base_ok, 1)
                if kf < NCAT // 2:
                    pe.wait_ge(cats_got[kf], 16 * Q * (2 - (kf == NU // 2)))
                for q in range(Q):
                    i = nc.tensor.transpose(ps[:, bank[kf % 2], P * q:P * q + P],
                                            base[:, q, P * kf:P * kf + P], ident[:, :])
                i.then_inc(bT, 1)

            def deep1(kf):
                pe.wait_ge(bT_mv, kf + 1)
                w = D1e[:, kf, :] if kf < KE else D1l[:, kf - KE, :]
                for m in range(M1):
                    i = mm(ps[:, m, :], w[:, P * m:P * m + P], baseT[:, kf, :], start=(kf == 0), stop=(kf == KT - 1))
                    if kf == KT - 1:
                        i.then_inc(pe_e, 1)

            pe.wait_ge(srow_ok, 4 * NBLK)
            pe.wait_ge(ld_d1e, 16)
            base_tile(0)
            m = 0
            for kf in range(1, KT):
                if kf == F_ATT // P:
                    pe.wait_ge(att_mv, NBLK)
                    for q in range(2):
                        i = nc.tensor.transpose(ps[:, BTR, P * q:P * q + P], attT[:, P * q:P * q + P], ident[:, :])
                    i.then_inc(pe_e, 1)
                else:
                    base_tile(kf)
                if kf - 1 == KE:
                    pe.wait_ge(ld_late, 48)
                deep1(kf - 1)
                if kf == F_ATT // P:
                    base_tile(kf)
                if kf >= 2 and m < PB // 2:
                    if m == 0:
                        pe.wait_ge(kk_ok, 1)
                    spread(NBLK - 1, m)
                    m += 1
            assert m == PB // 2
            deep1(KT - 1)
            pe.wait_ge(att_ok, HALF)
            for kf in range(KT):
                n = 32 * (kf % 4)
                i = mm(ps[n:n + 32, BWB, :], xw[:, kf, :], baseT[:, kf, :], start=(kf < 4), stop=(kf >= KT - 4),
                       tile_position=(0, n))
            i.then_inc(x_ok, 1)
            for m in range(M2):
                for kf in range(M1):
                    if m == 0:
                        pe.wait_ge(ach, 2 + kf + 1)
                    i = mm(ps[:, BCN + m, :], D2s[:, kf, P * m:P * m + P], g1[:, kf, :], start=(kf == 0), stop=(kf == M1 - 1))
                i.then_inc(pe_e, 1)
            for m in range(M2):
                for kf in range(M2):
                    if m == 0:
                        pe.wait_ge(ach, 2 + M1 + kf + 1)
                    i = mm(ps[:, m, :], D3s[:, kf, P * m:P * m + P], g2[:, kf, :], start=(kf == 0), stop=(kf == M2 - 1))
                i.then_inc(pe_e, 1)
            pe.wait_ge(x_mv, 1)
            for q in range(Q):
                mm(ps[:, BWB, 4 * q:4 * q + 4], xrow[:, P * q:P * q + P], xsum[:, :], start=True, stop=True)
            pe.wait_ge(ach, 2 + M1 + 2 * M2)
            for q in range(Q):
                for kf in range(M2):
                    i = mm(ps[:, BWB, 4 * Q + q:4 * Q + q + 1], g3[:, kf, P * q:P * q + P],
                           vecT[:, R_WH2 + kf:R_WH2 + kf + 1], start=(kf == 0), stop=(kf == M2 - 1))
            i.then_inc(pe_e, 1)
            pe.wait_ge(fin_ok, 1)
            nc.tensor.transpose(ps[0:Q, BWB, 0:P], fin[:, 11, :], ident[:, :]).then_inc(pe_e, 1)

        @block.scalar
        def _(act):
            def rows(dst, n, src):
                act.dma_start(vrow[dst:dst + n, :], src).then_inc(ld_vec, 16)
            rows(R_CW, 3 * KT, cross_w.rearrange("v (k p) -> (v k) p", p=P))
            rows(R_CB, 3 * KT, cross_b.rearrange("v (k p) -> (v k) p", p=P))
            rows(R_WH, KT + M2, Wh.rearrange("(k p) o -> k (p o)", p=P))
            rows(R_A1, HK, a1.rearrange("(k p) -> k p", p=P))
            rows(R_A2, 1, a2.rearrange("(k p) -> k p", p=P))
            rows(R_A3, 1, A3.rearrange("(k p) o -> k (p o)", p=P))
            rows(R_D1, M1, d1.rearrange("(k p) -> k p", p=P))
            rows(R_D2, M2, d2.rearrange("(k p) -> k p", p=P))
            rows(R_D3, M2, d3.rearrange("(k p) -> k p", p=P))
            act.dma_start(a3c[:, :], a3.rearrange("(a n) -> a n", a=1).to_broadcast([P, 1])).then_inc(ld_vec, 16)
            act.dma_start(bhc[:, :], bh.rearrange("(a n) -> a n", a=1).to_broadcast([P, 1])).then_inc(ld_vec, 16)
            act.wait_ge(prep, 2)
            col = 0
            for n, (x, w, bias) in enumerate(((user_num, Wu, bu), (item_num, Wi, bi), (ctx_num, Wc, bc))):
                d = x.shape[1]
                act.dma_start(nums[:, :, col:col + d], x.rearrange("(q p) f -> p q f", p=P)).then_inc(ld_vec, 16)
                act.dma_start(Wn[col:col + d, E * n:E * n + E], w).then_inc(ld_vec, 16)
                act.dma_start(Wn[18:19, E * n:E * n + E], bias.rearrange("(a n) -> a n", a=1)).then_inc(ld_vec, 16)
                col += d

            def table_part(n, part):
                t, (h0, h1_), raw = pieces[n]
                if part == 0:
                    act.wait_ge(ld_tab[n], 32 if n % 2 else 16)
                else:
                    act.wait_ge(tab_sub, n + 1 if n < 2 else 2 * n + 1)
                nc.scalar.activation(parts[t][:, h0:h1_, E * part:E * part + E], raw, ACT.Copy).then_inc(tab_hi, 1)

            def ids_out(t):
                for q in range(Q):
                    n = N_SET + Q * t + q
                    act.wait_ge(setT, n + 1)
                    v0 = 2 * (B * t + P * q)
                    nc.scalar.activation(idT[0:LH, :, v0:v0 + 2 * P].rearrange("l c (v h) -> l c h v", h=2),
                                         ps[0:LH, (BWB, BPL)[n % 2], :].rearrange("l (c h v) -> l c h v", c=2, h=2),
                                         ACT.Copy).then_inc(idE, 1)

            def transposed(b, g, u, reused):
                act.wait_ge(emb_t, TG * b + g + 1)
                if reused:
                    n = min(PB, -(-min(512 * (g + 1), CH * P) // L))
                    act.wait_ge(att_ok, PB * (b - 2) + n)
                w = min(512, CH * P - 512 * g)
                nc.scalar.activation(embT[:, u, 512 * g:512 * g + w], ps[:, BTR, 0:w], ACT.Copy).then_inc(embT_ok, 1)

            def relu1(b, j, first):
                s = PB * b + j
                for h in range(2):
                    act.wait_ge(z1_ok, 2 * s + h + 1)
                    if h == 0 and not (first and j < 2):
                        act.wait_ge(z2_ok, s - 1)
                    for m in range(HK):
                        bias = qbias[:, m, h, s:s + 1] if isinstance(s, int) else qbias[:, m, h, bass.ds(s, 1)]
                        i = nc.scalar.activation(h1[:, j % 2, m, L * h:L * h + L], ps[:, BZ1 + h, L * m:L * m + L],
                                                 ACT.Relu, bias=bias)
                    i.then_inc(h1_ok, 1)

            def counts_out(b, j, u, first, k):
                s = PB * b + j
                act.wait_ge(cn_ok, s + 1)
                if j == 0 and k is not None:
                    act.wait_ge(pl_ok, k + 1)
                v0 = PB * VS * u + VS * j
                nc.scalar.activation(cnt[:, :, v0:v0 + VS].rearrange("p h v -> p v h"),
                                     ps[:, BCN, 0:VS * NHI].rearrange("p (v h) -> p v h", v=VS),
                                     ACT.Copy).then_inc(cn_mv, 1)

            def relu2(b, j, first):
                s = PB * b + j
                if first and j == 0:
                    return
                act.wait_ge(z2_ok, s)
                if j % 4 == 1 and not (first and j == 1):
                    act.wait_ge(sc_ok, 4 * b + (j - 1) // 4)
                nc.scalar.activation(h2[:, (j - 1) % 4, :], ps[:, BZ2, 0:2 * L], ACT.Relu,
                                     bias=vecT[:, R_A2:R_A2 + 1]).then_inc(h2_ok, 1)

            def scores_out(b, j, first):
                if first and j == 1:
                    return
                n = (j - 2) // 4 % 4
                act.wait_ge(sc_ok, 4 * b + (j - 1) // 4)
                before = b - 1 if n == 3 else b
                if n >= 2:
                    act.wait_ge(sc_moved[n - 2], 32 * (before + 1))
                elif not first:
                    act.wait_ge(sc_moved[n + 2], 32 * before)
                nc.scalar.activation(srow[:, n % 2, :], ps[:, BSC, 0:2 * L], ACT.Identity,
                                     bias=a3c[:, 0:1]).then_inc(srow_ok, 1)

            def exps(b):
                act.wait_ge(soft, SOFT * b + 6)
                nc.scalar.activation(ex[:, :], smk[:, :], ACT.Exp, bias=st[:, 1:2], accum_out=st[:, 2:3]).then_inc(exp_ok, 1)

            def steps(b, u, first=False, last=False, k=None):
                for j in range(PB):
                    if first:
                        for g in EARLY.get(j, ()):
                            transposed(0, g, 0, False)
                        if j in (2, 7):
                            table_part(2 + j // 7, 1)
                        if j == 5:
                            table_part(3, 0)
                        if j == PB - TG:
                            act.wait_ge(tab_sub, 8)
                    relu1(b, j, first)
                    if first and j == 0:
                        act.wait_ge(tab_sub, 4)
                    counts_out(b, j, u, first, k)
                    relu2(b, j, first)
                    if j % 4 == 1:
                        scores_out(b, j, first)
                    if j == 3 and not first:
                        exps(b - 1)
                    if not last and j >= PB - TG:
                        transposed(b + 1, j - (PB - TG), 1 - u, not first)

            act.wait_ge(consts, 5)
            for r in (32, 64):
                nc.scalar.activation(sel[r:r + 32, :, :], sel[0:32, :, :], ACT.Copy).then_inc(sel_ok, 1)
            ids_out(0)
            transposed(0, 0, 0, False)
            transposed(0, 1, 0, False)
            act.wait_ge(setE, N_SET)
            table_part(0, 0)
            table_part(1, 0)
            ids_out(1)
            table_part(0, 1)
            transposed(0, 2, 0, False)
            table_part(1, 1)
            table_part(2, 0)
            steps(0, 0, first=True)
            with act.Fori(0, NBLK // 2 - 1) as k:
                steps(2 * k + 1, 1)
                steps(2 * k + 2, 0, k=k)
            steps(NBLK - 1, 1, last=True)
            relu2(NBLK, 0, False)
            scores_out(NBLK, 1, False)
            exps(NBLK - 1)

            act.wait_ge(pe_e, 2)
            for n in range(2):
                nc.scalar.activation(base[:, 2 * n:2 * n + 2, F_NUM:F_NUM + 3 * E],
                                     ps[:, BCN + n, 0:6 * E].rearrange("p (q f) -> p q f", q=2),
                                     ACT.Relu).then_inc(ach, 1)
            for kf in range(KT):
                act.wait_ge(bT, kf + 1)
                nc.scalar.activation(baseT[:, kf, :], ps[:, (BCN, BPL)[kf % 2], :], ACT.Copy).then_inc(bT_mv, 1)
            for m in range(M1):
                act.wait_ge(pe_e, 4 + m + 1)
                nc.scalar.activation(g1[:, m, :], ps[:, m, :], ACT.Relu, bias=vecT[:, R_D1 + m:R_D1 + m + 1]).then_inc(ach, 1)
            for m in range(M2):
                act.wait_ge(pe_e, 4 + M1 + m + 1)
                nc.scalar.activation(g2[:, m, :], ps[:, BCN + m, :], ACT.Relu, bias=vecT[:, R_D2 + m:R_D2 + m + 1]).then_inc(ach, 1)
            for m in range(M2):
                act.wait_ge(pe_e, 4 + M1 + M2 + m + 1)
                nc.scalar.activation(g3[:, m, :], ps[:, m, :], ACT.Identity, bias=vecT[:, R_D3 + m:R_D3 + m + 1]).then_inc(ach, 1)

        @block.vector
        def _(dve):
            v = nc.vector
            done = [0]

            def chain(i):
                done[0] += 1
                i.then_inc(prep, 1)
                dve.wait_ge(prep, done[0])

            v.memset(st[:, :], 0.0).then_inc(pl_mv, 1)
            chain(v.memset(Wn[:, :], 0.0))
            chain(v.memset(nums[:, :, 18:19], 1.0))
            v.memset(tab0[:, NHI - 2:NHI, :], 0.0).then_inc(tab_zero, 1)

            def clamp(f, i, w, signal=None):
                chain(v.tensor_scalar(w, i, 0.0, float(V), ALU.is_lt, ALU.mult))
                chain(v.tensor_tensor(w, i, w, ALU.add))
                last = v.tensor_scalar(f, w, 0.0, float(V - 1), ALU.max, ALU.min)
                chain(last) if signal is None else last.then_inc(signal, 1)

            dve.wait_ge(ld_cat, 48)
            clamp(cat_f[:, :, :], cat_i[:, :, :], cat_w[:, :, :])
            for f in range(NCAT):
                first = 0 if f < NU else NU if f < NU + NI else NU + NI
                i = v.tensor_scalar(cat_x[:, f, :], cat_f[:, :, f], float((f - first) * V), None, ALU.add)
            i.then_inc(cat_ok, 1)
            dve.wait_ge(ld_hid, 16)
            clamp(hid_f, hid_i, hid_w, hid_ok)
            dve.wait_ge(ld_w, 48)
            v.tensor_tensor(A1hd[:, :], A1d[:, 1, :], A1d[:, 2, :], ALU.subtract)
            v.tensor_copy(A1p[:, :], A1d[:, 3, :])
            v.tensor_tensor(A1s, A1d[:, 0, :], A1d[:, 2, :], ALU.add).then_inc(a1_ok, 1)

            n_set = [0]

            def set_out():
                k = (BWB, BPL)[n_set[0] % 2]
                n_set[0] += 1
                dve.wait_ge(setT, n_set[0])
                return k

            for h in range(2):
                k = set_out()
                v.tensor_copy(hidx[:, h, :].rearrange("p (g c) -> p g c", c=GR),
                              ps[:, k, :].rearrange("p (g c) -> p g c", c=P)[:, :, 0:GR]).then_inc(setE, 1)
            dve.wait_ge(setE, 2)
            for b in range(2):
                v.tensor_scalar(istage[:, b, :, :], hidx[:, :, CH * b:CH * b + CH], 1.0, None, ALU.mult).then_inc(staged, 1)
            k = set_out()
            v.tensor_copy(vecT[:, :], ps[:, k, 0:NR]).then_inc(setE, 1)
            dve.wait_ge(setE, 3)
            v.tensor_copy(A3s[:, :], vecT[:, R_A3:R_A3 + 1].to_broadcast([P, 32]))
            k = set_out()
            v.tensor_copy(qT[:, :], ps[:, k, 0:HALF]).then_inc(setE, 1)
            for h in range(2):
                k = set_out()
                for m in range(HK):
                    i = v.tensor_scalar(qbias[:, m, h, :], ps[:, k, HALF * m:HALF * m + HALF],
                                        vecT[:, R_A1 + m:R_A1 + m + 1], None, ALU.add)
                i.then_inc(setE, 1)
            dve.wait_ge(consts, 3)
            chain(v.tensor_copy(iota[:, :, :], iota_i.unsqueeze(2).to_broadcast([P, P, 2 * VS])))

            dve.wait_ge(ld_ids, 48)
            chain(v.tensor_scalar(msk_i, msk_i, 0.0, None, ALU.is_gt))
            with nc.allow_low_precision(reason="sums of 0 and 1"):
                chain(v.tensor_reduce(rlen[:, :], msk_i.rearrange("p (q l) -> p q l", l=L), AX_X, ALU.add))
            chain(v.tensor_scalar(rlen[:, :], rlen[:, :], 1e-6, None, ALU.max))
            chain(v.reciprocal(rlen[:, :], rlen[:, :]))
            for t, (w, lo, hi) in enumerate(((ids_w, ids_w, ids_f), (tag_lo, tag_lo, tag_hi))):
                if t == 1:
                    dve.wait_ge(ids_ok, 1)
                clamp(ids_c, ids_i[t], w)
                chain(v.tensor_scalar(w.bitcast(I32), ids_c, 7, 126, ALU.arith_shift_right, ALU.bitwise_and))
                chain(v.scalar_tensor_tensor(out=ids_i[t], in0=ids_c, scalar=1, in1=w.bitcast(I32),
                                             op0=ALU.bitwise_and, op1=ALU.bitwise_or))
                chain(v.tensor_scalar(ids_c, ids_c, 1, 127, ALU.arith_shift_right, ALU.bitwise_and))
                chain(v.tensor_copy(lo, ids_c))
                v.scalar_tensor_tensor(out=hi, in0=ids_i[t], scalar=1.0, in1=msk_i, op0=ALU.add,
                                       op1=ALU.mult).then_inc(ids_ok, 1)
            assert n_set[0] == N_SET

            def table_rest(n, part):
                t, (h0, h1_), raw = pieces[n]
                done = n + 1 + 2 * part if n < 2 else 2 * n + 1 + part
                dve.wait_ge(tab_hi, done)
                dst = raw if part == 0 else parts[t][:, h0:h1_, 2 * E:3 * E]
                v.tensor_tensor(dst, raw, parts[t][:, h0:h1_, E * part:E * part + E], ALU.subtract).then_inc(tab_sub, 1)
                if n == 2 and part == 1:
                    dve.wait_ge(tab_sub, done)
                    v.memset(tab1[1][:, 2 * NGH[1] - 2:2 * NGH[1], :], 0.0).then_inc(tab_zero, 1)

            def weights(s, j, free):
                if free is not None:
                    dve.wait_ge(z1_ok, free)
                q = qT[:, s:s + 1] if isinstance(s, int) else qT[:, bass.ds(s, 1)]
                v.scalar_tensor_tensor(out=wq[:, j % 2, :], in0=A1p[:, :], scalar=q, in1=A1hd[:, :],
                                       op0=ALU.mult, op1=ALU.add).then_inc(wq_ok, 1)

            def onehots(s, j, free):
                if free is not None:
                    dve.wait_ge(cn_ok, free)
                for comp, (oh, n0, n) in enumerate(((oh_lo, 0, P), (oh_hi, 1, NHI))):
                    code = idT[0:LH, comp, 2 * VS * s:2 * VS * s + 2 * VS] if isinstance(s, int) else \
                        idT[0:LH, comp, bass.ds(s * (2 * VS), 2 * VS)]
                    i = v.tensor_tensor(oh[0:LH, j % 2, :, :], iota[0:LH, n0:n0 + n, :],
                                        code.unsqueeze(1).to_broadcast([LH, n, 2 * VS]), ALU.is_equal)
                i.then_inc(oh_ok, 1)

            def softmax(b):
                for n in range(4):
                    dve.wait_ge(sc_moved[n], 32 * (b + 1))
                dve.wait_ge(ld_mrow, 32 * (b + 1))
                mk = mrow[:, :]
                v.tensor_scalar(mkb[:, :], mk, 1.0, None, ALU.mult).then_inc(soft, 1)
                v.tensor_tensor(smk[:, :], Sc[:, :], mk, ALU.mult).then_inc(soft, 1)
                v.tensor_scalar(pen[:, :], mk, 1e9, -1e9, ALU.mult, ALU.add).then_inc(soft, 1)
                dve.wait_ge(soft, SOFT * b + 3)
                v.tensor_tensor(smk[:, :], smk[:, :], pen[:, :], ALU.add).then_inc(soft, 1)
                dve.wait_ge(soft, SOFT * b + 4)
                v.tensor_reduce(st[:, 0:1], smk[:, :], AX_X, ALU.max).then_inc(soft, 1)
                dve.wait_ge(soft, SOFT * b + 5)
                v.tensor_scalar(st[:, 1:2], st[:, 0:1], -1.0, None, ALU.mult).then_inc(soft, 1)
                dve.wait_ge(exp_ok, b + 1)
                v.tensor_tensor_reduce(out=exm[:, :], in0=ex[:, :], in1=mkb[:, :], scale=1.0, scalar=0.0, op0=ALU.mult,
                                       op1=ALU.add, accum_out=st[:, 3:4]).then_inc(soft, 1)
                v.reciprocal(st[:, 4:5], st[:, 2:3]).then_inc(soft, 1)
                dve.wait_ge(soft, SOFT * b + 8)
                v.tensor_scalar(st[:, 5:6], st[:, 3:4], st[:, 4:5], 1e-6, ALU.mult, ALU.max).then_inc(soft, 1)
                dve.wait_ge(soft, SOFT * b + 9)
                v.reciprocal(st[:, 6:7], st[:, 5:6]).then_inc(soft, 1)
                dve.wait_ge(soft, SOFT * b + 10)
                v.tensor_scalar(wts[:, :], exm[:, :], st[:, 4:5], st[:, 6:7], ALU.mult, ALU.mult).then_inc(soft, 1)
                dve.wait_ge(soft, SOFT * b + 11)
                v.tensor_copy(wpart[0:32, :], wts[:, :]).then_inc(soft, 1)
                dve.wait_ge(soft, SOFT * b + 12)
                v.tensor_tensor(wts[:, :], wts[:, :], wpart[0:32, :], ALU.subtract).then_inc(soft, 1)
                dve.wait_ge(soft, SOFT * b + 13)
                v.tensor_copy(wmid[:, :], wts[:, :]).then_inc(soft, 1)
                dve.wait_ge(soft, SOFT * b + 14)
                v.tensor_copy(wpart[32:64, :], wmid[:, :]).then_inc(soft, 1)
                v.tensor_tensor(wpart[64:96, :], wts[:, :], wmid[:, :], ALU.subtract).then_inc(w_ok, 1)

            def attend(b, m, u):
                dve.wait_ge(wb_ok, PB // 2 * b + m + 1)
                for r in range(2):
                    j = 2 * m + r
                    if m:
                        dve.wait_ge(att_ok, PB * b + j - 1)
                    v.tensor_tensor_reduce(out=junk[:, j % 2, :], in0=ps[:, BWB, L * r:L * r + L],
                                           in1=embT[:, u, L * j:L * j + L], scale=1.0, scalar=0.0, op0=ALU.mult,
                                           op1=ALU.add, accum_out=attS[:, 0, j:j + 1]).then_inc(att_ok, 1)

            def place(b):
                dve.wait_ge(att_ok, PB * b + PB)
                dst = attT[:, PB * b:PB * b + PB] if isinstance(b, int) else attT[:, bass.ds(b * PB, PB)]
                v.tensor_scalar(dst, attS[:, 0, :], 1.0, None, ALU.mult).then_inc(att_mv, 1)

            def stage(b, u):
                dve.wait_ge(emb_t, TG * (b + 1))
                src = hidx[:, :, CH * (b + 2):CH * (b + 3)] if isinstance(b, int) else \
                    hidx[:, :, bass.ds(CH * (b + 2), CH)]
                v.tensor_scalar(istage[:, u, :, :], src, 1.0, None, ALU.mult).then_inc(staged, 1)

            def pool_out(k):
                dve.wait_ge(pl_ok, k + 1)
                dst = pooled[:, k, :] if isinstance(k, int) else pooled[:, bass.ds(k, 1), :].rearrange("p a e -> p (a e)")
                v.tensor_scalar(dst, ps[:, BPL, 2 * E:3 * E], 1.0, None, ALU.mult).then_inc(pl_ch, 1)
                dve.wait_ge(pl_ch, 2 * k + 1)
                v.tensor_tensor(dst, ps[:, BPL, E:2 * E], dst, ALU.add).then_inc(pl_ch, 1)
                dve.wait_ge(pl_ch, 2 * k + 2)
                v.tensor_tensor(dst, ps[:, BPL, 0:E], dst, ALU.add).then_inc(pl_mv, 1)

            def steps(b, u, first=False, last=False, k=None, nostage=False):
                for j in range(PB):
                    s = PB * b + j
                    start = first and j == 0
                    if first and j in (1, 3, 6, 8):
                        table_rest(2 + (j > 3), int(j in (3, 8)))
                    if not (last and j == PB - 1):
                        weights(s + 1, j + 1, None if start else 2 * s)
                        onehots(s + 1, j + 1, None if start else s)
                    if j == 1 and k is not None:
                        pool_out(k)
                    if not first and j == 3:
                        softmax(b - 1)
                    if not first and 5 <= j < 13:
                        attend(b - 1, j - 5, 1 - u)
                    if not first and j == 13:
                        place(b - 1)
                    if j == 8 and not nostage:
                        stage(b, u)

            weights(0, 0, None)
            dve.wait_ge(idE, Q)
            onehots(0, 0, None)
            for part in range(2):
                for n in range(2):
                    table_rest(n, part)
            steps(0, 0, first=True)
            with dve.Fori(0, NBLK // 2 - 2) as k:
                steps(2 * k + 1, 1)
                steps(2 * k + 2, 0, k=k)
            steps(NBLK - 3, 1)
            steps(NBLK - 2, 0, k=NBLK // 2 - 2, nostage=True)
            steps(NBLK - 1, 1, last=True, nostage=True)
            pool_out(2 * Q - 1)

            n = [0]

            def link(i):
                n[0] += 1
                i.then_inc(dch, 1)
                dve.wait_ge(dch, n[0])

            cw = lambda i: vecT[:, R_CW + KT * i:R_CW + KT * i + KT]
            cb = lambda i: vecT[:, R_CB + KT * i:R_CB + KT * i + KT]
            wh = vecT[:, R_WH:R_WH + KT]
            link(v.memset(xw[:, :, :], 0.0))
            link(v.tensor_tensor(kpart[:, 0, :], cb(0), cw(1), ALU.mult))
            link(v.tensor_tensor(kpart[:, 3, :], cb(0), cb(1), ALU.add))
            link(v.tensor_tensor(kpart[:, 1, :], kpart[:, 3, :], cw(2), ALU.mult))
            link(v.tensor_tensor(kpart[:, 3, :], kpart[:, 3, :], cb(2), ALU.add))
            link(v.tensor_tensor(kpart[:, 2, :], kpart[:, 3, :], wh, ALU.mult))
            for i in range(3):
                link(v.tensor_copy(xw[:, :, i], cw(i)))
            link(v.tensor_copy(xw[:, :, 3], wh))
            link(v.tensor_reduce(xsum[:, :], ident[:, :].rearrange("p (n c) -> p c n", n=4)[:, 0:4, :], AX_X, ALU.add))
            dve.wait_ge(z1_ok, 2 * HALF)
            link(v.memset(onesq, 1.0))
            v.tensor_reduce(kk[:, 0:3], kpart[:, 0:3, :], AX_X, ALU.add).then_inc(kpart_ok, 1)
            dve.wait_ge(pe_e, 1)
            v.tensor_copy(numT, ps[0:19, BTR, :]).then_inc(numT_ok, 1)
            for q in range(Q):
                for t in range(2):
                    link(v.tensor_scalar(base[:, q, F_POOL + E * t:F_POOL + E * t + E], pooled[:, Q * t + q, :],
                                         rlen[:, q:q + 1], None, ALU.mult))
            v.tensor_copy(by_quarter(base[:, :, F_ITEM:F_ITEM + E]), tvq).then_inc(tv_ok, 1)
            dve.wait_ge(pe_e, 3)
            v.tensor_copy(kk[:, 0:3], ps[:, BTR, 0:3]).then_inc(kk_ok, 1)
            softmax(NBLK - 1)
            for m in range(PB // 2):
                attend(NBLK - 1, m, 1)
            place(NBLK - 1)
            dve.wait_ge(pe_e, 4)
            att = base[:, :, F_ATT:F_ATT + E]
            for h in range(2):
                link(v.tensor_copy(att[:, 2 * h:2 * h + 2, :],
                                   ps[:, BTR, 0:2 * P].rearrange("p (q h e) -> p q h e", q=2, h=2)[:, :, h, :]))
            link(v.tensor_tensor(by_quarter(base[:, :, F_MUL:F_MUL + E]), tvq, by_quarter(att), ALU.mult))
            v.tensor_tensor(by_quarter(base[:, :, F_DIF:F_DIF + E]), tvq, by_quarter(att), ALU.subtract).then_inc(base_ok, 1)
            dve.wait_ge(x_ok, 1)
            v.tensor_copy(xrow, ps[:, BWB, :]).then_inc(x_mv, 1)
            dve.wait_ge(pe_e, 5 + M1 + 2 * M2)
            f = lambda i: fin[:, i, :]
            link(v.tensor_copy(fin[:, 0:4, :].rearrange("p i q -> p q i"),
                               ps[:, BWB, 0:4 * Q].rearrange("p (q i) -> p q i", i=4)))
            link(v.tensor_copy(f(4), ps[:, BWB, 4 * Q:5 * Q]))
            link(v.tensor_scalar(f(5), f(0), 1.0, None, ALU.add))
            for i, (c, t, nxt) in enumerate(((5, 6, 7), (7, 8, 9))):
                link(v.tensor_tensor(f(t), f(c), f(i + 1), ALU.mult))
                link(v.tensor_scalar(f(t), f(t), kk[:, i:i + 1], None, ALU.add))
                link(v.tensor_tensor(f(nxt), f(t), f(c), ALU.add))
            link(v.tensor_tensor(f(10), f(9), f(3), ALU.mult))
            link(v.tensor_tensor(f(10), f(10), f(4), ALU.add))
            v.tensor_scalar(f(11), f(10), kk[:, 2:3], bhc[:, 0:1], ALU.add, ALU.add).then_inc(fin_ok, 1)
            dve.wait_ge(pe_e, 6 + M1 + 2 * M2)
            v.tensor_copy(finT, ps[0:Q, BWB, 0:P]).then_inc(finT_ok, 1)


_INS = ["r_user_cat", "r_user_num", "r_ctx_cat", "r_ctx_num", "r_hist_ids", "r_hist_author_ids", "r_hist_tag_ids",
        "r_hist_mask", "r_item_cat", "r_item_num", "L0_rec_user_emb", "L0_rec_item_emb", "L0_rec_ctx_emb",
        "L0_rec_Wu", "L0_rec_bu", "L0_rec_Wi", "L0_rec_bi", "L0_rec_Wc", "L0_rec_bc", "L0_rec_A1", "L0_rec_a1",
        "L0_rec_A2", "L0_rec_a2", "L0_rec_A3", "L0_rec_a3", "L0_rec_cross_w", "L0_rec_cross_b", "L0_rec_D1",
        "L0_rec_d1", "L0_rec_D2", "L0_rec_d2", "L0_rec_D3", "L0_rec_d3", "L0_rec_Wh", "L0_rec_bh"]


def kernel(**inputs):
    import numpy as np
    import concourse.bacc as bacc
    from concourse.bass_utils import run_bass_kernel_spmd

    nc = bacc.Bacc("TRN2", target_bir_lowering=False, num_devices=1)
    arrays, args = {}, []
    for name in _INS:
        a = np.ascontiguousarray(inputs[name])
        arrays["in_" + name] = a
        args.append(nc.dram_tensor("in_" + name, a.shape, mybir.dt.from_np(a.dtype), kind="ExternalInput").ap())
    out = nc.dram_tensor("out_0", (inputs["r_hist_ids"].shape[0],), F32, kind="ExternalOutput").ap()
    recommender(nc, *args, out)
    r = run_bass_kernel_spmd(nc, [arrays], core_ids=[0])
    return r.results[0]["out_0"]
```

```python
from contextlib import ExitStack

import concourse.bass as bass
from concourse import mybir

ALU = mybir.AluOpType
ACT = mybir.ActivationFunctionType
AX_X = mybir.AxisListType.X
F32 = mybir.dt.float32
BF16 = mybir.dt.bfloat16
I32 = mybir.dt.int32
F32R = mybir.dt.float32r
U32 = mybir.dt.uint32

P = 128


def recommender(nc, user_cat, user_num, ctx_cat, ctx_num, hist_ids, author_ids, tag_ids, hist_mask,
                item_cat, item_num, user_emb, item_emb, ctx_emb, Wu, bu, Wi, bi, Wc, bc,
                A1, a1, A2, a2, A3, a3, cross_w, cross_b, D1, d1, D2, d2, D3, d3, Wh, bh, out):
    B, L = hist_ids.shape
    V, E = item_emb.shape[1:]
    NU, NI, NC = user_cat.shape[1], item_cat.shape[1], ctx_cat.shape[1]
    NCAT = NU + NI + NC
    HID, MID = A2.shape
    FEAT, H1 = D1.shape
    H2, H3 = D2.shape[1], D3.shape[1]
    Q = B // P
    HALF = B // 2
    PB = 16
    NBLK = HALF // PB
    CH = PB * L // P
    TG = -(-CH // 4)
    HC = HALF * L // P
    LH = L // 2
    NG = -(-V // (2 * P))
    NHI = 2 * NG
    NSL = 7
    SG = NG // NSL
    VS = 4
    KT = FEAT // P
    HK, M1, M2 = HID // P, H1 // P, H2 // P
    GR = 100
    assert 2 * E == P and PB * L == CH * P and NBLK % 2 == 0 and VS * PB * NBLK == 2 * B
    assert HK == 2 and MID == P and FEAT == KT * P and H3 == H2

    R_CW, R_CB, R_WH = 0, 3 * KT, 6 * KT
    R_WH2 = R_WH + KT
    R_A1 = R_WH2 + M2
    R_A2 = R_A1 + HK
    R_A3 = R_A2 + 1
    R_D1 = R_A3 + 1
    R_D2 = R_D1 + M1
    R_D3 = R_D2 + M2
    NR = R_D3 + M2
    F_ITEM, F_CTX, F_NUM = NU * E, (NU + NI) * E, NCAT * E
    F_ATT = F_NUM + 3 * E
    F_POOL = F_ATT + E
    F_MUL, F_DIF = F_POOL + 2 * E, F_POOL + 3 * E

    with ExitStack() as ctx:
        def sb(name, shape, dt=F32):
            return ctx.enter_context(nc.sbuf_tensor(name, shape, dt))

        def sem(name):
            return ctx.enter_context(nc.semaphore(name))

        emb = sb("emb", [P, CH, 2 * E])
        embT = sb("embT", [P, 2, CH * P])
        h1 = sb("h1", [P, 2, HK, 2 * L])
        h1h = sb("h1h", [P, 2, 2 * L])
        h1l = sb("h1l", [P, 2, 2 * L])
        h2 = sb("h2", [P, 4, 2 * L])
        parts_r = sb("parts", [P, 2, NHI * 3 * E], BF16)
        cnt_r = sb("cnt", [P, KT * B])
        oh_lo = sb("oh_lo", [P, 2, P, 2 * VS], BF16)
        oh_hi = sb("oh_hi", [P, 2, NHI, 2 * VS], BF16)
        wq = sb("wq", [P, 2, HID])
        sel = sb("sel", [96, PB, P], BF16)
        A1p = sb("A1p", [P, HID])
        A1hd = sb("A1hd", [P, HID])
        A2h = sb("A2h", [P, MID])
        A2l = sb("A2l", [P, MID])
        A2s = sb("A2s", [P, HK, MID])
        A3s = sb("A3s", [P, 32])
        iota = sb("iota", [P, P, 2 * VS], BF16)
        ident = sb("ident", [P, P])
        idT = sb("idT", [P, 2, 2 * B * 2], BF16)
        hidx = sb("hidx", [P, 2, HC], U32)
        istage = sb("istage", [P, 2, 2, CH], U32)
        qT = sb("qT", [P, HALF])
        qbias = sb("qbias", [P, HK, 2, HALF])
        attS = sb("attS", [P, 2, PB])
        attT = sb("attT", [P, HALF])
        junk = sb("junk", [P, 2, L], BF16)
        mrow = sb("mrow", [32, L], I32)
        srow = sb("srow", [P, 2 * L])
        Sc = sb("Sc", [32, L])
        smk = sb("smk", [32, L])
        mkb = sb("mkb", [32, L], BF16)
        ex = Sc
        exm = smk
        wts = sb("wts", [32, L])
        pen = wts
        wpart = sb("wpart", [96, L], BF16)
        wmid = mkb
        st = sb("st", [32, 8])
        cat_i = sb("cat_i", [P, Q, NCAT], I32)
        cat_x = sb("cat_x", [P, NCAT, Q], U32)
        tv = sb("tv", [P, Q, E])
        pooled = sb("pooled", [P, 2 * Q, E])
        rlen = sb("rlen", [P, Q])
        vecT = sb("vecT", [P, NR])
        a3c = sb("a3c", [P, 1])
        bhc = sb("bhc", [P, 1])
        nums = sb("nums", [P, Q, 19])
        Wn = sb("Wn", [19, 3 * E])
        kpart = sb("kpart", [P, 4, KT])
        kk = sb("kk", [P, 4])
        xw = sb("xw", [P, KT, 32])
        xsum = sb("xsum", [P, 4])
        fin = sb("fin", [P, 12, Q])

        parts = [parts_r[:, t, :].rearrange("p (h e) -> p h e", e=3 * E) for t in range(2)]
        cnt = cnt_r[:, :].bitcast(BF16)[:, 0:NHI * P].rearrange("p (h v) -> p h v", v=P)
        baseT = cnt_r[:, :].rearrange("p (k b) -> p k b", b=B)
        slot = [embT[:, 1, 2 * SG * E * i:2 * SG * E * (i + 1)].rearrange("p (h e) -> p h e", e=E) for i in range(3)]
        low = parts_r[:, 0, :].bitcast(F32)
        high = parts_r[:, 1, :].bitcast(F32)
        base = low[:, 0:Q * FEAT].rearrange("p (q f) -> p q f", f=FEAT)
        hid_i = low[0:GR, 0:1024].bitcast(I32)
        hid_w = low[0:GR, 1024:2048]
        hid_f = low[0:GR, 2048:3072]
        A1d = low[:, 3072:4096].rearrange("p (f n) -> p f n", n=HID)
        A1s = low[:, 4096:4096 + HID]
        h1f = h1[:, :, :, :].rearrange("p a b c -> p (a b c)")
        vrow = h1f[0:NR, 0:P]
        cat_w = h1f[:, P:P + Q * NCAT].rearrange("p (q f) -> p q f", f=NCAT)
        cat_f = h1f[:, P + Q * NCAT:P + 2 * Q * NCAT].rearrange("p (q f) -> p q f", f=NCAT)
        QL = Q * L
        ids_i = [high[:, 0:QL].bitcast(I32), high[:, QL:2 * QL].bitcast(I32)]
        msk_i = high[:, 2 * QL:3 * QL].bitcast(I32)
        ids_w = high[:, 3 * QL:4 * QL]
        ids_f = high[:, 4 * QL:5 * QL]
        ids_c = high[:, 5 * QL:6 * QL].bitcast(I32)
        tag_lo, tag_hi = high[:, 0:QL], high[:, QL:2 * QL]
        assert 6 * QL <= NHI * 3 * E // 2 and NG == NSL * SG and 6 * SG * E <= CH * P and V % 2 == 0 and Q * FEAT <= NHI * 3 * E // 2
        KE = (NHI * 3 * E // 2 - Q * FEAT) // H1
        D1e = low[:, Q * FEAT:Q * FEAT + KE * H1].rearrange("p (k n) -> p k n", n=H1)
        D1l = high[:, 0:(KT - KE) * H1].rearrange("p (k n) -> p k n", n=H1)
        late = (KT - KE) * H1
        D2s = high[:, late:late + M1 * H2].rearrange("p (k n) -> p k n", n=H2)
        D3s = high[:, late + M1 * H2:late + M1 * H2 + M2 * H3].rearrange("p (k n) -> p k n", n=H3)
        embf = emb[:, :, :].rearrange("p a b -> p (a b)")
        g1 = embf[:, 0:M1 * B].rearrange("p (k b) -> p k b", b=B)
        g2 = h1f[:, 0:M2 * B].rearrange("p (k b) -> p k b", b=B)
        g3 = embf[:, M1 * B:M1 * B + M2 * B].rearrange("p (k b) -> p k b", b=B)
        iota_i = junk[:, :, :].rearrange("p a b -> p (a b)").bitcast(I32)[:, 0:P]
        numT = oh_lo[:, :, :, :].rearrange("p a b c -> p (a b c)").bitcast(F32)[0:19, 0:B]
        onesq = wq[:, 0, 0:P]
        xrow = h2[:, :, :].rearrange("p a b -> p (a b)")[:, 0:B]
        finT = pen[0:Q, 0:P]
        tvq = tv[:, :, :].rearrange("p (a b) e -> p b a e", a=2)

        def by_quarter(x):
            return x.rearrange("p (b a) e -> p b a e", a=2)

        ps = ctx.enter_context(nc.psum_tensor("ps", [P, 8, 512], F32))
        BZ1, BZ2, BSC, BWB, BTR, BCN, BPL = 0, 2, 3, 4, 5, 6, 7

        ld_hid, ld_cat, ld_ids, ld_w, ld_vec, ld_late = map(sem, [
            "ld_hid", "ld_cat", "ld_ids", "ld_w", "ld_vec", "ld_late"])
        ld_tab = [sem(f"ld_tab{n}") for n in range(2 * NSL)]
        ld_d1e = sem("ld_d1e")
        ld_mrow = sem("ld_mrow")
        consts = sem("consts")
        sel_ok = sem("sel_ok")
        prep = sem("prep")
        hid_ok = sem("hid_ok")
        cat_ok = sem("cat_ok")
        ids_ok = sem("ids_ok")
        a1_ok = sem("a1_ok")
        hidx_ok = sem("hidx_ok")
        setT = sem("setT")
        setE = sem("setE")
        idE = sem("idE")
        tv_got = sem("tv_got")
        tab_hi = sem("tab_hi")
        tab_sub = sem("tab_sub")
        tab_zero = sem("tab_zero")
        staged = sem("staged")
        got = [sem(f"got{c}") for c in range(CH)]
        turns = sem("turns")
        emb_t = sem("emb_t")
        embT_ok = sem("embT_ok")
        wq_ok = sem("wq_ok")
        z1_ok = sem("z1_ok")
        h1_ok = sem("h1_ok")
        a2_hi = sem("a2_hi")
        a2_ok = sem("a2_ok")
        hi_a = sem("hi_a")
        lo_ok = sem("lo_ok")
        z2_ok = sem("z2_ok")
        h2_ok = sem("h2_ok")
        sc_ok = sem("sc_ok")
        srow_ok = sem("srow_ok")
        sc_moved = [sem(f"sc_moved{n}") for n in range(4)]
        soft = sem("soft")
        exp_ok = sem("exp_ok")
        w_ok = sem("w_ok")
        wb_ok = sem("wb_ok")
        att_ok = sem("att_ok")
        att_mv = sem("att_mv")
        oh_ok = sem("oh_ok")
        cn_ok = sem("cn_ok")
        cn_mv = sem("cn_mv")
        pl_ok = sem("pl_ok")
        pl_mv = sem("pl_mv")
        pl_ch = sem("pl_ch")
        cats_got = [sem(f"cats_got{k}") for k in range(NCAT // 2)]
        numT_ok = sem("numT_ok")
        kpart_ok = sem("kpart_ok")
        kk_ok = sem("kk_ok")
        tv_ok = sem("tv_ok")
        dch = sem("dch")
        ach = sem("ach")
        base_ok = sem("base_ok")
        x_ok = sem("x_ok")
        x_mv = sem("x_mv")
        fin_ok = sem("fin_ok")
        finT_ok = sem("finT_ok")
        bT = sem("bT")
        bT_mv = sem("bT_mv")
        pe_e = sem("pe_e")
        out_ok = sem("out_ok")

        block = ctx.enter_context(nc.Block())

        N_VEC = 20
        N_SET = 6
        GROUP = {2: 2, 4: 3, 7: 4, 9: 5, 12: 6}
        NEXT = PB - 2
        NS2 = 2 * NSL
        half1 = lambda n: max(2 * n, 1)
        half2 = lambda n: min(2 * n + 3, 2 * NS2)
        for j, g in GROUP.items():
            assert j < 512 * g // L
        SOFT = 15

        @block.sync
        def _(sp):
            sp.dma_start(hid_i.rearrange("c (g p) -> c g p", p=P),
                         hist_ids.rearrange("b l -> (b l)").rearrange("(g c p) -> c g p", c=GR, p=P)
                         ).then_inc(ld_hid, 16)
            for t, off in ((user_cat, 0), (item_cat, NU), (ctx_cat, NU + NI)):
                sp.dma_start(cat_i[:, :, off:off + t.shape[1]],
                             t.rearrange("(q p) f -> p q f", p=P)).then_inc(ld_cat, 16)
            for h in range(2):
                sp.dma_start(A1d[E * h:E * h + E, :, :], A1.rearrange("(f e) n -> e f n", e=E)).then_inc(ld_w, 16)
            sp.dma_start(A2s[:, :, :], A2.rearrange("(k p) m -> p k m", p=P)).then_inc(ld_w, 16)
            for t, src in enumerate((author_ids, tag_ids)):
                sp.dma_start(ids_i[t].rearrange("p (q l) -> p q l", l=L),
                             src.rearrange("(q p) l -> p q l", p=P)).then_inc(ld_ids, 16)
            sp.dma_start(msk_i.rearrange("p (q l) -> p q l", l=L),
                         hist_mask.rearrange("(q p) l -> p q l", p=P)).then_inc(ld_ids, 16)
            def load_mask(b):
                for h in range(2):
                    r0 = HALF * h + PB * b
                    sp.dma_start(mrow[PB * h:PB * h + PB, :],
                                 hist_mask[r0:r0 + PB, :] if isinstance(b, int) else hist_mask[bass.ds(r0, PB), :]
                                 ).then_inc(ld_mrow, 16)

            load_mask(0)
            sp.wait_ge(ld_vec, 16 * N_VEC)
            sp.wait_ge(ld_ids, 48)
            def load_slices(n0, n1):
                for n in range(n0, n1):
                    dst = slot[n % 3]
                    g0 = SG * (n % NSL)
                    rows = item_emb[(1, NI - 1)[n // NSL], 2 * P * g0:min(2 * P * (g0 + SG), V), :]
                    full = rows.shape[0] // (2 * P)
                    rest = rows.shape[0] - 2 * P * full
                    if rest:
                        sp.wait_ge(tab_zero, n // NSL + 1)
                    elif n >= 3:
                        sp.wait_ge(tab_sub, half2(n - 3))
                    sp.dma_start(dst[:, 0:2 * full, :].rearrange("p (g b) e -> p g (b e)", b=2),
                                 rows[0:2 * P * full, :].rearrange("(g p b) e -> p g (b e)", p=P, b=2)
                                 ).then_inc(ld_tab[n], 16)
                    if rest:
                        sp.dma_start(dst[0:rest // 2, 2 * full:2 * full + 2, :].rearrange("p b e -> p (b e)"),
                                     rows[2 * P * full:, :].rearrange("(p b) e -> p (b e)", b=2)
                                     ).then_inc(ld_tab[n], 16)

            SLICES = (9, 13, NS2)
            load_slices(0, SLICES[0])

            def move_scores(b, first):
                if not first:
                    sp.wait_ge(soft, SOFT * (b - 1) + 7)
                    load_mask(b)
                for n in range(4):
                    sp.wait_ge(srow_ok, 4 * b + n + 1)
                    for h in range(2):
                        sp.dma_start(Sc[PB * h + 4 * n:PB * h + 4 * n + 4, :],
                                     srow[0:97:32, L * h:L * h + L]).then_inc(sc_moved[n], 16)
                    if first and n < 2:
                        load_slices(SLICES[n], SLICES[n + 1])

            move_scores(0, True)
            with sp.Fori(1, NBLK) as b:
                move_scores(b, False)

            sp.wait_ge(pl_ok, 2 * Q)
            sp.dma_start(D1l, D1[P * KE:, :].rearrange("(k p) n -> p k n", p=P)).then_inc(ld_late, 16)
            sp.dma_start(D2s, D2.rearrange("(k p) n -> p k n", p=P)).then_inc(ld_late, 16)
            sp.dma_start(D3s, D3.rearrange("(k p) n -> p k n", p=P)).then_inc(ld_late, 16)
            sp.wait_ge(finT_ok, 1)
            sp.dma_start(out.rearrange("(q p) -> q p", p=P), finT).then_inc(out_ok, 16)
            sp.wait_ge(out_ok, 16)

        @block.gpsimd
        def _(pool):
            pool.memset(ident[:, :], 0.0).then_inc(consts, 1)
            pool.memset(sel[0:32, :, :], 0.0).then_inc(consts, 1)
            pool.iota(iota_i, pattern=[[1, P]], base=0, channel_multiplier=0).then_inc(consts, 1)
            pool.wait_ge(consts, 3)
            pool.affine_select(out=ident[:, :], in_=ident[:, :], compare_op=ALU.not_equal, fill=1.0, base=0,
                               pattern=[[-1, P]], channel_multiplier=1).then_inc(consts, 1)
            pool.affine_select(out=sel[0:32, :, :].rearrange("k j (h c) -> k j h c", h=2),
                               in_=sel[0:32, :, :].rearrange("k j (h c) -> k j h c", h=2),
                               compare_op=ALU.not_equal, fill=1.0, base=0,
                               pattern=[[-1, PB], [-PB, 2], [0, E]], channel_multiplier=1).then_inc(consts, 1)

            def gather(dst, table, idx, done):
                pool.indirect_dma_start(out=dst, out_offset=None, in_=table,
                                        in_offset=bass.IndirectOffsetOnAxis(ap=idx, axis=0)).then_inc(done, 16)

            pool.wait_ge(cat_ok, 1)
            for q in range(Q):
                gather(tv[:, q % 2 * 2 + q // 2, :], item_emb[0], cat_x[:, NU, q:q + 1], tv_got)




            def gather_block(b, u, first):
                pool.wait_ge(staged, b + 1)
                pool.sem_inc(turns, 1)
                for c in range(CH):
                    if not first and c % 4 == 0:
                        pool.wait_ge(emb_t, TG * (b - 1) + c // 4 + 1)
                        pool.sem_inc(turns, 1)
                    for h in range(2):
                        gather(emb[:, c, E * h:E * h + E], item_emb[0], istage[:, u, h, c:c + 1], got[c])

            gather_block(0, 0, True)
            with pool.Fori(1, NBLK - 1, 2) as b:
                gather_block(b, 1, False)
                gather_block(b + 1, 0, False)
            gather_block(NBLK - 1, 1, False)

            pool.wait_ge(pl_ok, Q)
            pool.dma_start(D1e, D1[0:P * KE, :].rearrange("(k p) n -> p k n", p=P)).then_inc(ld_d1e, 16)
            for f in range(NCAT):
                if f == NU:
                    continue
                t = user_emb if f < NU else item_emb if f < NU + NI else ctx_emb
                for q in range(Q):
                    gather(base[:, q, E * f:E * f + E], t.rearrange("f v e -> (f v) e"), cat_x[:, f, q:q + 1], cats_got[f // 2])

        @block.tensor
        def _(pe):
            mm = nc.tensor.matmul

            n_set = [0]

            def set_bank():
                n = n_set[0]
                if n >= N_SET + 2:
                    pe.wait_ge(idE, n - N_SET - 1)
                elif n >= 2:
                    pe.wait_ge(setE, n - 1)
                n_set[0] += 1
                return (BWB, BPL)[n % 2]

            pe.wait_ge(consts, 5)
            pe.wait_ge(hid_ok, 1)
            for h in range(2):
                k = set_bank()
                for g in range(4):
                    i = nc.tensor.transpose(ps[:, k, P * g:P * g + GR],
                                            hid_f[:, (4 * h + g) * P:(4 * h + g + 1) * P], ident[0:GR, 0:GR])
                i.then_inc(setT, 1)
            k = set_bank()
            pe.wait_ge(ld_vec, 16 * N_VEC)
            nc.tensor.transpose(ps[:, k, 0:NR], vrow[:, :], ident[0:NR, 0:NR]).then_inc(setT, 1)
            k = set_bank()
            pe.wait_ge(tv_got, 16 * Q)
            for q in range(2):
                i = nc.tensor.transpose(ps[:, k, P * q:P * q + P], tv[:, 2 * q:2 * q + 2, :].rearrange("p a e -> p (a e)"), ident[:, :])
            i.then_inc(setT, 1)
            pe.wait_ge(setE, 4)
            pe.wait_ge(a1_ok, 1)
            for h in range(2):
                k = set_bank()
                for m in range(HK):
                    i = mm(ps[:, k, HALF * m:HALF * m + HALF], A1s[E * h:E * h + E, P * m:P * m + P],
                           qT[E * h:E * h + E, :], start=True, stop=True)
                i.then_inc(setT, 1)

            def transpose_ids(t):
                for q in range(Q):
                    k = set_bank()
                    if q == 0:
                        pe.wait_ge(ids_ok, t + 1)
                    for comp, src in enumerate((ids_w, ids_f) if t == 0 else (tag_lo, tag_hi)):
                        for h in range(2):
                            i = nc.tensor.transpose(ps[0:LH, k, (2 * comp + h) * P:(2 * comp + h + 1) * P],
                                                    src[:, L * q + LH * h:L * q + LH * h + LH], ident[:, :])
                    i.then_inc(setT, 1)

            def transpose_group(b, g, first=False):
                if not (first and g == 0):
                    pe.wait_ge(embT_ok, TG * b + g)
                for n, c in enumerate(range(4 * g, min(4 * g + 4, CH))):
                    pe.wait_ge(got[c], 32 * (b + 1))
                    i = nc.tensor.transpose(ps[:, BTR, P * n:P * n + P], emb[:, c, :], ident[:, :])
                i.then_inc(emb_t, 1)

            def layer1(b, j, u, first):
                s = PB * b + j
                cover = lambda jj: -(-L * (jj + 1) // 512)
                if j == 0 or cover(j) != cover(j - 1):
                    pe.wait_ge(embT_ok, TG * b + min(cover(j), TG))
                pe.wait_ge(wq_ok, s + 1)
                for m in range(HK):
                    for h in range(2):
                        if m == 0 and not (first and j == 0):
                            pe.wait_ge(h1_ok, 2 * s - 1 + h)
                        i = mm(ps[:, BZ1 + h, L * m:L * m + L], wq[E * h:E * h + E, j % 2, P * m:P * m + P],
                               embT[E * h:E * h + E, u, L * j:L * j + L], start=True, stop=True)
                        if m == HK - 1:
                            i.then_inc(z1_ok, 1)

            def counts(b, j, first):
                s = PB * b + j
                pe.wait_ge(oh_ok, s + 1)
                if not (first and j == 0):
                    pe.wait_ge(cn_mv, s)
                for v in range(VS):
                    for h in range(2):
                        i = mm(ps[:, BCN, NHI * v:NHI * v + NHI], oh_lo[0:LH, j % 2, :, 2 * v + h],
                               oh_hi[0:LH, j % 2, :, 2 * v + h], start=(h == 0), stop=(h == 1))
                i.then_inc(cn_ok, 1)

            def pool_product(k, t, part):
                if part == 0:
                    pe.wait_ge(cn_mv, 2 * PB * (k + 1))
                    pe.wait_ge(pl_mv, k + 1)
                for hi in range(NG * part, NG * part + NG):
                    i = mm(ps[:, BPL, 0:3 * E], cnt[:, hi, :], parts[t][:, hi, :], start=(hi == 0), stop=(hi == NHI - 1))
                if part:
                    i.then_inc(pl_ok, 1)

            def layer2(b, j, first):
                s = PB * b + j
                if first and j == 0:
                    return
                if not (first and j == 1):
                    pe.wait_ge(h2_ok, s - 1)
                z2 = ps[:, BZ2, 0:2 * L]
                pe.wait_ge(h1_ok, 2 * s)
                mm(z2, A2s[:, 1, :], h1[:, (j - 1) % 2, 1, :], start=True, stop=False)
                pe.wait_ge(hi_a, s)
                hi = h1h[:, (j - 1) % 2, :].bitcast(F32R)
                mm(z2, A2h[:, :].bitcast(F32R), hi, start=False, stop=False)
                mm(z2, A2l[:, :].bitcast(F32R), hi, start=False, stop=False)
                pe.wait_ge(lo_ok, s)
                i = mm(z2, A2h[:, :].bitcast(F32R), h1l[:, (j - 1) % 2, :].bitcast(F32R), start=False, stop=True)
                i.then_inc(z2_ok, 1)

            def layer3(b, j, first):
                if first and j == 1:
                    return
                pe.wait_ge(h2_ok, PB * b + j - 1)
                if not (first and j == 5):
                    pe.wait_ge(srow_ok, 4 * b + (j - 5) // 4)
                for n in range(4):
                    i = mm(ps[32 * n:32 * n + 32, BSC, 0:2 * L], A3s[:, :], h2[:, n, :], start=True, stop=True,
                           tile_position=(0, 32 * n))
                i.then_inc(sc_ok, 1)

            def spread(b, m):
                if m == 0:
                    pe.wait_ge(sel_ok, 2)
                    pe.wait_ge(w_ok, b + 1)
                else:
                    pe.wait_ge(att_ok, PB * b + 2 * m)
                for r in range(2):
                    i = mm(ps[:, BWB, L * r:L * r + L], sel[:, 2 * m + r, :], wpart[:, :], start=True, stop=True)
                i.then_inc(wb_ok, 1)

            def steps(b, u, first=False, last=False, k=None, t=None):
                for j in range(PB):
                    layer1(b, j, u, first)
                    if k is not None and j < 2:
                        pool_product(k, t, j)
                        if j == 1:
                            counts(b, 0, first)
                    else:
                        counts(b, j, first)
                    if j % 4 == 1:
                        layer3(b, j, first)
                    layer2(b, j, first)
                    if k is not None and j == 1:
                        counts(b, 1, first)
                    if not first and 6 <= j < 14:
                        spread(b - 1, j - 6)
                    if j in GROUP:
                        transpose_group(b, GROUP[j])
                    if not last and j >= NEXT:
                        transpose_group(b + 1, j - NEXT)
                    if first and j == 3:
                        transpose_ids(1)

            transpose_ids(0)
            transpose_group(0, 0, True)
            transpose_group(0, 1)
            pe.wait_ge(a2_ok, 1)
            steps(0, 0, first=True)
            pe.wait_ge(idE, 2 * Q)
            pe.wait_ge(tab_sub, 2 * NS2)
            for t, k0, k1 in ((0, 0, Q), (1, Q, 2 * Q - 1)):
                with pe.Fori(k0, k1) as k:
                    steps(2 * k + 1, 1)
                    steps(2 * k + 2, 0, k=k, t=t)
            steps(NBLK - 1, 1, last=True)
            pool_product(2 * Q - 1, 1, 0)
            pool_product(2 * Q - 1, 1, 1)
            layer2(NBLK, 0, False)
            layer3(NBLK, 1, False)

            pe.wait_ge(prep, 2)
            pe.wait_ge(ld_vec, 16 * N_VEC)
            for q in range(Q):
                i = nc.tensor.transpose(ps[0:19, BTR, P * q:P * q + P], nums[:, q, :], ident[:, :])
            i.then_inc(pe_e, 1)
            pe.wait_ge(numT_ok, 1)
            pe.wait_ge(pl_mv, 2 * Q + 1)
            for q in range(Q):
                i = mm(ps[:, BCN + q // 2, 3 * E * (q % 2):3 * E * (q % 2) + 3 * E], numT[:, P * q:P * q + P],
                       Wn[:, :], start=True, stop=True)
            i.then_inc(pe_e, 1)
            pe.wait_ge(kpart_ok, 1)
            mm(ps[:, BTR, 0:3], onesq, kk[:, 0:3], start=True, stop=True).then_inc(pe_e, 1)

            bank = (BCN, BPL)

            def base_tile(kf):
                if kf < 2:
                    pe.wait_ge(ach, 2)
                else:
                    pe.wait_ge(bT_mv, kf - 1)
                if kf == F_ITEM // P:
                    pe.wait_ge(tv_ok, 1)
                if kf == F_ATT // P:
                    pe.wait_ge(base_ok, 1)
                if kf < NCAT // 2:
                    pe.wait_ge(cats_got[kf], 16 * Q * (2 - (kf == NU // 2)))
                for q in range(Q):
                    i = nc.tensor.transpose(ps[:, bank[kf % 2], P * q:P * q + P],
                                            base[:, q, P * kf:P * kf + P], ident[:, :])
                i.then_inc(bT, 1)

            def deep1(kf):
                pe.wait_ge(bT_mv, kf + 1)
                w = D1e[:, kf, :] if kf < KE else D1l[:, kf - KE, :]
                for m in range(M1):
                    i = mm(ps[:, m, :], w[:, P * m:P * m + P], baseT[:, kf, :], start=(kf == 0), stop=(kf == KT - 1))
                    if kf == KT - 1:
                        i.then_inc(pe_e, 1)

            pe.wait_ge(srow_ok, 4 * NBLK)
            pe.wait_ge(ld_d1e, 16)
            base_tile(0)
            m = 0
            for kf in range(1, KT):
                if kf == F_ATT // P:
                    pe.wait_ge(att_mv, NBLK)
                    for q in range(2):
                        i = nc.tensor.transpose(ps[:, BTR, P * q:P * q + P], attT[:, P * q:P * q + P], ident[:, :])
                    i.then_inc(pe_e, 1)
                else:
                    base_tile(kf)
                if kf - 1 == KE:
                    pe.wait_ge(ld_late, 48)
                deep1(kf - 1)
                if kf == F_ATT // P:
                    base_tile(kf)
                if kf >= 2 and m < PB // 2:
                    if m == 0:
                        pe.wait_ge(kk_ok, 1)
                    spread(NBLK - 1, m)
                    m += 1
            assert m == PB // 2
            deep1(KT - 1)
            pe.wait_ge(att_ok, HALF)
            for kf in range(KT):
                n = 32 * (kf % 4)
                i = mm(ps[n:n + 32, BWB, :], xw[:, kf, :], baseT[:, kf, :], start=(kf < 4), stop=(kf >= KT - 4),
                       tile_position=(0, n))
            i.then_inc(x_ok, 1)
            for m in range(M2):
                for kf in range(M1):
                    if m == 0:
                        pe.wait_ge(ach, 2 + kf + 1)
                    i = mm(ps[:, BCN + m, :], D2s[:, kf, P * m:P * m + P], g1[:, kf, :], start=(kf == 0), stop=(kf == M1 - 1))
                i.then_inc(pe_e, 1)
            for m in range(M2):
                for kf in range(M2):
                    if m == 0:
                        pe.wait_ge(ach, 2 + M1 + kf + 1)
                    i = mm(ps[:, m, :], D3s[:, kf, P * m:P * m + P], g2[:, kf, :], start=(kf == 0), stop=(kf == M2 - 1))
                i.then_inc(pe_e, 1)
            pe.wait_ge(x_mv, 1)
            for q in range(Q):
                mm(ps[:, BWB, 4 * q:4 * q + 4], xrow[:, P * q:P * q + P], xsum[:, :], start=True, stop=True)
            pe.wait_ge(ach, 2 + M1 + 2 * M2)
            for q in range(Q):
                for kf in range(M2):
                    i = mm(ps[:, BWB, 4 * Q + q:4 * Q + q + 1], g3[:, kf, P * q:P * q + P],
                           vecT[:, R_WH2 + kf:R_WH2 + kf + 1], start=(kf == 0), stop=(kf == M2 - 1))
            i.then_inc(pe_e, 1)
            pe.wait_ge(fin_ok, 1)
            nc.tensor.transpose(ps[0:Q, BWB, 0:P], fin[:, 11, :], ident[:, :]).then_inc(pe_e, 1)

        @block.scalar
        def _(act):
            def rows(dst, n, src):
                act.dma_start(vrow[dst:dst + n, :], src).then_inc(ld_vec, 16)
            rows(R_CW, 3 * KT, cross_w.rearrange("v (k p) -> (v k) p", p=P))
            rows(R_CB, 3 * KT, cross_b.rearrange("v (k p) -> (v k) p", p=P))
            rows(R_WH, KT + M2, Wh.rearrange("(k p) o -> k (p o)", p=P))
            rows(R_A1, HK, a1.rearrange("(k p) -> k p", p=P))
            rows(R_A2, 1, a2.rearrange("(k p) -> k p", p=P))
            rows(R_A3, 1, A3.rearrange("(k p) o -> k (p o)", p=P))
            rows(R_D1, M1, d1.rearrange("(k p) -> k p", p=P))
            rows(R_D2, M2, d2.rearrange("(k p) -> k p", p=P))
            rows(R_D3, M2, d3.rearrange("(k p) -> k p", p=P))
            act.dma_start(a3c[:, :], a3.rearrange("(a n) -> a n", a=1).to_broadcast([P, 1])).then_inc(ld_vec, 16)
            act.dma_start(bhc[:, :], bh.rearrange("(a n) -> a n", a=1).to_broadcast([P, 1])).then_inc(ld_vec, 16)
            act.wait_ge(prep, 2)
            col = 0
            for n, (x, w, bias) in enumerate(((user_num, Wu, bu), (item_num, Wi, bi), (ctx_num, Wc, bc))):
                d = x.shape[1]
                act.dma_start(nums[:, :, col:col + d], x.rearrange("(q p) f -> p q f", p=P)).then_inc(ld_vec, 16)
                act.dma_start(Wn[col:col + d, E * n:E * n + E], w).then_inc(ld_vec, 16)
                act.dma_start(Wn[18:19, E * n:E * n + E], bias.rearrange("(a n) -> a n", a=1)).then_inc(ld_vec, 16)
                col += d

            def first_part(n):
                act.wait_ge(ld_tab[n], 32 if n % NSL == NSL - 1 else 16)
                h = 2 * SG * (n % NSL)
                nc.scalar.activation(parts[n // NSL][:, h:h + 2 * SG, 0:E], slot[n % 3], ACT.Copy).then_inc(tab_hi, 1)

            def second_part(n):
                act.wait_ge(tab_sub, half1(n))
                h = 2 * SG * (n % NSL)
                nc.scalar.activation(parts[n // NSL][:, h:h + 2 * SG, E:2 * E], slot[n % 3], ACT.Copy).then_inc(tab_hi, 1)

            def ids_out(t):
                for q in range(Q):
                    n = N_SET + Q * t + q
                    act.wait_ge(setT, n + 1)
                    v0 = 2 * (B * t + P * q)
                    nc.scalar.activation(idT[0:LH, :, v0:v0 + 2 * P].rearrange("l c (v h) -> l c h v", h=2),
                                         ps[0:LH, (BWB, BPL)[n % 2], :].rearrange("l (c h v) -> l c h v", c=2, h=2),
                                         ACT.Copy).then_inc(idE, 1)

            def transposed(b, g, u, reused):
                act.wait_ge(emb_t, TG * b + g + 1)
                if reused:
                    act.wait_ge(att_ok, PB * (b - 1))
                w = min(512, CH * P - 512 * g)
                nc.scalar.activation(embT[:, u, 512 * g:512 * g + w], ps[:, BTR, 0:w], ACT.Copy).then_inc(embT_ok, 1)

            def relu1(b, j, first):
                s = PB * b + j
                for h in range(2):
                    act.wait_ge(z1_ok, 2 * s + h + 1)
                    if h == 0 and not (first and j < 2):
                        act.wait_ge(z2_ok, s - 1)
                    for m in range(HK):
                        bias = qbias[:, m, h, s:s + 1] if isinstance(s, int) else qbias[:, m, h, bass.ds(s, 1)]
                        i = nc.scalar.activation(h1[:, j % 2, m, L * h:L * h + L], ps[:, BZ1 + h, L * m:L * m + L],
                                                 ACT.Relu, bias=bias)
                    i.then_inc(h1_ok, 1)

            def high1(b, j):
                act.wait_ge(h1_ok, 2 * (PB * b + j) + 2)
                nc.scalar.activation(h1h[:, j % 2, :].bitcast(F32R), h1[:, j % 2, 0, :], ACT.Copy).then_inc(hi_a, 1)

            def counts_out(b, j, u, first, k):
                s = PB * b + j
                act.wait_ge(cn_ok, s + 1)
                if j == 0 and k is not None:
                    act.wait_ge(pl_ok, k + 1)
                v0 = PB * VS * u + VS * j
                nc.scalar.activation(cnt[:, :, v0:v0 + VS].rearrange("p h v -> p v h"),
                                     ps[:, BCN, 0:VS * NHI].rearrange("p (v h) -> p v h", v=VS),
                                     ACT.Copy).then_inc(cn_mv, 1)

            def relu2(b, j, first):
                s = PB * b + j
                if first and j == 0:
                    return
                act.wait_ge(z2_ok, s)
                if j % 4 == 1 and not (first and j == 1):
                    act.wait_ge(sc_ok, 4 * b + (j - 1) // 4)
                nc.scalar.activation(h2[:, (j - 1) % 4, :], ps[:, BZ2, 0:2 * L], ACT.Relu,
                                     bias=vecT[:, R_A2:R_A2 + 1]).then_inc(h2_ok, 1)

            def scores_out(b, j, first):
                if first and j == 1:
                    return
                n = (j - 2) // 4 % 4
                act.wait_ge(sc_ok, 4 * b + (j - 1) // 4)
                if n > 0:
                    act.wait_ge(sc_moved[n - 1], 32 * (b + (n < 3)))
                elif not first:
                    act.wait_ge(sc_moved[3], 32 * b)
                nc.scalar.activation(srow[:, :], ps[:, BSC, 0:2 * L], ACT.Identity,
                                     bias=a3c[:, 0:1]).then_inc(srow_ok, 1)

            def exps(b):
                act.wait_ge(soft, SOFT * b + 6)
                nc.scalar.activation(ex[:, :], smk[:, :], ACT.Exp, bias=st[:, 1:2], accum_out=st[:, 2:3]).then_inc(exp_ok, 1)

            def steps(b, u, first=False, last=False, k=None):
                for j in range(PB):
                    relu1(b, j, first)
                    if first and j + 1 < NS2:
                        second_part(j + 1)
                    high1(b, j)
                    if k is None or j > 1:
                        counts_out(b, j, u, first, k)
                    elif j == 1:
                        counts_out(b, 0, u, first, k)
                    relu2(b, j, first)
                    if j % 4 == 1:
                        scores_out(b, j, first)
                    if k is not None and j == 1:
                        counts_out(b, 1, u, first, k)
                    if j == 3 and not first:
                        exps(b - 1)
                    if j in GROUP:
                        transposed(b, GROUP[j], u, False)
                    if first and j == 3:
                        ids_out(1)
                    if first and j + 3 < NS2:
                        first_part(j + 3)
                    if not last and j >= NEXT:
                        if first and j == NEXT:
                            act.wait_ge(tab_sub, 2 * NS2)
                        transposed(b + 1, j - NEXT, 1 - u, not first and j == NEXT)

            act.wait_ge(consts, 5)
            for r in (32, 64):
                nc.scalar.activation(sel[r:r + 32, :, :], sel[0:32, :, :], ACT.Copy).then_inc(sel_ok, 1)
            act.wait_ge(setE, N_SET)
            first_part(0)
            first_part(1)
            ids_out(0)
            transposed(0, 0, 0, False)
            second_part(0)
            first_part(2)
            transposed(0, 1, 0, False)
            steps(0, 0, first=True)
            with act.Fori(0, NBLK // 2 - 1) as k:
                steps(2 * k + 1, 1)
                steps(2 * k + 2, 0, k=k)
            steps(NBLK - 1, 1, last=True)
            relu2(NBLK, 0, False)
            scores_out(NBLK, 1, False)

            act.wait_ge(pe_e, 2)
            for n in range(2):
                nc.scalar.activation(base[:, 2 * n:2 * n + 2, F_NUM:F_NUM + 3 * E],
                                     ps[:, BCN + n, 0:6 * E].rearrange("p (q f) -> p q f", q=2),
                                     ACT.Relu).then_inc(ach, 1)
            for kf in range(KT):
                act.wait_ge(bT, kf + 1)
                nc.scalar.activation(baseT[:, kf, :], ps[:, (BCN, BPL)[kf % 2], :], ACT.Copy).then_inc(bT_mv, 1)
                if kf == 0:
                    exps(NBLK - 1)
            for m in range(M1):
                act.wait_ge(pe_e, 4 + m + 1)
                nc.scalar.activation(g1[:, m, :], ps[:, m, :], ACT.Relu, bias=vecT[:, R_D1 + m:R_D1 + m + 1]).then_inc(ach, 1)
            for m in range(M2):
                act.wait_ge(pe_e, 4 + M1 + m + 1)
                nc.scalar.activation(g2[:, m, :], ps[:, BCN + m, :], ACT.Relu, bias=vecT[:, R_D2 + m:R_D2 + m + 1]).then_inc(ach, 1)
            for m in range(M2):
                act.wait_ge(pe_e, 4 + M1 + M2 + m + 1)
                nc.scalar.activation(g3[:, m, :], ps[:, m, :], ACT.Identity, bias=vecT[:, R_D3 + m:R_D3 + m + 1]).then_inc(ach, 1)

        @block.vector
        def _(dve):
            v = nc.vector
            done = [0]

            def chain(i):
                done[0] += 1
                i.then_inc(prep, 1)
                dve.wait_ge(prep, done[0])

            v.memset(st[:, :], 0.0).then_inc(pl_mv, 1)
            chain(v.memset(Wn[:, :], 0.0))
            chain(v.memset(nums[:, :, 18:19], 1.0))

            def clamp(f, i, w, signal=None):
                chain(v.tensor_scalar(w, i, 0.0, float(V), ALU.is_lt, ALU.mult))
                chain(v.tensor_tensor(w, i, w, ALU.add))
                last = v.tensor_scalar(f, w, 0.0, float(V - 1), ALU.max, ALU.min)
                chain(last) if signal is None else last.then_inc(signal, 1)

            dve.wait_ge(ld_hid, 16)
            clamp(hid_f, hid_i, hid_w, hid_ok)
            dve.wait_ge(ld_cat, 48)
            clamp(cat_f[:, :, :], cat_i[:, :, :], cat_w[:, :, :])
            for f in range(NCAT):
                first = 0 if f < NU else NU if f < NU + NI else NU + NI
                i = v.tensor_scalar(cat_x[:, f, :], cat_f[:, :, f], float((f - first) * V), None, ALU.add)
            i.then_inc(cat_ok, 1)
            n_set = [0]

            def set_out():
                k = (BWB, BPL)[n_set[0] % 2]
                n_set[0] += 1
                dve.wait_ge(setT, n_set[0])
                return k

            for h in range(2):
                k = set_out()
                v.tensor_copy(hidx[:, h, :].rearrange("p (g c) -> p g c", c=GR),
                              ps[:, k, :].rearrange("p (g c) -> p g c", c=P)[:, :, 0:GR]).then_inc(setE, 1)
            dve.wait_ge(setE, 2)
            for b in range(2):
                v.tensor_scalar(istage[:, b, :, :], hidx[:, :, CH * b:CH * b + CH], 1.0, None, ALU.mult).then_inc(staged, 1)
            dve.wait_ge(ld_w, 48)
            v.tensor_tensor(A1hd[:, :], A1d[:, 1, :], A1d[:, 2, :], ALU.subtract)
            v.tensor_copy(A1p[:, :], A1d[:, 3, :])
            v.tensor_tensor(A1s, A1d[:, 0, :], A1d[:, 2, :], ALU.add).then_inc(a1_ok, 1)

            v.tensor_copy(A2h[:, :].bitcast(F32R), A2s[:, 0, :]).then_inc(a2_hi, 1)
            dve.wait_ge(a2_hi, 1)
            v.tensor_tensor(A2l[:, :].bitcast(F32R), A2s[:, 0, :], A2h[:, :], ALU.subtract).then_inc(a2_ok, 1)

            dve.wait_ge(ld_ids, 48)
            chain(v.tensor_scalar(msk_i, msk_i, 0.0, None, ALU.is_gt))

            def id_clamp(t):
                clamp(ids_c, ids_i[t], tag_lo if t else ids_w)

            def id_high(t):
                w = tag_lo if t else ids_w
                chain(v.tensor_scalar(w.bitcast(I32), ids_c, 7, 126, ALU.arith_shift_right, ALU.bitwise_and))
                chain(v.scalar_tensor_tensor(out=ids_i[t], in0=ids_c, scalar=1, in1=w.bitcast(I32),
                                             op0=ALU.bitwise_and, op1=ALU.bitwise_or))

            def id_rest(t):
                lo, hi = (tag_lo, tag_hi) if t else (ids_w, ids_f)
                chain(v.tensor_scalar(ids_c, ids_c, 1, 127, ALU.arith_shift_right, ALU.bitwise_and))
                chain(v.tensor_copy(lo, ids_c))
                v.scalar_tensor_tensor(out=hi, in0=ids_i[t], scalar=1.0, in1=msk_i, op0=ALU.add,
                                       op1=ALU.mult).then_inc(ids_ok, 1)

            def lengths():
                with nc.allow_low_precision(reason="sums of 0 and 1"):
                    chain(v.tensor_reduce(rlen[:, :], msk_i.rearrange("p (q l) -> p q l", l=L), AX_X, ALU.add))
                chain(v.tensor_scalar(rlen[:, :], rlen[:, :], 1e-6, None, ALU.max))
                chain(v.reciprocal(rlen[:, :], rlen[:, :]))

            id_clamp(0)
            id_high(0)
            id_rest(0)
            k = set_out()
            v.tensor_copy(vecT[:, :], ps[:, k, 0:NR]).then_inc(setE, 1)
            dve.wait_ge(setE, 3)
            v.tensor_copy(A3s[:, :], vecT[:, R_A3:R_A3 + 1].to_broadcast([P, 32]))
            k = set_out()
            v.tensor_copy(qT[:, :], ps[:, k, 0:HALF]).then_inc(setE, 1)
            for h in range(2):
                k = set_out()
                for m in range(HK):
                    i = v.tensor_scalar(qbias[:, m, h, :], ps[:, k, HALF * m:HALF * m + HALF],
                                        vecT[:, R_A1 + m:R_A1 + m + 1], None, ALU.add)
                i.then_inc(setE, 1)
            assert n_set[0] == N_SET
            dve.wait_ge(consts, 3)
            chain(v.tensor_copy(iota[:, :, :], iota_i.unsqueeze(2).to_broadcast([P, P, 2 * VS])))

            def residual(n):
                dve.wait_ge(tab_hi, half1(n))
                h = 2 * SG * (n % NSL)
                v.tensor_tensor(slot[n % 3], slot[n % 3], parts[n // NSL][:, h:h + 2 * SG, 0:E],
                                ALU.subtract).then_inc(tab_sub, 1)

            def third_part(n):
                dve.wait_ge(tab_hi, half2(n))
                part = parts[n // NSL][:, 2 * SG * (n % NSL):2 * SG * (n % NSL + 1), :]
                v.tensor_tensor(part[:, :, 2 * E:3 * E], slot[n % 3], part[:, :, E:2 * E], ALU.subtract).then_inc(tab_sub, 1)
                if (n + 3) % NSL == NSL - 1:
                    dve.wait_ge(tab_sub, half2(n))
                    v.memset(slot[n % 3][:, 2 * SG - 2:2 * SG, :], 0.0).then_inc(tab_zero, 1)

            def weights(s, j, free):
                if free is not None:
                    dve.wait_ge(z1_ok, free)
                q = qT[:, s:s + 1] if isinstance(s, int) else qT[:, bass.ds(s, 1)]
                v.scalar_tensor_tensor(out=wq[:, j % 2, :], in0=A1p[:, :], scalar=q, in1=A1hd[:, :],
                                       op0=ALU.mult, op1=ALU.add).then_inc(wq_ok, 1)

            def low1(s, j):
                dve.wait_ge(hi_a, s + 1)
                v.tensor_tensor(h1l[:, j % 2, :].bitcast(F32R), h1[:, j % 2, 0, :], h1h[:, j % 2, :],
                                ALU.subtract).then_inc(lo_ok, 1)

            def onehots(s, j, free):
                if free is not None:
                    dve.wait_ge(cn_ok, free)
                for comp, (oh, n0, n) in enumerate(((oh_lo, 0, P), (oh_hi, 1, NHI))):
                    code = idT[0:LH, comp, 2 * VS * s:2 * VS * s + 2 * VS] if isinstance(s, int) else \
                        idT[0:LH, comp, bass.ds(s * (2 * VS), 2 * VS)]
                    i = v.tensor_tensor(oh[0:LH, j % 2, :, :], iota[0:LH, n0:n0 + n, :],
                                        code.unsqueeze(1).to_broadcast([LH, n, 2 * VS]), ALU.is_equal)
                i.then_inc(oh_ok, 1)

            def softmax_top(b):
                for n in range(4):
                    dve.wait_ge(sc_moved[n], 32 * (b + 1))
                dve.wait_ge(ld_mrow, 32 * (b + 1))
                mk = mrow[:, :]
                v.tensor_scalar(mkb[:, :], mk, 1.0, None, ALU.mult).then_inc(soft, 1)
                v.tensor_tensor(smk[:, :], Sc[:, :], mk, ALU.mult).then_inc(soft, 1)
                v.tensor_scalar(pen[:, :], mk, 1e9, -1e9, ALU.mult, ALU.add).then_inc(soft, 1)
                dve.wait_ge(soft, SOFT * b + 3)
                v.tensor_tensor(smk[:, :], smk[:, :], pen[:, :], ALU.add).then_inc(soft, 1)
                dve.wait_ge(soft, SOFT * b + 4)
                v.tensor_reduce(st[:, 0:1], smk[:, :], AX_X, ALU.max).then_inc(soft, 1)
                dve.wait_ge(soft, SOFT * b + 5)
                v.tensor_scalar(st[:, 1:2], st[:, 0:1], -1.0, None, ALU.mult).then_inc(soft, 1)

            def softmax_norm(b):
                dve.wait_ge(exp_ok, b + 1)
                v.tensor_tensor_reduce(out=exm[:, :], in0=ex[:, :], in1=mkb[:, :], scale=1.0, scalar=0.0, op0=ALU.mult,
                                       op1=ALU.add, accum_out=st[:, 3:4]).then_inc(soft, 1)
                v.reciprocal(st[:, 4:5], st[:, 2:3]).then_inc(soft, 1)
                dve.wait_ge(soft, SOFT * b + 8)
                v.tensor_scalar(st[:, 5:6], st[:, 3:4], st[:, 4:5], 1e-6, ALU.mult, ALU.max).then_inc(soft, 1)
                dve.wait_ge(soft, SOFT * b + 9)
                v.reciprocal(st[:, 6:7], st[:, 5:6]).then_inc(soft, 1)
                dve.wait_ge(soft, SOFT * b + 10)
                v.tensor_scalar(wts[:, :], exm[:, :], st[:, 4:5], st[:, 6:7], ALU.mult, ALU.mult).then_inc(soft, 1)

            def softmax_parts(b):
                dve.wait_ge(soft, SOFT * b + 11)
                v.tensor_copy(wpart[0:32, :], wts[:, :]).then_inc(soft, 1)
                dve.wait_ge(soft, SOFT * b + 12)
                v.tensor_tensor(wts[:, :], wts[:, :], wpart[0:32, :], ALU.subtract).then_inc(soft, 1)
                dve.wait_ge(soft, SOFT * b + 13)
                v.tensor_copy(wmid[:, :], wts[:, :]).then_inc(soft, 1)
                dve.wait_ge(soft, SOFT * b + 14)
                v.tensor_copy(wpart[32:64, :], wmid[:, :]).then_inc(soft, 1)
                v.tensor_tensor(wpart[64:96, :], wts[:, :], wmid[:, :], ALU.subtract).then_inc(w_ok, 1)

            def attend(b, m, u):
                dve.wait_ge(wb_ok, PB // 2 * b + m + 1)
                for r in range(2):
                    j = 2 * m + r
                    if m:
                        dve.wait_ge(att_ok, PB * b + j - 1)
                    v.tensor_tensor_reduce(out=junk[:, j % 2, :], in0=ps[:, BWB, L * r:L * r + L],
                                           in1=embT[:, u, L * j:L * j + L], scale=1.0, scalar=0.0, op0=ALU.mult,
                                           op1=ALU.add, accum_out=attS[:, 0, j:j + 1]).then_inc(att_ok, 1)

            def place(b):
                dve.wait_ge(att_ok, PB * b + PB)
                dst = attT[:, PB * b:PB * b + PB] if isinstance(b, int) else attT[:, bass.ds(b * PB, PB)]
                v.tensor_scalar(dst, attS[:, 0, :], 1.0, None, ALU.mult).then_inc(att_mv, 1)

            def stage(b, u):
                dve.wait_ge(emb_t, TG * (b + 1))
                src = hidx[:, :, CH * (b + 2):CH * (b + 3)] if isinstance(b, int) else \
                    hidx[:, :, bass.ds(CH * (b + 2), CH)]
                v.tensor_scalar(istage[:, u, :, :], src, 1.0, None, ALU.mult).then_inc(staged, 1)

            def pool_out(k):
                dve.wait_ge(pl_ok, k + 1)
                dst = pooled[:, k, :] if isinstance(k, int) else pooled[:, bass.ds(k, 1), :].rearrange("p a e -> p (a e)")
                v.tensor_scalar(dst, ps[:, BPL, 2 * E:3 * E], 1.0, None, ALU.mult).then_inc(pl_ch, 1)
                dve.wait_ge(pl_ch, 2 * k + 1)
                v.tensor_tensor(dst, ps[:, BPL, E:2 * E], dst, ALU.add).then_inc(pl_ch, 1)
                dve.wait_ge(pl_ch, 2 * k + 2)
                v.tensor_tensor(dst, ps[:, BPL, 0:E], dst, ALU.add).then_inc(pl_mv, 1)

            def steps(b, u, first=False, last=False, k=None, nostage=False):
                for j in range(PB):
                    s = PB * b + j
                    start = first and j == 0
                    if not start:
                        low1(s - 1, j - 1)
                    if not (last and j == PB - 1):
                        weights(s + 1, j + 1, None if start else 2 * s)
                        onehots(s + 1, j + 1, None if start else s)
                    if first and j == 0:
                        dve.wait_ge(ids_ok, 1)
                        id_clamp(1)
                    if first and j == 1:
                        id_high(1)
                    if first and j == 2:
                        id_rest(1)
                    if first and j + 2 < NS2:
                        residual(j + 2)
                    if first and j + 1 < NS2:
                        third_part(j + 1)
                    if j == 2 and k is not None:
                        pool_out(k)
                    if not first and 3 <= j < 6:
                        (softmax_top, softmax_norm, softmax_parts)[j - 3](b - 1)
                    if not first and 6 <= j < 14:
                        attend(b - 1, j - 6, 1 - u)
                    if not first and j == 14:
                        place(b - 1)
                    if j == 13 and not nostage:
                        stage(b, u)

            weights(0, 0, None)
            residual(0)
            residual(1)
            lengths()
            dve.wait_ge(idE, Q)
            onehots(0, 0, None)
            third_part(0)
            steps(0, 0, first=True)
            with dve.Fori(0, NBLK // 2 - 2) as k:
                steps(2 * k + 1, 1)
                steps(2 * k + 2, 0, k=k)
            steps(NBLK - 3, 1)
            steps(NBLK - 2, 0, k=NBLK // 2 - 2, nostage=True)
            steps(NBLK - 1, 1, last=True, nostage=True)
            low1(HALF - 1, PB - 1)
            pool_out(2 * Q - 1)

            n = [0]

            def link(i):
                n[0] += 1
                i.then_inc(dch, 1)
                dve.wait_ge(dch, n[0])

            cw = lambda i: vecT[:, R_CW + KT * i:R_CW + KT * i + KT]
            cb = lambda i: vecT[:, R_CB + KT * i:R_CB + KT * i + KT]
            wh = vecT[:, R_WH:R_WH + KT]
            link(v.memset(xw[:, :, :], 0.0))
            link(v.tensor_tensor(kpart[:, 0, :], cb(0), cw(1), ALU.mult))
            link(v.tensor_tensor(kpart[:, 3, :], cb(0), cb(1), ALU.add))
            link(v.tensor_tensor(kpart[:, 1, :], kpart[:, 3, :], cw(2), ALU.mult))
            link(v.tensor_tensor(kpart[:, 3, :], kpart[:, 3, :], cb(2), ALU.add))
            link(v.tensor_tensor(kpart[:, 2, :], kpart[:, 3, :], wh, ALU.mult))
            for i in range(3):
                link(v.tensor_copy(xw[:, :, i], cw(i)))
            link(v.tensor_copy(xw[:, :, 3], wh))
            link(v.tensor_reduce(xsum[:, :], ident[:, :].rearrange("p (n c) -> p c n", n=4)[:, 0:4, :], AX_X, ALU.add))
            dve.wait_ge(z1_ok, 2 * HALF)
            link(v.memset(onesq, 1.0))
            v.tensor_reduce(kk[:, 0:3], kpart[:, 0:3, :], AX_X, ALU.add).then_inc(kpart_ok, 1)
            dve.wait_ge(pe_e, 1)
            v.tensor_copy(numT, ps[0:19, BTR, :]).then_inc(numT_ok, 1)
            for q in range(Q):
                for t in range(2):
                    link(v.tensor_scalar(base[:, q, F_POOL + E * t:F_POOL + E * t + E], pooled[:, Q * t + q, :],
                                         rlen[:, q:q + 1], None, ALU.mult))
            v.tensor_copy(by_quarter(base[:, :, F_ITEM:F_ITEM + E]), tvq).then_inc(tv_ok, 1)
            dve.wait_ge(pe_e, 3)
            v.tensor_copy(kk[:, 0:3], ps[:, BTR, 0:3]).then_inc(kk_ok, 1)
            softmax_top(NBLK - 1)
            softmax_norm(NBLK - 1)
            softmax_parts(NBLK - 1)
            for m in range(PB // 2):
                attend(NBLK - 1, m, 1)
            place(NBLK - 1)
            dve.wait_ge(pe_e, 4)
            att = base[:, :, F_ATT:F_ATT + E]
            for h in range(2):
                link(v.tensor_copy(att[:, 2 * h:2 * h + 2, :],
                                   ps[:, BTR, 0:2 * P].rearrange("p (q h e) -> p q h e", q=2, h=2)[:, :, h, :]))
            link(v.tensor_tensor(by_quarter(base[:, :, F_MUL:F_MUL + E]), tvq, by_quarter(att), ALU.mult))
            v.tensor_tensor(by_quarter(base[:, :, F_DIF:F_DIF + E]), tvq, by_quarter(att), ALU.subtract).then_inc(base_ok, 1)
            dve.wait_ge(x_ok, 1)
            v.tensor_copy(xrow, ps[:, BWB, :]).then_inc(x_mv, 1)
            dve.wait_ge(pe_e, 5 + M1 + 2 * M2)
            f = lambda i: fin[:, i, :]
            link(v.tensor_copy(fin[:, 0:4, :].rearrange("p i q -> p q i"),
                               ps[:, BWB, 0:4 * Q].rearrange("p (q i) -> p q i", i=4)))
            link(v.tensor_copy(f(4), ps[:, BWB, 4 * Q:5 * Q]))
            link(v.tensor_scalar(f(5), f(0), 1.0, None, ALU.add))
            for i, (c, t, nxt) in enumerate(((5, 6, 7), (7, 8, 9))):
                link(v.tensor_tensor(f(t), f(c), f(i + 1), ALU.mult))
                link(v.tensor_scalar(f(t), f(t), kk[:, i:i + 1], None, ALU.add))
                link(v.tensor_tensor(f(nxt), f(t), f(c), ALU.add))
            link(v.tensor_tensor(f(10), f(9), f(3), ALU.mult))
            link(v.tensor_tensor(f(10), f(10), f(4), ALU.add))
            v.tensor_scalar(f(11), f(10), kk[:, 2:3], bhc[:, 0:1], ALU.add, ALU.add).then_inc(fin_ok, 1)
            dve.wait_ge(pe_e, 6 + M1 + 2 * M2)
            v.tensor_copy(finT, ps[0:Q, BWB, 0:P]).then_inc(finT_ok, 1)


_INS = ["r_user_cat", "r_user_num", "r_ctx_cat", "r_ctx_num", "r_hist_ids", "r_hist_author_ids", "r_hist_tag_ids",
        "r_hist_mask", "r_item_cat", "r_item_num", "L0_rec_user_emb", "L0_rec_item_emb", "L0_rec_ctx_emb",
        "L0_rec_Wu", "L0_rec_bu", "L0_rec_Wi", "L0_rec_bi", "L0_rec_Wc", "L0_rec_bc", "L0_rec_A1", "L0_rec_a1",
        "L0_rec_A2", "L0_rec_a2", "L0_rec_A3", "L0_rec_a3", "L0_rec_cross_w", "L0_rec_cross_b", "L0_rec_D1",
        "L0_rec_d1", "L0_rec_D2", "L0_rec_d2", "L0_rec_D3", "L0_rec_d3", "L0_rec_Wh", "L0_rec_bh"]


def kernel(**inputs):
    import numpy as np
    import concourse.bacc as bacc
    from concourse.bass_utils import run_bass_kernel_spmd

    nc = bacc.Bacc("TRN2", target_bir_lowering=False, num_devices=1)
    arrays, args = {}, []
    for name in _INS:
        a = np.ascontiguousarray(inputs[name])
        arrays["in_" + name] = a
        args.append(nc.dram_tensor("in_" + name, a.shape, mybir.dt.from_np(a.dtype), kind="ExternalInput").ap())
    out = nc.dram_tensor("out_0", (inputs["r_hist_ids"].shape[0],), F32, kind="ExternalOutput").ap()
    recommender(nc, *args, out)
    r = run_bass_kernel_spmd(nc, [arrays], core_ids=[0])
    return r.results[0]["out_0"]
```
